# Optimizing a Trainium2 kernel written in Bass

```python
import numpy as np
import jax
import jax.numpy as jnp

def _softmax(x, axis=-1):
    return jax.nn.softmax(x, axis=axis)

def _gelu(x):
    return jax.nn.gelu(x, approximate=True)

def _silu(x):
    return jax.nn.silu(x)

def _sigmoid(x):
    return jax.nn.sigmoid(x)

def _layernorm(x, axis=-1, eps=1e-05):
    m = jnp.mean(x, axis=axis, keepdims=True)
    v = jnp.var(x, axis=axis, keepdims=True)
    return (x - m) / jnp.sqrt(v + eps)

def _scatter_add(tgt, idx, src, axis=0):
    return tgt.at[idx].add(src)

def _segment_sum(src, seg, n):
    return jax.ops.segment_sum(src, seg, n)
kernel_name = 'mk_macaron_d2_jaxref_r8_f25a0c'

def setup_inputs(seed: int=0):
    np.random.seed(seed)
    _w = jnp.asarray

    def _L0_attn_setup():
        import jax, jax.numpy as jnp
        import numpy as np
        from jax import lax
        D_MODEL = 128
        LN_EPS = 1e-05

        def _layer_norm(x, gamma, beta):
            mu = jnp.mean(x, axis=-1, keepdims=True)
            var = jnp.mean(jnp.square(x - mu), axis=-1, keepdims=True)
            return (x - mu) * lax.rsqrt(var + LN_EPS) * gamma + beta
        key = jax.random.key(seed)
        ks = jax.random.split(key, 9)
        B, L, D = (2, 256, D_MODEL)
        x = jax.random.normal(ks[0], (B, L, D), dtype=jnp.float32)
        A_param = jax.random.normal(ks[1], (D,), dtype=jnp.float32) * 0.1
        B_vec = jax.random.normal(ks[2], (D,), dtype=jnp.float32)
        C_vec = jax.random.normal(ks[3], (D,), dtype=jnp.float32)
        D_vec = jax.random.normal(ks[4], (D,), dtype=jnp.float32)
        W_proj = jax.random.normal(ks[5], (D, D), dtype=jnp.float32) * (1.0 / np.sqrt(D))
        b_proj = jax.random.normal(ks[6], (D,), dtype=jnp.float32) * 0.01
        gamma = jnp.ones((D,), dtype=jnp.float32)
        beta = jnp.zeros((D,), dtype=jnp.float32)
        return {'x': x, 'A_param': A_param, 'B_vec': B_vec, 'C_vec': C_vec, 'D_vec': D_vec, 'W_proj': W_proj, 'b_proj': b_proj, 'gamma': gamma, 'beta': beta}
    _L0_attn_in = _L0_attn_setup()

    def _L0_ffn_setup():
        import jax, jax.numpy as jnp
        import numpy as np
        B, S, H, E, K, I = (1, 64, 128, 16, 4, 128)
        ALPHA, LIMIT = (1.702, 7.0)
        key = jax.random.key(seed)
        ks = jax.random.split(key, 7)
        return {'hidden_states': jax.random.normal(ks[0], (B, S, H), jnp.float32), 'router_w': jax.random.normal(ks[1], (H, E), jnp.float32) * 0.02, 'router_b': jax.random.normal(ks[2], (E,), jnp.float32) * 0.02, 'gate_up_proj': jax.random.normal(ks[3], (E, H, 2 * I), jnp.float32) * 0.02, 'gate_up_bias': jax.random.normal(ks[4], (E, 2 * I), jnp.float32) * 0.02, 'down_proj': jax.random.normal(ks[5], (E, I, H), jnp.float32) * 0.02, 'down_bias': jax.random.normal(ks[6], (E, H), jnp.float32) * 0.02}
    _L0_ffn_in = _L0_ffn_setup()

    def _L1_attn_setup():
        import jax, jax.numpy as jnp
        import numpy as np
        D_MODEL = 128
        N_HEADS = 16
        HEAD_DIM = D_MODEL // N_HEADS
        D_LATENT = 32
        LAMBDA_DECAY = 0.01
        TIME_STEP = 0.01
        CLAMP = 10000.0

        def _reference_tuple_inner(x, Wq, Wk, Wv, Wo, W_down_kv, W_up_k, W_up_v):
            B, S, _ = x.shape
            q = x @ Wq
            k = x @ Wk
            v = x @ Wv
            latent_kv = (k + v) @ W_down_kv
            k_rec = latent_kv @ W_up_k
            v_rec = latent_kv @ W_up_v

            def heads(t):
                return t.reshape(B, S, N_HEADS, HEAD_DIM).transpose(0, 2, 1, 3)
            qh, kh, vh = (heads(q), heads(k_rec), heads(v_rec))
            scale = 1.0 / (jnp.sqrt(jnp.float32(D_MODEL)) + 1e-08)
            scores = jnp.einsum('bhqd,bhkd->bhqk', qh, kh) * scale
            scores = jnp.clip(jnp.nan_to_num(scores, nan=-1000000000.0), -CLAMP, CLAMP)
            idx = jnp.arange(S, dtype=jnp.float32)
            decay = jnp.exp(-LAMBDA_DECAY * TIME_STEP * jnp.abs(idx[:, None] - idx[None, :]))
            scores = scores * decay[None, None, :, :]
            scores = jnp.clip(jnp.nan_to_num(scores, nan=-1000000000.0), -CLAMP, CLAMP)
            attn = jax.nn.softmax(scores, axis=-1)
            out = jnp.einsum('bhqk,bhkd->bhqd', attn, vh)
            out = out.transpose(0, 2, 1, 3).reshape(B, S, D_MODEL)
            return (out @ Wo, latent_kv)
        key = jax.random.key(seed)
        ks = jax.random.split(key, 8)
        B, S = (2, 256)

        def w(k, i, o):
            return jax.random.normal(k, (i, o), dtype=jnp.float32) * 0.02
        return {'x': jax.random.normal(ks[0], (B, S, D_MODEL), dtype=jnp.float32), 'Wq': w(ks[1], D_MODEL, D_MODEL), 'Wk': w(ks[2], D_MODEL, D_MODEL), 'Wv': w(ks[3], D_MODEL, D_MODEL), 'Wo': w(ks[4], D_MODEL, D_MODEL), 'W_down_kv': w(ks[5], D_MODEL, D_LATENT), 'W_up_k': w(ks[6], D_LATENT, D_MODEL), 'W_up_v': w(ks[7], D_LATENT, D_MODEL)}
    _L1_attn_in = _L1_attn_setup()

    def _L1_ffn_setup():
        import jax, jax.numpy as jnp
        import numpy as np
        D_MODEL = 128
        D_OUT = 128
        RANK = 16
        NUM_TRUE = 8
        NUM_NULL = 2
        TOP_K = 2
        SCALING = 32.0 / 16.0
        key = jax.random.key(seed)
        ks = jax.random.split(key, 6)
        x = jax.random.normal(ks[0], (4, 512, D_MODEL), dtype=jnp.float32)
        base_w = jax.random.normal(ks[1], (D_OUT, D_MODEL), dtype=jnp.float32) / np.sqrt(D_MODEL)
        base_b = jax.random.normal(ks[2], (D_OUT,), dtype=jnp.float32) * 0.01
        gate_w = jax.random.normal(ks[3], (NUM_TRUE + NUM_NULL, D_MODEL), dtype=jnp.float32) / np.sqrt(D_MODEL)
        lora_A = jax.random.normal(ks[4], (NUM_TRUE, RANK, D_MODEL), dtype=jnp.float32) / np.sqrt(D_MODEL)
        lora_B = jax.random.normal(ks[5], (NUM_TRUE, D_OUT, RANK), dtype=jnp.float32) * 0.01
        return {'x': x, 'base_w': base_w, 'base_b': base_b, 'gate_w': gate_w, 'lora_A': lora_A, 'lora_B': lora_B}
    _L1_ffn_in = _L1_ffn_setup()
    _d = {'L0_attn_x': _L0_attn_in['x'], 'L0_attn_A_param': _L0_attn_in['A_param'], 'L0_attn_B_vec': _L0_attn_in['B_vec'], 'L0_attn_C_vec': _L0_attn_in['C_vec'], 'L0_attn_D_vec': _L0_attn_in['D_vec'], 'L0_attn_W_proj': _L0_attn_in['W_proj'], 'L0_attn_b_proj': _L0_attn_in['b_proj'], 'L0_attn_gamma': _L0_attn_in['gamma'], 'L0_attn_beta': _L0_attn_in['beta'], 'L0_ffn_router_w': _L0_ffn_in['router_w'], 'L0_ffn_router_b': _L0_ffn_in['router_b'], 'L0_ffn_gate_up_proj': _L0_ffn_in['gate_up_proj'], 'L0_ffn_gate_up_bias': _L0_ffn_in['gate_up_bias'], 'L0_ffn_down_proj': _L0_ffn_in['down_proj'], 'L0_ffn_down_bias': _L0_ffn_in['down_bias'], 'L1_attn_Wq': _L1_attn_in['Wq'], 'L1_attn_Wk': _L1_attn_in['Wk'], 'L1_attn_Wv': _L1_attn_in['Wv'], 'L1_attn_Wo': _L1_attn_in['Wo'], 'L1_attn_W_down_kv': _L1_attn_in['W_down_kv'], 'L1_attn_W_up_k': _L1_attn_in['W_up_k'], 'L1_attn_W_up_v': _L1_attn_in['W_up_v'], 'L1_ffn_base_w': _L1_ffn_in['base_w'], 'L1_ffn_base_b': _L1_ffn_in['base_b'], 'L1_ffn_gate_w': _L1_ffn_in['gate_w'], 'L1_ffn_lora_A': _L1_ffn_in['lora_A'], 'L1_ffn_lora_B': _L1_ffn_in['lora_B']}
    _x0 = _d['L0_attn_x']
    _d['L0_attn_x'] = jax.random.normal(jax.random.fold_in(jax.random.key(seed), 1), (2, 1024, 128), dtype=_x0.dtype)
    del _x0
    return _d

def reference(L0_attn_x, L0_attn_A_param, L0_attn_B_vec, L0_attn_C_vec, L0_attn_D_vec, L0_attn_W_proj, L0_attn_b_proj, L0_attn_gamma, L0_attn_beta, L0_ffn_router_w, L0_ffn_router_b, L0_ffn_gate_up_proj, L0_ffn_gate_up_bias, L0_ffn_down_proj, L0_ffn_down_bias, L1_attn_Wq, L1_attn_Wk, L1_attn_Wv, L1_attn_Wo, L1_attn_W_down_kv, L1_attn_W_up_k, L1_attn_W_up_v, L1_ffn_base_w, L1_ffn_base_b, L1_ffn_gate_w, L1_ffn_lora_A, L1_ffn_lora_B):

    def _L0_attn_ref(x, A_param, B_vec, C_vec, D_vec, W_proj, b_proj, gamma, beta):
        import jax, jax.numpy as jnp
        import numpy as np
        from jax import lax
        D_MODEL = 128
        LN_EPS = 1e-05

        def _layer_norm(x, gamma, beta):
            mu = jnp.mean(x, axis=-1, keepdims=True)
            var = jnp.mean(jnp.square(x - mu), axis=-1, keepdims=True)
            return (x - mu) * lax.rsqrt(var + LN_EPS) * gamma + beta
        Bsz, L, D = x.shape
        A = jax.nn.sigmoid(A_param)
        t = jnp.arange(L, dtype=jnp.float32)
        A_t = A[:, None] ** t[None, :]
        K = (C_vec[:, None] * A_t * B_vec[:, None])[:, None, :]
        x_t = jnp.transpose(x, (0, 2, 1))
        out = lax.conv_general_dilated(x_t, K, window_strides=(1,), padding=[(L - 1, L - 1)], dimension_numbers=('NCH', 'OIH', 'NCH'), feature_group_count=D)
        out = out[..., :L] + D_vec[None, :, None] * x_t
        out = jnp.transpose(out, (0, 2, 1))
        out = jnp.dot(jax.nn.gelu(out, approximate=False), W_proj.T) + b_proj
        return _layer_norm(x + out, gamma, beta)

    def _L0_ffn_ref(hidden_states, router_w, router_b, gate_up_proj, gate_up_bias, down_proj, down_bias):
        import jax, jax.numpy as jnp
        import numpy as np
        B, S, H, E, K, I = (1, 64, 128, 16, 4, 128)
        ALPHA, LIMIT = (1.702, 7.0)
        b, s, h = hidden_states.shape
        x = hidden_states.reshape(-1, h)
        logits = x @ router_w + router_b
        topv, topi = jax.lax.top_k(logits, K)
        topw = jax.nn.softmax(topv, axis=-1)
        one_hot = (topi[..., None] == jnp.arange(E)).astype(topw.dtype)
        scores = jnp.einsum('tk,tke->te', topw, one_hot)
        gu = jnp.einsum('th,ehf->tef', x, gate_up_proj) + gate_up_bias
        gate = jnp.minimum(gu[..., ::2], LIMIT)
        up = jnp.clip(gu[..., 1::2], -LIMIT, LIMIT)
        glu = gate * jax.nn.sigmoid(gate * ALPHA)
        act = (up + 1.0) * glu
        expert_out = jnp.einsum('tei,eih->teh', act, down_proj) + down_bias
        out = jnp.einsum('te,teh->th', scores, expert_out)
        return out.reshape(b, s, h)

    def _L1_attn_ref(x, Wq, Wk, Wv, Wo, W_down_kv, W_up_k, W_up_v):
        import jax, jax.numpy as jnp
        import numpy as np
        D_MODEL = 128
        N_HEADS = 16
        HEAD_DIM = D_MODEL // N_HEADS
        D_LATENT = 32
        LAMBDA_DECAY = 0.01
        TIME_STEP = 0.01
        CLAMP = 10000.0

        def _reference_tuple_inner(x, Wq, Wk, Wv, Wo, W_down_kv, W_up_k, W_up_v):
            B, S, _ = x.shape
            q = x @ Wq
            k = x @ Wk
            v = x @ Wv
            latent_kv = (k + v) @ W_down_kv
            k_rec = latent_kv @ W_up_k
            v_rec = latent_kv @ W_up_v

            def heads(t):
                return t.reshape(B, S, N_HEADS, HEAD_DIM).transpose(0, 2, 1, 3)
            qh, kh, vh = (heads(q), heads(k_rec), heads(v_rec))
            scale = 1.0 / (jnp.sqrt(jnp.float32(D_MODEL)) + 1e-08)
            scores = jnp.einsum('bhqd,bhkd->bhqk', qh, kh) * scale
            scores = jnp.clip(jnp.nan_to_num(scores, nan=-1000000000.0), -CLAMP, CLAMP)
            idx = jnp.arange(S, dtype=jnp.float32)
            decay = jnp.exp(-LAMBDA_DECAY * TIME_STEP * jnp.abs(idx[:, None] - idx[None, :]))
            scores = scores * decay[None, None, :, :]
            scores = jnp.clip(jnp.nan_to_num(scores, nan=-1000000000.0), -CLAMP, CLAMP)
            attn = jax.nn.softmax(scores, axis=-1)
            out = jnp.einsum('bhqk,bhkd->bhqd', attn, vh)
            out = out.transpose(0, 2, 1, 3).reshape(B, S, D_MODEL)
            return (out @ Wo, latent_kv)
        return _reference_tuple_inner(x, Wq, Wk, Wv, Wo, W_down_kv, W_up_k, W_up_v)[0]

    def _L1_ffn_ref(x, base_w, base_b, gate_w, lora_A, lora_B):
        import jax, jax.numpy as jnp
        import numpy as np
        D_MODEL = 128
        D_OUT = 128
        RANK = 16
        NUM_TRUE = 8
        NUM_NULL = 2
        TOP_K = 2
        SCALING = 32.0 / 16.0
        xf = x.reshape(-1, x.shape[-1])
        logits = jnp.einsum('td,ed->te', xf, gate_w)
        probs = jax.nn.softmax(logits, axis=-1)
        weights, selected = jax.lax.top_k(probs, TOP_K)
        true_mask = (selected < NUM_TRUE).astype(weights.dtype)
        tw = weights * true_mask
        denom = tw.sum(axis=-1, keepdims=True)
        denom = jnp.where(denom > 0, denom, jnp.ones_like(denom))
        nw = tw / denom
        onehot = jax.nn.one_hot(selected, NUM_TRUE, dtype=nw.dtype)
        ew = jnp.einsum('tk,tke->te', nw, onehot)
        z = jnp.einsum('td,erd->ter', xf, lora_A)
        moe = jnp.einsum('ter,te,eor->to', z, ew, lora_B) * SCALING
        base = jnp.einsum('td,od->to', xf, base_w) + base_b
        out = (base + moe).reshape(x.shape[:-1] + (D_OUT,))
        return out
    x = L0_attn_x
    x = x + 0.5 * _L0_ffn_ref(_layernorm(x, axis=-1), L0_ffn_router_w, L0_ffn_router_b, L0_ffn_gate_up_proj, L0_ffn_gate_up_bias, L0_ffn_down_proj, L0_ffn_down_bias)
    x = x + _L0_attn_ref(_layernorm(x, axis=-1), L0_attn_A_param, L0_attn_B_vec, L0_attn_C_vec, L0_attn_D_vec, L0_attn_W_proj, L0_attn_b_proj, L0_attn_gamma, L0_attn_beta)
    x = x + 0.5 * _L0_ffn_ref(_layernorm(x, axis=-1), L0_ffn_router_w, L0_ffn_router_b, L0_ffn_gate_up_proj, L0_ffn_gate_up_bias, L0_ffn_down_proj, L0_ffn_down_bias)
    x = x + 0.5 * _L1_ffn_ref(_layernorm(x, axis=-1), L1_ffn_base_w, L1_ffn_base_b, L1_ffn_gate_w, L1_ffn_lora_A, L1_ffn_lora_B)
    x = x + _L1_attn_ref(_layernorm(x, axis=-1), L1_attn_Wq, L1_attn_Wk, L1_attn_Wv, L1_attn_Wo, L1_attn_W_down_kv, L1_attn_W_up_k, L1_attn_W_up_v)
    x = x + 0.5 * _L1_ffn_ref(_layernorm(x, axis=-1), L1_ffn_base_w, L1_ffn_base_b, L1_ffn_gate_w, L1_ffn_lora_A, L1_ffn_lora_B)
    return x

_drawn_inputs = setup_inputs


def setup_inputs(seed=0):
    import zlib

    import numpy as np

    out = dict(_drawn_inputs(seed))
    spreads = {'L0_attn_gamma': (1.0, 0.2), 'L0_attn_beta': (0.0, 0.1)}
    factors = {'L0_attn_A_param': 8.0,
     'L0_attn_B_vec': 6.495,
     'L0_attn_C_vec': 5.479,
     'L0_attn_b_proj': 8.0,
     'L0_ffn_router_w': 5.307,
     'L0_ffn_router_b': 8.0,
     'L0_ffn_gate_up_proj': 5.744,
     'L0_ffn_gate_up_bias': 8.0,
     'L0_ffn_down_proj': 5.644,
     'L0_ffn_down_bias': 7.76,
     'L1_attn_Wq': 8.0,
     'L1_attn_Wk': 8.0,
     'L1_attn_Wv': 8.0,
     'L1_attn_Wo': 8.0,
     'L1_attn_W_down_kv': 8.0,
     'L1_attn_W_up_k': 8.0,
     'L1_attn_W_up_v': 8.0,
     'L1_ffn_base_b': 8.0,
     'L1_ffn_gate_w': 3.008,
     'L1_ffn_lora_A': 2.819,
     'L1_ffn_lora_B': 2.757}
    for name, (base, spread) in spreads.items():
        noise = np.random.default_rng([zlib.crc32(name.encode()), seed]).standard_normal(out[name].shape)
        drawn = base * np.exp(spread * noise) if base else spread * noise
        out[name] = jnp.asarray(drawn.astype(out[name].dtype))
    for name, factor in factors.items():
        out[name] = (out[name] * factor).astype(out[name].dtype)
    return out
```

```python
import numpy as np
import concourse.bass as bass
from concourse import mybir
from contextlib import ExitStack

F32 = mybir.dt.float32
F32R = mybir.dt.float32r
ALU = mybir.AluOpType
ACT = mybir.ActivationFunctionType
AX = mybir.AxisListType

D = 128
NB, L = 2, 1024
T = NB * L
CH = 512
NC = T // CH
TPC = CH // 128
EPS = 1e-5
E0, TOP0 = 16, 4
E1, TOP1, TRUE1, RANK = 10, 2, 8, 16
LIMIT, ALPHA = 7.0, 1.702
GLU_AT_LIMIT = LIMIT / (1.0 + float(np.exp(-ALPHA * LIMIT)))
SENTINEL, TAKEN = 3.0e38, -3.0e38

LN_FFN0A, LN_SSM, LN_INNER, LN_FFN0B, LN_FFN1A, LN_ATTN, LN_FFN1B = range(7)
X_IN, X_FFN0A, X_SSM, X_FFN0B, X_FFN1A, X_ATTN, X_FFN1B = range(7)

H, HD = 16, 8
LAT = 32
G4, HG = 4, 4
KB = L // 128
QC = L // CH
SCALE = float(np.float32(1.0) / (np.sqrt(np.float32(D)) + np.float32(1e-8)))
CLAMP = 1.0e4
DECAY = 0.01 * 0.01
VW = HD + 1
NP = 4
SAFE_BOUND = 40.0
WQ, WK, WV, WO = 4, 5, 6, 7
PICK_STEPS = 6
ROUTERS = {"ffn0a": 0, "ffn0b": 1, "ffn1a": 2, "ffn1b": 3}


def nth(group, c):
    return group * NC + c + 1


def nth_hi(n, c):
    return nth(n - (n > LN_INNER), c)


def build(nc, io):
    ctx = ExitStack()
    with ctx:
        def sb(name, shape, dt=F32):
            return ctx.enter_context(nc.sbuf_tensor(name, shape, dt))

        def sem(name):
            return ctx.enter_context(nc.semaphore(name))

        x = sb("x", [D, T])
        x_tok = sb("x_tok", [128, T // 128, D])
        xn_hi = sb("xn_hi", [D, T], F32R)
        xn_lo = sb("xn_lo", [D, T], F32R)
        ident = sb("ident", [128, 128])
        raw_w = sb("raw_w", [128, E0 * 3 * D])
        w0_hi = sb("w0_hi", [128, E0, 3, D], F32R)
        w0_lo = sb("w0_lo", [128, E0, 3, D], F32R)
        b_gate = sb("b_gate", [128, E0])
        b_up = sb("b_up", [128, E0])
        b_up1 = sb("b_up1", [128, E0])
        raw_s = sb("raw_s", [128, 8, D])
        sq_hi = sb("sq_hi", [128, 8, D], F32R)
        sq_lo = sb("sq_lo", [128, 8, D], F32R)
        raw_r = sb("raw_r", [128, E0 + 16])
        r_hi = sb("r_hi", [128, E0 + 16], F32R)
        r_lo = sb("r_lo", [128, E0 + 16], F32R)
        raw_db = sb("raw_db", [2 * E0, D])
        db_hi = sb("db_hi", [2 * E0, D], F32R)
        db_lo = sb("db_lo", [2 * E0, D], F32R)
        router_b = sb("router_b", [128, E0])
        sel0_all = sb("sel0", [128, E0, 128], F32R)
        sel0 = sel0_all[0:2 * E0]
        sel1 = sb("sel1", [2 * TRUE1, 128], F32R)
        vecs = sb("vecs", [128, 8])
        ab = sb("ab", [128, 8])
        pw = sb("pw", [128, L])
        zero1 = sb("zero1", [128, 1])
        half_pow = sb("half_pow", [128, TPC])

        stats = sb("stats", [128, 2, TPC, 6])
        mean_var = sb("mean_var", [128, 2, TPC, 2])
        var_eps = sb("var_eps", [128, 2, TPC])
        rstd = sb("rstd", [128, 2, TPC])
        xt = sb("xt", [128, 2, TPC, D])

        logit = sb("logit", [128, 2, TPC, 20])
        logit1 = sb("logit1", [128, 2, TPC, 16])
        top8 = sb("top8", [128, 2, TPC, 8])
        taken = sb("taken", [128, 2, TPC, 20])
        shifted = sb("shifted", [128, 2, TPC, 16])
        expd = sb("expd", [128, 2, TPC, 16])
        mask = sb("mask", [128, 2, TPC, 16])
        picked = sb("picked", [128, 2, TPC, 16])
        denom = sb("denom", [128, 2, TPC])
        is_zero = sb("is_zero", [128, 2, TPC])
        denom1 = sb("denom1", [128, 2, TPC])
        recip = sb("recip", [128, 2, TPC])
        share = sb("share", [128, 2, TPC, 16])
        share_hl = sb("share_hl", [128, 2, TPC, 2 * E0])
        score_all = sb("score_t", [128, T], F32R)
        score_t = score_all[0:2 * E0]

        NACT = 3
        glu = sb("glu", [128, 2, CH])
        up = sb("up", [128, 2, CH])
        glu_s = sb("glu_s", [128, 2, CH])
        act = sb("act", [128, NACT, CH])
        act_hi = sb("act_hi", [128, NACT, CH], F32R)
        act_lo = sb("act_lo", [128, NACT, CH], F32R)

        xn = raw_w[:, 0:T]
        ssm_in = raw_w[:, T:T + 2 * CH]
        ssm_sum = raw_w[:, 2 * T - 2 * CH:2 * T]
        ssm_y = glu
        ssm_z = up
        gelu = glu_s
        resid = sb("resid", [128, 2, CH])
        tmp = sb("tmp", [128, 2, CH])

        w_down = sb("w_down", [D, LAT])
        w_up = sb("w_up", [LAT, 2, D])
        sel_h = sb("sel_h", [128, G4, 4, 128], F32R)
        head_rows = sb("head_rows", [128, HG])
        same_head = sb("same_head", [128, 128])
        q_decay = sb("q_decay", [128, 2, L])
        k_decay = sb("k_decay", [128, 2, KB])
        fix = sb("fix", [128, CH])
        minus_one = sb("minus_one", [1, 128])
        half_one = sb("half_one", [1, 1])
        q_stack = (w0_hi[:].rearrange("p e w d -> p (e w d)")[:, 0:G4 * L].rearrange("p (g t) -> p g t", g=G4),
                   w0_lo[:].rearrange("p e w d -> p (e w d)")[:, 0:G4 * L].rearrange("p (g t) -> p g t", g=G4))
        k_parts = [w[:].rearrange("p e w d -> p (e w d)")[:, G4 * L:(G4 + 2) * L].rearrange("p (g t) -> p g t", g=2)
                   for w in (w0_hi, w0_lo)]
        k_stack = [k_parts[g // 2][:, g % 2, :] for g in range(G4)]
        values = raw_w[:, 0:KB * H * VW].rearrange("p (k h v) -> p k h v", k=KB, h=H)
        def head_keys(b, g, j):
            flat = lambda t: t.rearrange("p e t -> p (e t)")
            return (flat(act_hi[:, 0:2, :]), flat(act_lo[:, 0:2, :]), xn_hi[:, L * b:L * (b + 1)],
                    xn_lo[:, L * b:L * (b + 1)], score_all[:, 0:L], score_all[:, L:2 * L],
                    flat(sel0_all[:])[:, 0:L], flat(sel0_all[:])[:, L:2 * L])[g % 2 * HG + j]

        probs = raw_w[:, E0 * 3 * D - NP * 2 * CH:].rearrange("p (n t) -> p n t", n=NP)
        qk_f = glu_s
        kv_f, lat_f, q_sq, k_sq = glu[:, 0, :], glu[0:LAT, 1, :], up[:, 0, :], up[:, 1, :]
        gen_small = sb("gen_small", [128, 3])
        head_max = sb("head_max", [128, NB, 2, QC])
        tops = sb("tops", [128, NB, 3])
        bound = sb("bound", [1, NB, 2])
        small_scores = sb("small_scores", [1, NB], mybir.dt.int32)
        minus_c = sb("minus_c", [128, NB])
        out_t = resid
        out_recip = sb("out_recip", [128, TPC, HG])

        flat = raw_w[:, E0 * 3 * D - NP * 2 * CH:]
        gen_s, gen_pt, gen_decays = flat[:, 0:L], flat[:, L:2 * L], flat[:, 2 * L:4 * L - 128]
        gen_k = act_hi[:, 0:2, :].rearrange("p a t -> p (a t)")
        gen_q = act_hi[:, 2, 0:128]
        gen_v = tmp[:].rearrange("p a t -> p (a t)")[:, 0:KB * HG * VW].rearrange("p (k h v) -> p k h v", k=KB, h=HG)
        gen_decay = up[:].rearrange("p a t -> p (a t)")
        gen_heads = tmp[:, 1, CH - HG * HD:]
        gen_unscale, gen_recip, gen_spare = gen_small[:, 0:1], gen_small[:, 1:2], gen_small[:, 2:3]

        bank = ctx.enter_context(nc.psum_tensor("bank", [128, 8, CH], F32))
        T1, T2, LG, ST = (0, 1), (2, 3), 4, 5
        G, U, S, O = (0, 1), (2, 3), (4, 5), (6, 7)

        names = """x_loaded0 x_loaded1 x_loaded2 x_loaded3 half_scaled w_loaded0 w_loaded1 w_loaded2 w_loaded3 small_loaded out_stored
            ident_loaded consts_ready x_ready tok_in t1_ready stats_step stats_ready eps_step
            rstd_ready normalized t2_ready xn_hi_ready xn_ready w0_hi_ready w0_lo_ready
            small_hi_ready small_ready prep_step ab_ready
            logits_ready logit_step top_step taken_step shift_ready exp_ready pick_step
            share_hi_step share_ready score_psum_ready score_ready
            g_ready u_ready s_ready glu_ready up_ready glu_s_ready act_ready hi_ready lo_ready
            down_done
            ssm_step y_ready gelu_ready gelu_hi_ready gelu_lo_ready proj_ready resid_ready
            z_ready z_copied ew_ready zs_ready zs_hi_ready zs_lo_ready out1_ready fin_ready out_copied
            cast_loaded prep_loaded
            qkv_ready q_decayed q_sq_ready kv_copied lat_ready lat_copied kv_rec_ready k_sq_ready
            k_lo_ready v_copied q_hi_ready q_lo_ready norms_ready maxes_ready tops_ready
            tops_row bound_step bound_ready sqrt_ready minus_c_ready flag_ready neg_ready
            stack_ready stack_copied stack_copied_v ao_ready ao_t_ready ao_hi_ready ao_lo_ready attn_out""".split()
        names += [f"{n}{b}" for b in range(NB) for n in
                  ("keys_masked", "scored", "fixed", "exped", "pv_done", "ot_copied", "ot_ready", "recip_ready", "normed",
                   "gen_staged", "gen_scored", "gen_clipped", "gen_decayed", "gen_max", "gen_neg", "gen_probs",
                   "gen_t", "gen_tc", "gen_pv", "gen_recip", "gen_out", "gen_table")]
        s = {n: sem(n) for n in names}

        block = ctx.enter_context(nc.Block())

        def chunk(c):
            return slice(c * CH, (c + 1) * CH)

        def skewed(stages, n=NC):
            for step in range(n + len(stages) - 1):
                for i, stage in reversed(list(enumerate(stages))):
                    if 0 <= step - i < n:
                        stage(step - i)

        UNITS = G4 * QC * KB * 2

        def unit(u):
            return u // (4 * KB), u // (2 * KB) % QC, u // 2 % KB, u % 2

        def fixes(u):
            g, qc, kb, hp = unit(u)
            return 2 * (CH // 128) * (u // (2 * KB)) + 2 * (kb % (CH // 128)) + hp + 1

        def stack_place(i, c):
            g, kind = i // 3, i % 3
            at = slice(CH * (c % QC), CH * (c % QC + 1))
            return k_stack[g][:, at] if kind == 2 else q_stack[kind][:, g, at]

        def idle(c):
            pass

        SMALL = [(raw_r[:, 0:E0], "router_w"), (raw_r[:, E0:E0 + E1], "gate_w"),
                 (router_b[:], "router_b"), (raw_db[0:E0, :], "down_bias"), (raw_db[E0:2 * E0, :], "down_bias"),
                 (b_gate[:], "b_gate"), (b_up[:], "b_up"), (vecs[:], "vecs"), (raw_s[:], "squares")]
        LATER = [(w_down[:], "w_down"), (w_up[:], "w_up"), (same_head[:], "same_head"),
                 (head_rows[:], "head_rows"), (q_decay[:], "q_decay"), (k_decay[:], "k_decay"), (fix[:], "fix")]

        @block.sync
        def _(sp):
            x_rows = io["x"].rearrange("(n p) d -> p n d", p=128)
            sp.dma_start(ident[:], io["ident"]).then_inc(s["ident_loaded"], 16)
            for c in range(NC):
                sp.dma_start(x_tok[:, TPC * c:TPC * (c + 1), :], x_rows[:, TPC * c:TPC * (c + 1), :])\
                  .then_inc(s[f"x_loaded{c}"], 16)
            per = E0 // 4
            raw = raw_w[:].rearrange("p (e w d) -> p e w d", e=E0, w=3)
            for g in range(4):
                es = slice(per * g, per * (g + 1))
                sp.dma_start(raw[:, es, 0:2, :], io["gate_up"][:, es]).then_inc(s[f"w_loaded{g}"], 16)
                sp.dma_start(raw[:, es, 2, :], io["down"][:, es]).then_inc(s[f"w_loaded{g}"], 16)
            for dst, name in LATER:
                sp.dma_start(dst, io[name]).then_inc(s["prep_loaded"], 16)
            out_rows = io["out"].rearrange("(n p) d -> p n d", p=128)
            for c in range(NC):
                sp.wait_ge(s["out_copied"], c + 1)
                sp.dma_start(out_rows[:, TPC * c:TPC * (c + 1), :], x_tok[:, TPC * c:TPC * (c + 1), :])\
                  .then_inc(s["out_stored"], 16)
            sp.wait_ge(s["out_stored"], 16 * NC)

        @block.gpsimd
        def _(pool):
            for dst, name in SMALL:
                pool.dma_start(dst, io[name]).then_inc(s["small_loaded"], 16)
            for dst, name in ((sel0, "sel0"), (sel1, "sel1"), (sel_h, "sel_h")):
                pool.dma_start(dst[:], io[name]).then_inc(s["cast_loaded"], 16)
            pool.memset(half_pow[:], -0.5)
            pool.memset(minus_one[:], -1.0)
            pool.memset(half_one[:], 0.5)
            pool.memset(zero1[:], 0.0)
            pool.memset(raw_r[:, E0 + E1:], 0.0)
            pool.memset(logit[:, :, :, E0:20], SENTINEL)
            pool.memset(logit1[:, :, :, E1:16], SENTINEL)
            pool.memset(share_hl[:], 0.0)
            pool.memset(pw[:, 0:1], 1.0).then_inc(s["consts_ready"], 1)

            def norm(n):
                for c in range(NC):
                    k = n * NC + c
                    pool.wait_ge(s["stats_ready"], k + 1)
                    if k >= 2:
                        pool.wait_ge(s["normalized"], k - 1)
                    pool.tensor_scalar(var_eps[:, k % 2, :], mean_var[:, k % 2, :, 1], EPS, None, ALU.add)\
                        .then_inc(s["eps_step"], 1)
                    pool.wait_ge(s["eps_step"], k + 1)
                    pool.tensor_tensor(rstd[:, k % 2, :], var_eps[:, k % 2, :], half_pow[:], ALU.pow)\
                        .then_inc(s["rstd_ready"], 1)

            def experts(f):
                for j in range(f * NC * E0, (f + 1) * NC * E0):
                    pool.wait_ge(s["hi_ready"], j + 1)
                    if j >= NACT:
                        pool.wait_ge(s["down_done"], j - NACT + 1)
                    pool.tensor_tensor(act_lo[:, j % NACT, :], act[:, j % NACT, :],
                                       act_hi[:, j % NACT, :].bitcast(F32), ALU.subtract)\
                        .then_inc(s["lo_ready"], 1)

            norm(LN_FFN0A)
            experts(0)
            norm(LN_SSM)
            norm(LN_INNER)
            norm(LN_FFN0B)
            experts(1)
            norm(LN_FFN1A)
            norm(LN_ATTN)
            for b in range(NB):
                pool.wait_ge(s["bound_ready"], b + 1)
                pool.tensor_tensor(bound[:, b, 1:2], bound[:, b, 0:1], half_one[:], ALU.pow)\
                    .then_inc(s["sqrt_ready"], 1)
                pool.wait_ge(s["minus_c_ready"], b + 1)
                pool.wait_ge(s["flag_ready"], b + 1)
                fast = pool.value_load(small_scores[0:1, b:b + 1], min_val=0, max_val=1)
                with pool.If(fast):
                    for g in range(G4):
                        if g >= 2:
                            pool.wait_ge(s[f"scored{b}"], UNITS // G4 * (g - 1))
                        for j in range(HG):
                            pool.tensor_scalar(head_keys(b, g, j), k_stack[g].bitcast(F32), head_rows[:, j:j + 1],
                                               None, ALU.mult).then_inc(s[f"keys_masked{b}"], 1)
            norm(LN_FFN1B)

        @block.scalar
        def _(eng):
            def split_small():
                eng.wait_ge(s["small_loaded"], 16 * len(SMALL))
                eng.wait_ge(s["consts_ready"], 1)
                eng.activation(raw_s[:, 1, :], raw_s[:, 1, :], ACT.Copy, scale=0.5).then_inc(s["half_scaled"], 1)
                eng.wait_ge(s["half_scaled"], 1)
                for dst, src in ((r_hi, raw_r), (db_hi, raw_db), (sq_hi, raw_s)):
                    eng.activation(dst[:], src[:], ACT.Copy).then_inc(s["small_hi_ready"], 1)
                eng.activation(ab[:, 0:1], vecs[:, 0:1], ACT.Exp, scale=-1.0).then_inc(s["small_hi_ready"], 1)

            def split_experts():
                raw = raw_w[:].rearrange("p (e w d) -> p e w d", e=E0, w=3)
                for g in range(4):
                    es = slice(E0 // 4 * g, E0 // 4 * (g + 1))
                    eng.wait_ge(s[f"w_loaded{g}"], 32)
                    eng.activation(w0_hi[:, es], raw[:, es], ACT.Copy).then_inc(s["w0_hi_ready"], 1)

            def norm_hi(n, c):
                k = n * NC + c
                eng.wait_ge(s["t2_ready"], k + 1)
                dst = xn[:, chunk(c)] if n == LN_SSM else xn_hi[:, chunk(c)]
                eng.activation(dst, bank[:, T2[k % 2], :], ACT.Copy).then_inc(s["xn_hi_ready"], 1)

            def router_exp(r, c):
                kr = r * NC + c
                eng.wait_ge(s["shift_ready"], kr + 1)
                ne = E0 if r < 2 else E1
                eng.activation(expd[:, kr % 2, :, 0:ne], shifted[:, kr % 2, :, 0:ne], ACT.Exp)\
                   .then_inc(s["exp_ready"], 1)

            def router_out(r, c):
                kr = r * NC + c
                nr = 2 * E0 if r < 2 else 2 * TRUE1
                eng.wait_ge(s["score_psum_ready"], kr + 1)
                eng.activation(score_t[0:nr, chunk(c)], bank[0:nr, ST, :], ACT.Copy)\
                   .then_inc(s["score_ready"], 1)

            def experts(f):
                first, last = f * NC * E0, (f + 1) * NC * E0
                for j in range(first, last + 1):
                    if j < last:
                        e = j % E0
                        eng.wait_ge(s["g_ready"], j + 1)
                        if j >= 2:
                            eng.wait_ge(s["glu_s_ready"], j - 1)
                        eng.activation(glu[:, j % 2, :], bank[:, G[j % 2], :], ACT.Gelu_apprx_sigmoid,
                                       bias=b_gate[:, e:e + 1]).then_inc(s["glu_ready"], 1)
                    if j > first:
                        i = j - 1
                        eng.wait_ge(s["act_ready"], i + 1)
                        if i >= NACT:
                            eng.wait_ge(s["down_done"], i - NACT + 1)
                        eng.activation(act_hi[:, i % NACT, :], act[:, i % NACT, :], ACT.Copy)\
                           .then_inc(s["hi_ready"], 1)

            def ssm_gelu(c):
                eng.wait_ge(s["y_ready"], c + 1)
                if c >= 2:
                    eng.wait_ge(s["gelu_lo_ready"], c - 1)
                eng.activation(gelu[:, c % 2, :], ssm_z[:, c % 2, :], ACT.Gelu).then_inc(s["gelu_ready"], 1)
                eng.wait_ge(s["gelu_ready"], c + 1)
                if c >= 2:
                    eng.wait_ge(s["proj_ready"], c - 1)
                eng.activation(act_hi[:, c % 2, :], gelu[:, c % 2, :], ACT.Copy).then_inc(s["gelu_hi_ready"], 1)

            def lora(r):
                for c in range(NC):
                    k = (r - 2) * NC + c
                    eng.wait_ge(s["z_ready"], k + 1)
                    if k >= 2:
                        eng.wait_ge(s["zs_ready"], k - 1)
                    eng.activation(glu[:, k % 2, :], bank[:, G[k % 2], :], ACT.Copy).then_inc(s["z_copied"], 1)
                    eng.wait_ge(s["zs_ready"], k + 1)
                    if k >= 2:
                        eng.wait_ge(s["out1_ready"], k - 1)
                    eng.activation(act_hi[:, k % 2, :], act[:, k % 2, :], ACT.Copy).then_inc(s["zs_hi_ready"], 1)

            def attn_chunk(c):
                o = 4 * (c % 2)
                eng.wait_ge(s["qkv_ready"], c + 1)
                eng.activation(kv_f, bank[:, o + 1, :], ACT.Copy).then_inc(s["kv_copied"], 1)
                if c >= 1:
                    eng.wait_ge(s["norms_ready"], c)
                eng.wait_ge(s["q_decayed"], 2 * c + 2)
                eng.activation(q_sq, bank[:, o, :], ACT.Square, scale=SCALE).then_inc(s["q_sq_ready"], 1)
                eng.wait_ge(s["lat_ready"], c + 1)
                eng.activation(lat_f, bank[0:LAT, o + 2, :], ACT.Copy).then_inc(s["lat_copied"], 1)
                if c >= 1:
                    eng.wait_ge(s["stack_ready"], 3 * G4 * c)
                for i in range(2):
                    eng.wait_ge(s["q_decayed"], 2 * c + i + 1)
                    eng.activation(act_hi[:, i, :], qk_f[:, i, :], ACT.Copy).then_inc(s["q_hi_ready"], 1)
                eng.wait_ge(s["kv_rec_ready"], c + 1)
                eng.activation(act_hi[:, 2, :], bank[:, o + 3, :], ACT.Copy)
                eng.activation(k_sq, bank[:, o + 3, :], ACT.Square).then_inc(s["k_sq_ready"], 1)
                eng.activation(values[:, TPC * (c % QC):TPC * (c % QC + 1), :, 0:HD],
                               bank[:, o + 1, :].rearrange("p (t h d) -> p t h d", t=TPC, h=H), ACT.Copy)\
                   .then_inc(s["v_copied"], 1)

            def attn_stacks(c):
                for i in range(0, 3 * G4, 2):
                    n = c * 3 * G4 + i
                    eng.wait_ge(s["stack_ready"], n + 1)
                    eng.activation(stack_place(i, c), bank[:, i % 4, :], ACT.Copy).then_inc(s["stack_copied"], 1)

            def attn_fast(b):
                for u in range(UNITS):
                    g, qc, kb, hp = unit(u)
                    if kb // (CH // 128) == qc:
                        eng.wait_ge(s[f"fixed{b}"], fixes(u))
                    else:
                        eng.wait_ge(s[f"scored{b}"], u + 1)
                    if u >= NP:
                        eng.wait_ge(s[f"pv_done{b}"], (u - NP) // 2 + 1)
                    side = 1 if kb // (CH // 128) > qc else 0
                    pair = bank[:, 2 * (u % 3):2 * (u % 3) + 2, :].rearrange("p a q -> p (a q)")
                    eng.activation(probs[:, u % NP, :], pair, ACT.Exp, bias=minus_c[:, b:b + 1],
                                   scale=k_decay[:, side, kb:kb + 1]).then_inc(s[f"exped{b}"], 1)

            def attn_out(b):
                for c in range(QC * b, QC * (b + 1)):
                    eng.wait_ge(s["ao_t_ready"], c + 1)
                    eng.activation(act_hi[:, c % 2, :], bank[:, 4 + c % 2, :], ACT.Copy).then_inc(s["ao_hi_ready"], 1)

            def attention():
                skewed([idle, lambda c: norm_hi(LN_ATTN, c)])
                for b in range(NB):
                    for c in range(QC * b, QC * (b + 1)):
                        attn_chunk(c)
                        attn_stacks(c)
                    eng.wait_ge(s["neg_ready"], b + 1)
                    eng.activation(minus_c[:, b:b + 1], bank[:, 3, 0:1], ACT.Copy).then_inc(s["minus_c_ready"], 1)
                    eng.wait_ge(s["minus_c_ready"], b + 1)
                    eng.wait_ge(s["flag_ready"], b + 1)
                    fast = eng.value_load(small_scores[0:1, b:b + 1], min_val=0, max_val=1)
                    with eng.If(fast):
                        attn_fast(b)
                    with eng.Else():
                        attn_general(b)
                    attn_out(b)

            def attn_general(b):
                eng.dma_start(gen_decays, io["decay"]).then_inc(s[f"gen_table{b}"], 16)
                with eng.Fori(0, G4 * KB) as block_of_queries:
                    for j in range(HG):
                        n = block_of_queries * HG + j
                        eng.wait_ge(s[f"gen_neg{b}"], n + 1)
                        eng.activation(gen_s, gen_s, ACT.Exp, bias=tops[:, b, 1:2],
                                       accum_out=tops[:, b, 2:3]).then_inc(s[f"gen_probs{b}"], 1)
                        eng.wait_ge(s[f"gen_t{b}"], n + 1)
                        eng.activation(gen_pt, bank[:, 2:4, :].rearrange("p a q -> p (a q)"), ACT.Copy)\
                           .then_inc(s[f"gen_tc{b}"], 1)

            def routed_norm(n, r):
                skewed([idle, idle, lambda c: norm_hi(n, c), lambda c: router_exp(r, c), idle,
                        lambda c: router_out(r, c)])

            skewed([lambda c: norm_hi(LN_FFN0A, c)])
            split_small()
            skewed([lambda c: router_exp(0, c), idle, lambda c: router_out(0, c)])
            split_experts()
            experts(0)
            skewed([idle, idle, lambda c: norm_hi(LN_SSM, c), ssm_gelu])
            routed_norm(LN_FFN0B, 1)
            experts(1)
            routed_norm(LN_FFN1A, 2)
            lora(2)
            attention()
            routed_norm(LN_FFN1B, 3)
            lora(3)
            for c in range(NC):
                eng.wait_ge(s["fin_ready"], c + 1)
                eng.activation(x_tok[:, TPC * c:TPC * (c + 1), :],
                               bank[:, T1[c % 2], :].rearrange("p (t d) -> p t d", d=D), ACT.Copy)\
                   .then_inc(s["out_copied"], 1)

        @block.vector
        def _(eng):
            def take_in(c):
                eng.wait_ge(s["tok_in"], c + 1)
                eng.tensor_copy(x[:, chunk(c)], bank[:, O[c % 2], :]).then_inc(s["x_ready"], 1)

            def norm_stats(n, c):
                k = n * NC + c
                b = k % 2
                if n == LN_FFN0A:
                    eng.wait_ge(s[f"x_loaded{c}"], 16)
                    tiles = x_tok[:, TPC * c:TPC * (c + 1), :]
                else:
                    eng.wait_ge(s["t1_ready"], k + 1 - NC)
                    tiles = bank[:, T1[b], :].rearrange("p (t d) -> p t d", d=D)
                for t in range(TPC):
                    last = eng.bn_stats(stats[:, b, t, :], tiles[:, t, :])
                last.then_inc(s["stats_step"], 1)
                eng.wait_ge(s["stats_step"], k + 1)
                for t in range(TPC):
                    last = eng.bn_aggr(mean_var[:, b, t, :], stats[:, b, t, :])
                last.then_inc(s["stats_ready"], 1)

            def norm_rows(n, c):
                k = n * NC + c
                b = k % 2
                tiles = (x_tok[:, TPC * c:TPC * (c + 1), :] if n == LN_FFN0A else
                         bank[:, T1[b], :].rearrange("p (t d) -> p t d", d=D))
                eng.wait_ge(s["rstd_ready"], k + 1)
                if k >= 2:
                    eng.wait_ge(s["t2_ready"], k - 1)
                for t in range(TPC):
                    last = eng.tensor_scalar(xt[:, b, t, :], tiles[:, t, :], mean_var[:, b, t, 0:1],
                                             rstd[:, b, t:t + 1], ALU.subtract, ALU.mult)
                last.then_inc(s["normalized"], 1)

            def norm_lo(n, c):
                k = n * NC + c
                eng.wait_ge(s["xn_hi_ready"], nth_hi(n, c))
                eng.tensor_tensor(xn_lo[:, chunk(c)], bank[:, T2[k % 2], :],
                                  xn_hi[:, chunk(c)].bitcast(F32), ALU.subtract).then_inc(s["xn_ready"], 1)

            def router_pick(r, c):
                kr, b = r * NC + c, (r * NC + c) % 2
                moe = r < 2
                ne, sent = (E0, 20 - E0) if moe else (E1, 16 - E1)
                lg = logit if moe else logit1
                width = ne + sent
                eng.wait_ge(s["logits_ready"], kr + 1)
                src = bank[:, LG, 0:TPC * 16].rearrange("p (t e) -> p t e", e=16)[:, :, 0:ne]
                if moe:
                    eng.tensor_tensor(lg[:, b, :, 0:ne], src, router_b[:, None, :].to_broadcast([128, TPC, E0]),
                                      ALU.add).then_inc(s["logit_step"], 1)
                else:
                    eng.tensor_copy(lg[:, b, :, 0:ne], src).then_inc(s["logit_step"], 1)
                eng.wait_ge(s["logit_step"], kr + 1)
                for t in range(TPC):
                    last = eng.max(top8[:, b, t, :], lg[:, b, t, :])
                last.then_inc(s["top_step"], 1)
                eng.wait_ge(s["top_step"], kr + 1)
                for t in range(TPC):
                    eng.match_replace(out=taken[:, b, t, 0:width], in_to_replace=top8[:, b, t, :],
                                      in_values=lg[:, b, t, :], imm_value=TAKEN)
                eng.tensor_tensor(shifted[:, b, :, 0:ne], lg[:, b, :, 0:ne],
                                  top8[:, b, :, sent:sent + 1].to_broadcast([128, TPC, ne]), ALU.subtract)\
                    .then_inc(s["shift_ready"], 1)
                eng.wait_ge(s["shift_ready"], kr + 1)
                eng.tensor_tensor(mask[:, b, :, 0:ne], taken[:, b, :, 0:ne], lg[:, b, :, 0:ne],
                                  ALU.not_equal).then_inc(s["taken_step"], 1)

            def router_share(r, c):
                kr, b = r * NC + c, (r * NC + c) % 2
                moe = r < 2
                ne = E0 if moe else TRUE1
                eng.wait_ge(s["exp_ready"], kr + 1)
                eng.wait_ge(s["taken_step"], kr + 1)
                step = PICK_STEPS * kr

                def then(ins):
                    nonlocal step
                    step += 1
                    ins.then_inc(s["pick_step"], 1)
                    eng.wait_ge(s["pick_step"], step)

                then(eng.tensor_tensor(picked[:, b, :, 0:ne], expd[:, b, :, 0:ne], mask[:, b, :, 0:ne], ALU.mult))
                then(eng.tensor_reduce(denom[:, b, :], picked[:, b, :, 0:ne], axis=AX.X, op=ALU.add))
                then(eng.tensor_scalar(is_zero[:, b, :], denom[:, b, :], 0.0, None, ALU.is_equal))
                then(eng.tensor_tensor(denom1[:, b, :], denom[:, b, :], is_zero[:, b, :], ALU.add))
                then(eng.reciprocal(recip[:, b, :], denom1[:, b, :]))
                then(eng.scalar_tensor_tensor(out=share[:, b, :, 0:ne], in0=picked[:, b, :, 0:ne],
                                              scalar=0.5 if moe else 1.0,
                                              in1=recip[:, b, :, None].to_broadcast([128, TPC, ne]),
                                              op0=ALU.mult, op1=ALU.mult))
                if kr >= 2:
                    eng.wait_ge(s["score_psum_ready"], kr - 1)
                eng.tensor_copy(share_hl[:, b, :, 0:ne].bitcast(F32R), share[:, b, :, 0:ne])\
                    .then_inc(s["share_hi_step"], 1)
                eng.wait_ge(s["share_hi_step"], kr + 1)
                eng.tensor_tensor(share_hl[:, b, :, ne:2 * ne].bitcast(F32R), share[:, b, :, 0:ne],
                                  share_hl[:, b, :, 0:ne], ALU.subtract).then_inc(s["share_ready"], 1)

            def split_small():
                eng.wait_ge(s["small_hi_ready"], 4)
                for dst, src, hi in ((r_lo, raw_r, r_hi), (db_lo, raw_db, db_hi), (sq_lo, raw_s, sq_hi)):
                    eng.tensor_tensor(dst[:], src[:], hi[:].bitcast(F32), ALU.subtract)
                eng.tensor_scalar(b_up1[:], b_up[:], 1.0, None, ALU.add).then_inc(s["small_ready"], 1)

            def ssm_powers():
                step = 0

                def then(ins):
                    nonlocal step
                    step += 1
                    ins.then_inc(s["prep_step"], 1)
                    eng.wait_ge(s["prep_step"], step)

                then(eng.tensor_scalar(ab[:, 1:2], ab[:, 0:1], 1.0, None, ALU.add))
                then(eng.reciprocal(ab[:, 2:3], ab[:, 1:2]))
                then(eng.tensor_tensor(ab[:, 3:4], vecs[:, 2:3], vecs[:, 1:2], ALU.mult))
                then(eng.tensor_scalar(ab[:, 4:5], vecs[:, 7:8], 0.5, None, ALU.mult))
                eng.tensor_tensor_scan(pw[:, 1:L], ab[:, 2:3].to_broadcast([128, L - 1]),
                                       zero1[:, 0:1].to_broadcast([128, L - 1]), 1.0, ALU.mult, ALU.add)\
                    .then_inc(s["ab_ready"], 1)

            def split_experts():
                raw = raw_w[:].rearrange("p (e w d) -> p e w d", e=E0, w=3)
                for g in range(4):
                    es = slice(E0 // 4 * g, E0 // 4 * (g + 1))
                    eng.wait_ge(s["w0_hi_ready"], g + 1)
                    eng.tensor_tensor(w0_lo[:, es], raw[:, es], w0_hi[:, es].bitcast(F32), ALU.subtract)\
                        .then_inc(s["w0_lo_ready"], 1)

            def experts(f, version):
                for j in range(f * NC * E0, (f + 1) * NC * E0):
                    e, c = j % E0, j // E0 % NC
                    eng.wait_ge(s["u_ready"], j + 1)
                    eng.tensor_scalar(up[:, j % 2, :], bank[:, U[j % 2], :], b_up1[:, e:e + 1], 1.0 - LIMIT,
                                      ALU.add, ALU.max).then_inc(s["up_ready"], 1)
                    eng.wait_ge(s["glu_ready"], j + 1)
                    eng.wait_ge(s["s_ready"], j + 1)
                    eng.scalar_tensor_tensor(out=glu_s[:, j % 2, :], in0=glu[:, j % 2, :], scalar=GLU_AT_LIMIT,
                                             in1=bank[:, S[j % 2], :], op0=ALU.min, op1=ALU.mult)\
                        .then_inc(s["glu_s_ready"], 1)
                    eng.wait_ge(s["glu_s_ready"], j + 1)
                    if j >= NACT:
                        eng.wait_ge(s["lo_ready"], j - NACT + 1)
                    eng.scalar_tensor_tensor(out=act[:, j % NACT, :], in0=up[:, j % 2, :], scalar=1.0 + LIMIT,
                                             in1=glu_s[:, j % 2, :], op0=ALU.min, op1=ALU.mult)\
                        .then_inc(s["act_ready"], 1)
                    if e == 2 and c > 0:
                        add_out(f, c - 1)
                add_out(f, NC - 1)

            def add_out(f, c):
                eng.wait_ge(s["down_done"], E0 * nth(f, c))
                eng.tensor_tensor(x[:, chunk(c)], bank[:, O[c % 2], :], x[:, chunk(c)], ALU.add)\
                    .then_inc(s["x_ready"], 1)

            def ssm_scan(c):
                k = LN_SSM * NC + c
                at = c * CH % L
                b = c % 2
                step = 2 * c
                eng.wait_ge(s["xn_hi_ready"], nth_hi(LN_SSM, c))
                eng.wait_ge(s["ab_ready"], 1)
                eng.tensor_tensor(ssm_in[:, b * CH:(b + 1) * CH], bank[:, T2[k % 2], :], pw[:, at:at + CH],
                                  ALU.mult).then_inc(s["xn_ready"], 1)
                eng.wait_ge(s["xn_ready"], k + 1)
                first = 0.0 if at == 0 else ssm_sum[:, (1 - b) * CH + CH - 1:(1 - b) * CH + CH]
                eng.tensor_tensor_scan(ssm_sum[:, b * CH:(b + 1) * CH], ssm_in[:, b * CH:(b + 1) * CH],
                                       zero1[:, 0:1].to_broadcast([128, CH]), first, ALU.add, ALU.add)\
                    .then_inc(s["ssm_step"], 1)
                eng.wait_ge(s["ssm_step"], step + 1)
                hi = L - 1 - at
                back = pw[:, hi - CH + 1:hi + 1][:, ::-1]
                eng.scalar_tensor_tensor(out=ssm_y[:, b, :], in0=ssm_sum[:, b * CH:(b + 1) * CH],
                                         scalar=ab[:, 3:4], in1=back, op0=ALU.mult, op1=ALU.mult)\
                    .then_inc(s["ssm_step"], 1)
                eng.wait_ge(s["ssm_step"], step + 2)
                if c >= 2:
                    eng.wait_ge(s["gelu_ready"], c - 1)
                eng.scalar_tensor_tensor(out=ssm_z[:, b, :], in0=xn[:, chunk(c)], scalar=vecs[:, 3:4],
                                         in1=ssm_y[:, b, :], op0=ALU.mult, op1=ALU.add).then_inc(s["y_ready"], 1)

            def ssm_lo(c):
                eng.wait_ge(s["gelu_hi_ready"], c + 1)
                if c >= 2:
                    eng.wait_ge(s["proj_ready"], c - 1)
                eng.tensor_tensor(act_lo[:, c % 2, :], gelu[:, c % 2, :], act_hi[:, c % 2, :].bitcast(F32),
                                  ALU.subtract).then_inc(s["gelu_lo_ready"], 1)

            def ssm_resid(c):
                eng.wait_ge(s["proj_ready"], c + 1)
                k = LN_INNER * NC + c
                if c >= 2:
                    eng.wait_ge(s["t1_ready"], k - 1 - NC)
                eng.scalar_tensor_tensor(out=resid[:, c % 2, :], in0=bank[:, O[c % 2], :], scalar=vecs[:, 4:5],
                                         in1=xn[:, chunk(c)], op0=ALU.add, op1=ALU.add)\
                    .then_inc(s["resid_ready"], 1)

            def ssm_out(c):
                k = LN_INNER * NC + c
                eng.wait_ge(s["t2_ready"], k + 1)
                eng.tensor_scalar(tmp[:, c % 2, :], bank[:, T2[k % 2], :], vecs[:, 5:6], vecs[:, 6:7],
                                  ALU.mult, ALU.add).then_inc(s["xn_ready"], 1)
                eng.wait_ge(s["xn_ready"], k + 1)
                eng.tensor_tensor(x[:, chunk(c)], tmp[:, c % 2, :], x[:, chunk(c)], ALU.add)\
                    .then_inc(s["x_ready"], 1)

            def lora(r):
                for c in range(NC):
                    k = (r - 2) * NC + c
                    eng.wait_ge(s["z_copied"], k + 1)
                    eng.wait_ge(s["ew_ready"], k + 1)
                    if k >= 2:
                        eng.wait_ge(s["zs_lo_ready"], k - 1)
                    eng.tensor_tensor(act[:, k % 2, :], glu[:, k % 2, :], bank[:, S[k % 2], :], ALU.mult)\
                        .then_inc(s["zs_ready"], 1)
                    eng.wait_ge(s["zs_hi_ready"], k + 1)
                    if k >= 2:
                        eng.wait_ge(s["out1_ready"], k - 1)
                    eng.tensor_tensor(act_lo[:, k % 2, :], act[:, k % 2, :], act_hi[:, k % 2, :].bitcast(F32),
                                      ALU.subtract).then_inc(s["zs_lo_ready"], 1)
                    if c > 0:
                        lora_out(r, c - 1)
                lora_out(r, NC - 1)

            def lora_out(r, c):
                k = (r - 2) * NC + c
                eng.wait_ge(s["out1_ready"], k + 1)
                eng.scalar_tensor_tensor(out=x[:, chunk(c)], in0=bank[:, O[k % 2], :], scalar=ab[:, 4:5],
                                         in1=x[:, chunk(c)], op0=ALU.add, op1=ALU.add)\
                    .then_inc(s["x_ready"], 1)

            def routed_norm(n, r):
                skewed([lambda c: norm_stats(n, c), lambda c: norm_rows(n, c), lambda c: norm_lo(n, c),
                        lambda c: router_pick(r, c), lambda c: router_share(r, c)])

            def attn_chunk(c):
                o = 4 * (c % 2)
                eng.wait_ge(s["qkv_ready"], c + 1)
                if c == 0:
                    eng.wait_ge(s["prep_loaded"], 16 * len(LATER))
                at = slice(c % QC * CH, (c % QC + 1) * CH)
                for i in range(2):
                    eng.tensor_tensor(qk_f[:, i, :], bank[:, o, :], q_decay[:, i, at], ALU.mult)\
                        .then_inc(s["q_decayed"], 1)
                for i in range(2):
                    eng.wait_ge(s["q_hi_ready"], 2 * c + i + 1)
                    eng.tensor_tensor(act_lo[:, i, :], qk_f[:, i, :], act_hi[:, i, :].bitcast(F32), ALU.subtract)\
                        .then_inc(s["q_lo_ready"], 1)
                eng.wait_ge(s["k_sq_ready"], c + 1)
                eng.tensor_tensor(act_lo[:, 2, :], bank[:, o + 3, :], act_hi[:, 2, :].bitcast(F32), ALU.subtract)\
                    .then_inc(s["k_lo_ready"], 1)
                b = c // QC
                eng.wait_ge(s["norms_ready"], c + 1)
                eng.reduce_max(head_max[:, b, 0, c % QC:c % QC + 1], bank[:, o, :], axis=AX.X)
                eng.reduce_max(head_max[:, b, 1, c % QC:c % QC + 1], bank[:, o + 2, :], axis=AX.X)\
                    .then_inc(s["maxes_ready"], 1)

            def attn_stacks(c):
                for i in range(1, 3 * G4, 2):
                    n = c * 3 * G4 + i
                    eng.wait_ge(s["stack_ready"], n + 1)
                    eng.tensor_copy(stack_place(i, c), bank[:, i % 4, :]).then_inc(s["stack_copied_v"], 1)

            def attn_bound(b):
                eng.wait_ge(s["maxes_ready"], QC * (b + 1))
                eng.tensor_reduce(tops[:, b, 0:2], head_max[:, b], axis=AX.X, op=ALU.max)\
                    .then_inc(s["bound_step"], 1)
                eng.wait_ge(s["bound_step"], b + 1)
                eng.tensor_tensor(tops[:, b, 2:3], tops[:, b, 0:1], tops[:, b, 1:2], ALU.mult)\
                    .then_inc(s["tops_ready"], 1)
                eng.wait_ge(s["tops_row"], b + 1)
                eng.reduce_max(bound[:, b, 0:1], bank[0:1, 3, 0:128], axis=AX.X).then_inc(s["bound_ready"], 1)
                eng.wait_ge(s["bound_ready"], b + 1)
                eng.tensor_scalar(small_scores[:, b:b + 1], bound[:, b, 0:1], SAFE_BOUND ** 2, None, ALU.is_le)\
                    .then_inc(s["flag_ready"], 1)
                eng.wait_ge(s["flag_ready"], b + 1)

            def attn_fast(b):
                def take_out(n):
                    g, qc = n // QC, n % QC
                    o = 6 + n % 2
                    eng.wait_ge(s[f"pv_done{b}"], KB * (n + 1))
                    if n >= 2:
                        eng.wait_ge(s[f"ot_ready{b}"], n - 1)
                    eng.tensor_copy(out_t[:, n % 2, :], bank[:, o, :]).then_inc(s[f"ot_copied{b}"], 1)

                def normalize(n):
                    g, qc = n // QC, n % QC
                    rows = bank[:, 6 + n % 2, :].rearrange("p (t j m) -> p t j m", t=TPC, j=HG)
                    eng.wait_ge(s[f"ot_ready{b}"], n + 1)
                    eng.reciprocal(out_recip[:], rows[:, :, :, HD]).then_inc(s[f"recip_ready{b}"], 1)
                    eng.wait_ge(s[f"recip_ready{b}"], n + 1)
                    at = KB * b + TPC * qc
                    place = x_tok[:, at:at + TPC, HG * HD * g:HG * HD * (g + 1)]
                    ins = eng.tensor_tensor(place.rearrange("p t (j d) -> p t j d", j=HG), rows[:, :, :, 0:HD],
                                            out_recip[:, :, :, None].to_broadcast([128, TPC, HG, HD]), ALU.mult)
                    ins.then_inc(s[f"normed{b}"], 1)

                for u in range(UNITS):
                    g, qc, kb, hp = unit(u)
                    if kb // (CH // 128) == qc:
                        i = kb % (CH // 128)
                        w = 128 * (i + 1)
                        turned = fix[:, None, CH - w:CH].to_broadcast([128, 2, w])
                        pair = bank[:, 2 * (u % 3):2 * (u % 3) + 2, 0:w]
                        eng.wait_ge(s[f"scored{b}"], u + 1)
                        eng.tensor_tensor(pair, pair, turned, ALU.mult)\
                            .then_inc(s[f"fixed{b}"], 1)
                    n = u // (2 * KB)
                    if u % (2 * KB) == 4 and n > 0:
                        take_out(n - 1)
                    if u % (2 * KB) == 8 and n > 0:
                        normalize(n - 1)
                take_out(G4 * QC - 1)
                normalize(G4 * QC - 1)

            def attn_general(b):
                eng.wait_ge(s[f"gen_table{b}"], 16)
                for half in range(2):
                    with eng.Fori(0, 2) as gl:
                        with eng.Fori(0, KB) as qb:
                            eng.tensor_copy(gen_k, k_parts[half][:, bass.ds(gl, 1), :].bitcast(F32)
                                            .rearrange("p a t -> p (a t)"))
                            eng.tensor_copy(gen_q, q_stack[0][:, bass.ds(2 * half + gl, 1), bass.ds(128 * qb, 128)]
                                            .bitcast(F32).rearrange("p a t -> p (a t)"))
                            eng.tensor_copy(gen_unscale, k_decay[:, 0, bass.ds(qb, 1)])
                            eng.tensor_copy(gen_decay, gen_decays[:, bass.ds(L - 128 - 128 * qb, L)])
                            eng.tensor_copy(gen_v, values[:, :, bass.ds(HG * (2 * half + gl), HG), :])\
                                .then_inc(s[f"gen_staged{b}"], 1)
                            for j in range(HG):
                                n = (2 * half * KB + gl * KB + qb) * HG + j
                                eng.wait_ge(s[f"gen_scored{b}"], n + 1)
                                eng.tensor_scalar(gen_s, bank[:, 0:2, :].rearrange("p a q -> p (a q)"), gen_unscale,
                                                  -CLAMP, ALU.mult, ALU.max).then_inc(s[f"gen_clipped{b}"], 1)
                                eng.wait_ge(s[f"gen_clipped{b}"], n + 1)
                                eng.scalar_tensor_tensor(out=gen_s, in0=gen_s, scalar=CLAMP,
                                                         in1=gen_decay,
                                                         op0=ALU.min, op1=ALU.mult).then_inc(s[f"gen_decayed{b}"], 1)
                                eng.wait_ge(s[f"gen_decayed{b}"], n + 1)
                                eng.reduce_max(tops[:, b, 0:1], gen_s, axis=AX.X).then_inc(s[f"gen_max{b}"], 1)
                                eng.wait_ge(s[f"gen_max{b}"], n + 1)
                                eng.tensor_scalar(tops[:, b, 1:2], tops[:, b, 0:1], -1.0, None, ALU.mult)\
                                    .then_inc(s[f"gen_neg{b}"], 1)
                                eng.wait_ge(s[f"gen_pv{b}"], n + 1)
                                eng.reciprocal(gen_recip, tops[:, b, 2:3]).then_inc(s[f"gen_recip{b}"], 1)
                                eng.wait_ge(s[f"gen_recip{b}"], n + 1)
                                eng.tensor_scalar(gen_heads[:, HD * j:HD * (j + 1)], bank[:, 4, 0:HD], gen_recip,
                                                  None, ALU.mult).then_inc(s[f"gen_out{b}"], 1)
                            eng.wait_ge(s[f"gen_out{b}"], (2 * half * KB + gl * KB + qb + 1) * HG)
                            eng.tensor_copy(gen_spare, gen_recip)
                            eng.tensor_copy(x_tok[:, bass.ds(KB * b + qb, 1), bass.ds(HG * HD * (2 * half + gl), HG * HD)]
                                            .rearrange("p a d -> p (a d)"), gen_heads)

            def attn_out(b):
                for c in range(QC * b, QC * (b + 1)):
                    eng.wait_ge(s["ao_hi_ready"], c + 1)
                    eng.tensor_tensor(act_lo[:, c % 2, :], bank[:, 4 + c % 2, :], act_hi[:, c % 2, :].bitcast(F32),
                                      ALU.subtract).then_inc(s["ao_lo_ready"], 1)
                for c in range(QC * b, QC * (b + 1)):
                    eng.wait_ge(s["attn_out"], c + 1)
                    eng.tensor_tensor(x[:, chunk(c)], bank[:, 6 + c % 2, :], x[:, chunk(c)], ALU.add)\
                        .then_inc(s["x_ready"], 1)

            def attention():
                skewed([lambda c: norm_stats(LN_ATTN, c), lambda c: norm_rows(LN_ATTN, c),
                        lambda c: norm_lo(LN_ATTN, c)])
                eng.memset(values[:, :, :, HD:VW], 1.0)
                for b in range(NB):
                    for c in range(QC * b, QC * (b + 1)):
                        attn_chunk(c)
                        attn_stacks(c)
                    attn_bound(b)
                    fast = eng.value_load(small_scores[0:1, b:b + 1], min_val=0, max_val=1)
                    with eng.If(fast):
                        attn_fast(b)
                    with eng.Else():
                        attn_general(b)
                    eng.memset(tops[:, b, 0:1], 0.0).then_inc(s["ao_ready"], 1)
                    attn_out(b)

            eng.wait_ge(s["consts_ready"], 1)
            skewed([take_in, lambda c: norm_stats(LN_FFN0A, c), lambda c: norm_rows(LN_FFN0A, c),
                    lambda c: norm_lo(LN_FFN0A, c)])
            split_small()
            skewed([lambda c: router_pick(0, c), lambda c: router_share(0, c)])
            split_experts()
            ssm_powers()
            experts(0, X_FFN0A)
            skewed([lambda c: norm_stats(LN_SSM, c), lambda c: norm_rows(LN_SSM, c), ssm_scan, ssm_lo, ssm_resid,
                    lambda c: norm_stats(LN_INNER, c), lambda c: norm_rows(LN_INNER, c), ssm_out])
            routed_norm(LN_FFN0B, 1)
            experts(1, X_FFN0B)
            routed_norm(LN_FFN1A, 2)
            lora(2)
            attention()
            routed_norm(LN_FFN1B, 3)
            lora(3)

        @block.tensor
        def _(pe):
            def split_matmul(out, w_hi, w_lo, v_hi, v_lo, start, stop):
                pe.matmul(out, w_hi, v_hi, start=start, stop=False)
                pe.matmul(out, w_lo, v_hi, start=False, stop=False)
                return pe.matmul(out, w_hi, v_lo, start=False, stop=stop)

            def take_in(c):
                pe.wait_ge(s[f"x_loaded{c}"], 16)
                if c >= 2:
                    pe.wait_ge(s["x_ready"], nth(X_IN, c - 2))
                for t in range(TPC):
                    last = pe.transpose(bank[:, O[c % 2], 128 * t:128 * (t + 1)], x_tok[:, TPC * c + t, :], ident[:])
                last.then_inc(s["tok_in"], 1)

            def norm_in(n, c, version):
                k = n * NC + c
                b = k % 2
                if n == LN_INNER:
                    pe.wait_ge(s["resid_ready"], c + 1)
                else:
                    pe.wait_ge(s["x_ready"], nth(version, c))
                pe.wait_ge(s["normalized"], k - 1)
                for t in range(TPC):
                    src = (resid[:, c % 2, 128 * t:128 * (t + 1)] if n == LN_INNER else
                           x[:, c * CH + 128 * t:c * CH + 128 * (t + 1)])
                    last = pe.transpose(bank[:, T1[b], 128 * t:128 * (t + 1)], src, ident[:])
                last.then_inc(s["t1_ready"], 1)

            def norm_out(n, c):
                k = n * NC + c
                b = k % 2
                pe.wait_ge(s["normalized"], k + 1)
                if c >= 2:
                    pe.wait_ge(s["xn_ready"], k - 1)
                for t in range(TPC):
                    last = pe.transpose(bank[:, T2[b], 128 * t:128 * (t + 1)], xt[:, b, t, :], ident[:])
                last.then_inc(s["t2_ready"], 1)

            def router_logits(r, n, c):
                kr = r * NC + c
                w_hi, w_lo = (r_hi[:, 0:16], r_lo[:, 0:16]) if r < 2 else (r_hi[:, 16:32], r_lo[:, 16:32])
                pe.wait_ge(s["xn_ready"], nth(n, c))
                pe.wait_ge(s["small_ready"], 1)
                if kr >= 1:
                    pe.wait_ge(s["logit_step"], kr)
                for t in range(TPC):
                    at = slice(c * CH + 128 * t, c * CH + 128 * (t + 1))
                    out = bank[:, LG, 16 * t:16 * (t + 1)]
                    last = split_matmul(out, xn_hi[:, at], xn_lo[:, at], w_hi, w_lo, True, True)
                last.then_inc(s["logits_ready"], 1)

            def router_scores(r, c):
                kr = r * NC + c
                nr = 2 * E0 if r < 2 else 2 * TRUE1
                pe.wait_ge(s["share_ready"], kr + 1)
                if kr >= 1:
                    pe.wait_ge(s["score_ready"], kr)
                for t in range(TPC):
                    last = pe.transpose(bank[0:nr, ST, 128 * t:128 * (t + 1)], share_hl[:, kr % 2, t, 0:nr], ident[:])
                last.then_inc(s["score_psum_ready"], 1)

            def experts(f):
                def down(j):
                    e, c, slot = j % E0, j // E0 % NC, j % NACT
                    out = bank[:, O[c % 2], :]
                    if e == 0:
                        if c >= 2:
                            pe.wait_ge(s["x_ready"], nth(X_FFN0A if f == 0 else X_FFN0B, c - 2))
                        pe.matmul(out, db_hi[:], score_t[:, chunk(c)], start=True, stop=False)
                        pe.matmul(out, db_lo[:], score_t[:, chunk(c)], start=False, stop=False)
                    pe.wait_ge(s["hi_ready"], j + 1)
                    pe.matmul(out, w0_hi[:, e, 2, :], act_hi[:, slot, :], start=False, stop=False)
                    pe.matmul(out, w0_lo[:, e, 2, :], act_hi[:, slot, :], start=False, stop=False)
                    pe.wait_ge(s["lo_ready"], j + 1)
                    last = pe.matmul(out, w0_hi[:, e, 2, :], act_lo[:, slot, :], start=False, stop=e == E0 - 1)
                    last.then_inc(s["down_done"], 1)

                first, end = f * NC * E0, (f + 1) * NC * E0
                pe.wait_ge(s["cast_loaded"], 48)
                for j in range(first, end + 2):
                    if j < end:
                        e, c, b = j % E0, j // E0 % NC, j % 2
                        at = chunk(c)
                        if f == 0 and c == 0 and e % 4 == 0:
                            pe.wait_ge(s["w0_lo_ready"], e // 4 + 1)
                        if j >= 2:
                            pe.wait_ge(s["glu_ready"], j - 1)
                        split_matmul(bank[:, G[b], :], w0_hi[:, e, 0, :], w0_lo[:, e, 0, :],
                                     xn_hi[:, at], xn_lo[:, at], True, True).then_inc(s["g_ready"], 1)
                        if j >= 2:
                            pe.wait_ge(s["up_ready"], j - 1)
                        split_matmul(bank[:, U[b], :], w0_hi[:, e, 1, :], w0_lo[:, e, 1, :],
                                     xn_hi[:, at], xn_lo[:, at], True, True).then_inc(s["u_ready"], 1)
                        if j >= 2:
                            pe.wait_ge(s["glu_s_ready"], j - 1)
                        if j == first:
                            pe.wait_ge(s["score_ready"], nth(f, NC - 1))
                        pe.matmul(bank[:, S[b], :], sel0[:, e, :], score_t[:, at], start=True, stop=True)\
                          .then_inc(s["s_ready"], 1)
                    if j - 2 >= first:
                        down(j - 2)

            def ssm_proj(c):
                pe.wait_ge(s["gelu_lo_ready"], c + 1)
                if c >= 2:
                    pe.wait_ge(s["resid_ready"], c - 1)
                split_matmul(bank[:, O[c % 2], :], sq_hi[:, 0, :], sq_lo[:, 0, :], act_hi[:, c % 2, :],
                             act_lo[:, c % 2, :], True, True).then_inc(s["proj_ready"], 1)

            def lora(r):
                n = LN_FFN1A if r == 2 else LN_FFN1B

                def front(c):
                    k = (r - 2) * NC + c
                    at = chunk(c)
                    if k >= 2:
                        pe.wait_ge(s["z_copied"], k - 1)
                    split_matmul(bank[:, G[k % 2], :], sq_hi[:, 2, :], sq_lo[:, 2, :], xn_hi[:, at], xn_lo[:, at],
                                 True, True).then_inc(s["z_ready"], 1)
                    if k >= 2:
                        pe.wait_ge(s["zs_ready"], k - 1)
                    pe.wait_ge(s["score_ready"], nth(r, NC - 1))
                    pe.matmul(bank[:, S[k % 2], :], sel1[:], score_t[0:2 * TRUE1, at], start=True, stop=True)\
                      .then_inc(s["ew_ready"], 1)
                    if c >= 2:
                        pe.wait_ge(s["x_ready"], nth(X_FFN1A if r == 2 else X_FFN1B, c - 2))
                    split_matmul(bank[:, O[k % 2], :], sq_hi[:, 1, :], sq_lo[:, 1, :], xn_hi[:, at], xn_lo[:, at],
                                 True, False)

                def back(c):
                    k = (r - 2) * NC + c
                    pe.wait_ge(s["zs_lo_ready"], k + 1)
                    split_matmul(bank[:, O[k % 2], :], sq_hi[:, 3, :], sq_lo[:, 3, :], act_hi[:, k % 2, :],
                                 act_lo[:, k % 2, :], False, True).then_inc(s["out1_ready"], 1)

                skewed([front, back])

            def routed_norm(n, r, version):
                skewed([lambda c: norm_in(n, c, version), lambda c: norm_out(n, c),
                        lambda c: router_logits(r, n, c), idle, lambda c: router_scores(r, c)])

            def attn_chunk(c):
                o = 4 * (c % 2)
                at = chunk(c)
                pe.wait_ge(s["xn_ready"], nth(LN_ATTN, c))
                if c == 0:
                    pe.wait_ge(s["xn_ready"], nth(LN_ATTN, NC - 1))
                elif c == QC:
                    pe.wait_ge(s["x_ready"], nth(X_ATTN, QC - 1))
                split_matmul(bank[:, o, :], sq_hi[:, WQ, :], sq_lo[:, WQ, :], xn_hi[:, at], xn_lo[:, at], True, True)
                split_matmul(bank[:, o + 1, :], sq_hi[:, WK, :], sq_lo[:, WK, :], xn_hi[:, at], xn_lo[:, at],
                             True, False)
                split_matmul(bank[:, o + 1, :], sq_hi[:, WV, :], sq_lo[:, WV, :], xn_hi[:, at], xn_lo[:, at],
                             False, True).then_inc(s["qkv_ready"], 1)
                pe.wait_ge(s["prep_loaded"], 16 * len(LATER))
                pe.wait_ge(s["kv_copied"], c + 1)
                pe.matmul(bank[0:LAT, o + 2, :], w_down[:], kv_f, start=True, stop=True).then_inc(s["lat_ready"], 1)
                pe.wait_ge(s["lat_copied"], c + 1)
                pe.matmul(bank[:, o + 3, :], w_up[:, 0, :], lat_f, start=True, stop=True)
                for t in range(TPC):
                    last = pe.matmul(bank[:, o + 1, 128 * t:128 * (t + 1)], lat_f[:, 128 * t:128 * (t + 1)],
                                     w_up[:, 1, :], start=True, stop=True)
                last.then_inc(s["kv_rec_ready"], 1)
                pe.wait_ge(s["q_decayed"], 2 * c + 2)
                pe.wait_ge(s["k_sq_ready"], c + 1)
                pe.matmul(bank[:, o, :], same_head[:], q_sq, start=True, stop=True)
                pe.matmul(bank[:, o + 2, :], same_head[:], k_sq, start=True, stop=True)\
                  .then_inc(s["norms_ready"], 1)

            def attn_stacks(c):
                pe.wait_ge(s["cast_loaded"], 48)
                pe.wait_ge(s["maxes_ready"], c + 1)
                pe.wait_ge(s["k_lo_ready"], c + 1)
                pe.wait_ge(s["v_copied"], c + 1)
                for i in range(3 * G4):
                    n = c * 3 * G4 + i
                    g, kind = i // 3, i % 3
                    if n >= 4:
                        pe.wait_ge(s["stack_copied"] if i % 2 == 0 else s["stack_copied_v"], (n - 4) // 2 + 1)
                    part = 2 if kind == 2 else 0
                    out = bank[:, i % 4, :]
                    pe.matmul(out, sel_h[:, g, part, :], act_hi[:, kind, :], start=True, stop=False)
                    pe.matmul(out, sel_h[:, g, part + 1, :], act_lo[:, kind, :], start=False, stop=True)\
                      .then_inc(s["stack_ready"], 1)

            def attn_bound(b):
                pe.wait_ge(s["stack_copied"], 3 * G4 // 2 * QC * (b + 1))
                pe.wait_ge(s["stack_copied_v"], 3 * G4 // 2 * QC * (b + 1))
                pe.wait_ge(s["tops_ready"], b + 1)
                pe.transpose(bank[0:1, 3, 0:128], tops[:, b, 2:3], ident[:]).then_inc(s["tops_row"], 1)
                pe.wait_ge(s["sqrt_ready"], b + 1)
                pe.wait_ge(s["flag_ready"], b + 1)
                pe.matmul(bank[:, 3, 0:1], minus_one[:], bound[:, b, 1:2], start=True, stop=True)\
                  .then_inc(s["neg_ready"], 1)
                pe.wait_ge(s["minus_c_ready"], b + 1)

            def attn_fast(b):
                def scores(u):
                    g, qc, kb, hp = unit(u)
                    side = 1 if kb // (CH // 128) > qc else 0
                    if u >= 3:
                        pe.wait_ge(s[f"exped{b}"], u - 2)
                    if qc == 0 and kb == 0:
                        pe.wait_ge(s[f"keys_masked{b}"], HG * g + 2 * hp + 2)
                    for a in range(2):
                        j = 2 * hp + a
                        last = pe.matmul(bank[:, 2 * (u % 3) + a, :], head_keys(b, g, j)[:, 128 * kb:128 * (kb + 1)],
                                         q_stack[side][:, g, CH * qc:CH * (qc + 1)], start=True, stop=True)
                    last.then_inc(s[f"scored{b}"], 1)

                def weigh(t):
                    n, kb = t // KB, t % KB
                    g = n // QC
                    if kb == 0 and n >= 2:
                        pe.wait_ge(s[f"normed{b}"], n - 1)
                    for j in range(HG):
                        u = 2 * t + j // 2
                        pe.wait_ge(s[f"exped{b}"], u + 1)
                        last = pe.matmul(bank[32 * j:32 * j + VW, 6 + n % 2, :], values[:, kb, HG * g + j, :],
                                         probs[:, u % NP, CH * (j % 2):CH * (j % 2 + 1)],
                                         start=kb == 0, stop=kb == KB - 1, tile_position=(0, 32 * j))
                    last.then_inc(s[f"pv_done{b}"], 1)

                def turn(n):
                    pe.wait_ge(s[f"ot_copied{b}"], n + 1)
                    for t in range(TPC):
                        last = pe.transpose(bank[:, 6 + n % 2, 128 * t:128 * (t + 1)],
                                            out_t[:, n % 2, 128 * t:128 * (t + 1)], ident[:])
                    last.then_inc(s[f"ot_ready{b}"], 1)

                steps = UNITS // 2
                for t in range(steps + 1):
                    if t < steps:
                        scores(2 * t)
                        scores(2 * t + 1)
                    if t >= 1:
                        weigh(t - 1)
                    if t % KB == 4 and t >= KB:
                        turn(t // KB - 1)
                turn(G4 * QC - 1)

            def attn_general(b):
                with pe.Fori(0, G4 * KB) as block_of_queries:
                    pe.wait_ge(s[f"gen_staged{b}"], block_of_queries + 1)
                    for j in range(HG):
                        n = block_of_queries * HG + j
                        rows = slice(32 * j, 32 * (j + 1))
                        for a in range(2):
                            last = pe.matmul(bank[:, a, :], act_hi[rows, 2, 0:128], act_hi[rows, a, :],
                                             start=True, stop=True)
                        last.then_inc(s[f"gen_scored{b}"], 1)
                        pe.wait_ge(s[f"gen_probs{b}"], n + 1)
                        for kb in range(KB):
                            last = pe.transpose(bank[:, 2 + kb // 4, 128 * (kb % 4):128 * (kb % 4 + 1)],
                                                gen_s[:, 128 * kb:128 * (kb + 1)], ident[:])
                        last.then_inc(s[f"gen_t{b}"], 1)
                        pe.wait_ge(s[f"gen_tc{b}"], n + 1)
                        for kb in range(KB):
                            last = pe.matmul(bank[:, 4, 0:HD], gen_pt[:, 128 * kb:128 * (kb + 1)],
                                             gen_v[:, kb, j, 0:HD], start=kb == 0, stop=kb == KB - 1)
                        last.then_inc(s[f"gen_pv{b}"], 1)

            def attn_out(b):
                pe.wait_ge(s["ao_ready"], b + 1)
                for c in range(QC * b, QC * (b + 1)):
                    for t in range(TPC):
                        last = pe.transpose(bank[:, 4 + c % 2, 128 * t:128 * (t + 1)], x_tok[:, TPC * c + t, :],
                                            ident[:])
                    last.then_inc(s["ao_t_ready"], 1)
                for c in range(QC * b, QC * (b + 1)):
                    pe.wait_ge(s["ao_lo_ready"], c + 1)
                    split_matmul(bank[:, 6 + c % 2, :], sq_hi[:, WO, :], sq_lo[:, WO, :], act_hi[:, c % 2, :],
                                 act_lo[:, c % 2, :], True, True).then_inc(s["attn_out"], 1)

            def attention():
                skewed([lambda c: norm_in(LN_ATTN, c, X_FFN1A), lambda c: norm_out(LN_ATTN, c)])
                for b in range(NB):
                    for c in range(QC * b, QC * (b + 1)):
                        attn_chunk(c)
                        attn_stacks(c)
                    attn_bound(b)
                    fast = pe.value_load(small_scores[0:1, b:b + 1], min_val=0, max_val=1)
                    with pe.If(fast):
                        attn_fast(b)
                    with pe.Else():
                        attn_general(b)
                    attn_out(b)

            pe.wait_ge(s["ident_loaded"], 16)
            skewed([take_in, idle, lambda c: norm_out(LN_FFN0A, c)])
            skewed([lambda c: router_logits(0, LN_FFN0A, c), idle, lambda c: router_scores(0, c)])
            experts(0)
            skewed([lambda c: norm_in(LN_SSM, c, X_FFN0A), lambda c: norm_out(LN_SSM, c), idle, ssm_proj,
                    lambda c: norm_in(LN_INNER, c, None), idle, lambda c: norm_out(LN_INNER, c)])
            routed_norm(LN_FFN0B, 1, X_SSM)
            experts(1)
            routed_norm(LN_FFN1A, 2, X_FFN0B)
            lora(2)
            attention()
            routed_norm(LN_FFN1B, 3, X_ATTN)
            lora(3)
            for c in range(NC):
                pe.wait_ge(s["x_ready"], nth(X_FFN1B, c))
                if c >= 2:
                    pe.wait_ge(s["out_copied"], c - 1)
                for t in range(TPC):
                    at = slice(c * CH + 128 * t, c * CH + 128 * (t + 1))
                    last = pe.transpose(bank[:, T1[c % 2], 128 * t:128 * (t + 1)], x[:, at], ident[:])
                last.then_inc(s["fin_ready"], 1)


def position_tables():
    t = np.arange(L, dtype=np.float64)
    side = np.array([-1.0, 1.0])
    grow = np.exp(-DECAY * side[:, None] * (t - L // 2))
    p, q = np.arange(128)[:, None], np.arange(CH)[None, :]
    row = np.arange(128)
    col_head, col_slot, col_d = row // 32, row % 32 // HD, row % HD
    sel = np.zeros((128, G4, 4, 128))
    for g in range(G4):
        same = row[:, None] == (HG * g + col_head[None, :]) * HD + col_d[None, :]
        for part, slots in enumerate(((0, 1), (2, 3), (0, 2), (1, 3))):
            sel[:, g, part, :] = same & np.isin(col_slot, slots)[None, :]
    tables = {
        "q_decay": np.broadcast_to(SCALE * grow[::-1][None], (128, 2, L)),
        "k_decay": grow.reshape(2, KB, 128).transpose(2, 0, 1),
        "fix": np.exp(-2 * DECAY * np.maximum(CH - 128 + p - q, 0)),
        "decay": np.exp(-DECAY * np.abs(np.arange(128)[:, None] - (np.arange(2 * L - 128) - (L - 128))[None, :])),
        "same_head": row[:, None] // HD == row[None, :] // HD,
        "sel_h": sel,
        "head_rows": row[:, None] // 32 == np.arange(HG)[None, :],
    }
    return {k: v.astype(np.float32) for k, v in tables.items()}


def kernel(**inputs):
    import concourse.bacc as bacc
    from concourse.bass_utils import run_bass_kernel_spmd

    a = {k: np.asarray(v) for k, v in inputs.items()}
    p = "L0_ffn_"
    gate_up = a[p + "gate_up_proj"].reshape(E0, D, D, 2)
    bias = a[p + "gate_up_bias"].reshape(E0, D, 2)
    k32, m128 = np.arange(2 * E0), np.arange(128)
    host = {
        "x": a["L0_attn_x"].reshape(T, D),
        "gate_up": gate_up.transpose(1, 0, 3, 2),
        "down": a[p + "down_proj"].transpose(1, 0, 2),
        "down_bias": a[p + "down_bias"],
        "router_w": a[p + "router_w"],
        "router_b": np.broadcast_to(a[p + "router_b"], (128, E0)),
        "gate_w": a["L1_ffn_gate_w"].T,
        "b_gate": bias[:, :, 0].T,
        "b_up": bias[:, :, 1].T,
        "vecs": np.stack([a["L0_attn_" + n] for n in ("A_param", "B_vec", "C_vec", "D_vec", "b_proj", "gamma",
                                                      "beta")] + [a["L1_ffn_base_b"]], axis=1),
        "squares": np.stack([a["L0_attn_W_proj"].T, a["L1_ffn_base_w"].T,
                             a["L1_ffn_lora_A"].reshape(TRUE1 * RANK, D).T,
                             a["L1_ffn_lora_B"].transpose(0, 2, 1).reshape(TRUE1 * RANK, D),
                             a["L1_attn_Wq"], a["L1_attn_Wk"], a["L1_attn_Wv"], a["L1_attn_Wo"]], axis=1),
        "w_down": a["L1_attn_W_down_kv"],
        "w_up": np.stack([a["L1_attn_W_up_k"], a["L1_attn_W_up_v"]], axis=1),
        **position_tables(),
        "ident": np.eye(128, dtype=np.float32),
        "sel0": np.broadcast_to((k32[:, None] % E0 == np.arange(E0))[:, :, None], (2 * E0, E0, 128))
                  .astype(np.float32),
        "sel1": (np.arange(2 * TRUE1)[:, None] % TRUE1 == m128 // RANK).astype(np.float32),
    }
    nc = bacc.Bacc("TRN2", target_bir_lowering=False, num_devices=1)
    arrays, io = {}, {}
    for name, v in host.items():
        v = np.ascontiguousarray(v)
        arrays[f"in_{name}"] = v
        io[name] = nc.dram_tensor(f"in_{name}", v.shape, mybir.dt.from_np(v.dtype), kind="ExternalInput").ap()
    io["out"] = nc.dram_tensor("out_0", (T, D), F32, kind="ExternalOutput").ap()
    build(nc, io)
    result = run_bass_kernel_spmd(nc, [arrays], core_ids=[0])
    return result.results[0]["out_0"].reshape(NB, L, D)
```

```python
import numpy as np
import concourse.bass as bass
from concourse import mybir
from contextlib import ExitStack

F32 = mybir.dt.float32
F32R = mybir.dt.float32r
ALU = mybir.AluOpType
ACT = mybir.ActivationFunctionType
AX = mybir.AxisListType

D = 128
NB, L = 2, 1024
T = NB * L
CH = 512
NC = T // CH
TPC = CH // 128
EPS = 1e-5
E0, TOP0 = 16, 4
E1, TOP1, TRUE1, RANK = 10, 2, 8, 16
LIMIT, ALPHA = 7.0, 1.702
GLU_AT_LIMIT = LIMIT / (1.0 + float(np.exp(-ALPHA * LIMIT)))
SENTINEL, TAKEN = 3.0e38, -3.0e38

LN_FFN0A, LN_SSM, LN_INNER, LN_FFN0B, LN_FFN1A, LN_ATTN, LN_FFN1B = range(7)
X_IN, X_FFN0A, X_SSM, X_FFN0B, X_FFN1A, X_ATTN, X_FFN1B = range(7)

H, HD = 16, 8
LAT = 32
G4, HG = 4, 4
KB = L // 128
QC = L // CH
SCALE = float(np.float32(1.0) / (np.sqrt(np.float32(D)) + np.float32(1e-8)))
CLAMP = 1.0e4
DECAY = 0.01 * 0.01
VW = HD + 1
NP = 4
SAFE_BOUND = 40.0
WQ, WK, WV, WO = 4, 5, 6, 7
PICK_STEPS = 5
ROUTERS = {"ffn0a": 0, "ffn0b": 1, "ffn1a": 2, "ffn1b": 3}


def nth(group, c):
    return group * NC + c + 1


def nth_hi(n, c):
    return nth(n - (n > LN_INNER), c)


def build(nc, io):
    ctx = ExitStack()
    with ctx:
        def sb(name, shape, dt=F32):
            return ctx.enter_context(nc.sbuf_tensor(name, shape, dt))

        def sem(name):
            return ctx.enter_context(nc.semaphore(name))

        x = sb("x", [D, T])
        x_tok = sb("x_tok", [128, T // 128, D])
        xn_hi = sb("xn_hi", [D, T], F32R)
        xn_lo = sb("xn_lo", [D, T], F32R)
        ident = sb("ident", [128, 128])
        raw_w = sb("raw_w", [128, E0 * 3 * D])
        w0_hi = sb("w0_hi", [128, E0, 3, D], F32R)
        w0_lo = sb("w0_lo", [128, E0, 3, D], F32R)
        b_gate = sb("b_gate", [128, E0])
        b_up = sb("b_up", [128, E0])
        b_up1 = sb("b_up1", [128, E0])
        raw_s = sb("raw_s", [128, 8, D])
        sq_hi = sb("sq_hi", [128, 8, D], F32R)
        sq_lo = sb("sq_lo", [128, 8, D], F32R)
        raw_r = sb("raw_r", [128, E0 + 16])
        r_hi = sb("r_hi", [128, E0 + 16], F32R)
        r_lo = sb("r_lo", [128, E0 + 16], F32R)
        raw_db = sb("raw_db", [2 * E0, D])
        db_hi = sb("db_hi", [2 * E0, D], F32R)
        db_lo = sb("db_lo", [2 * E0, D], F32R)
        router_b = sb("router_b", [128, E0])
        sel0_all = sb("sel0", [128, E0, 128], F32R)
        sel0 = sel0_all[0:2 * E0]
        sel1 = sb("sel1", [2 * TRUE1, 128], F32R)
        vecs = sb("vecs", [128, 8])
        ab = sb("ab", [128, 8])
        pw = sb("pw", [128, L])
        zero1 = sb("zero1", [128, 1])
        half_pow = sb("half_pow", [128, TPC])

        stats = sb("stats", [128, 2, TPC, 6])
        mean_var = sb("mean_var", [128, 2, TPC, 2])
        var_eps = sb("var_eps", [128, 2, TPC])
        rstd = sb("rstd", [128, 2, TPC])
        minus_mean = sb("minus_mean", [128, 2, TPC])
        offset = sb("offset", [128, 2, TPC])
        xt = sb("xt", [128, 2, TPC, D])

        logit = sb("logit", [128, 2, TPC, 20])
        logit1 = sb("logit1", [128, 2, TPC, 16])
        top8 = sb("top8", [128, 2, TPC, 8])
        taken = sb("taken", [128, 2, TPC, 20])
        shifted = sb("shifted", [128, 2, TPC, 16])
        expd = sb("expd", [128, 2, TPC, 16])
        picked = sb("picked", [128, 2, TPC, 16])
        denom = sb("denom", [128, 2, TPC])
        denom1 = sb("denom1", [128, 2, TPC])
        recip = sb("recip", [128, 2, TPC])
        share = sb("share", [128, 2, TPC, 16])
        share_hl = sb("share_hl", [128, 2, TPC, 2 * E0])
        score_all = sb("score_t", [128, T], F32R)
        score_t = score_all[0:2 * E0]

        NACT = 3
        glu = sb("glu", [128, 2, CH])
        up = sb("up", [128, 2, CH])
        glu_s = sb("glu_s", [128, 2, CH])
        act = sb("act", [128, NACT, CH])
        act_hi = sb("act_hi", [128, NACT, CH], F32R)
        act_lo = sb("act_lo", [128, NACT, CH], F32R)

        xn = raw_w[:, 0:T]
        ssm_in = raw_w[:, T:T + 2 * CH]
        ssm_sum = raw_w[:, 2 * T - 2 * CH:2 * T]
        ssm_y = glu
        ssm_z = up
        gelu = glu_s
        resid = sb("resid", [128, 2, CH])
        tmp = sb("tmp", [128, 2, CH])

        w_down = sb("w_down", [D, LAT])
        w_up = sb("w_up", [LAT, 2, D])
        sel_h = sb("sel_h", [128, G4, 4, 128], F32R)
        head_rows = sb("head_rows", [128, HG])
        same_head = sb("same_head", [128, 128])
        q_decay = sb("q_decay", [128, 2, L])
        k_decay = sb("k_decay", [128, 2, KB])
        fix = sb("fix", [128, CH])
        minus_one = sb("minus_one", [1, 128])
        half_one = sb("half_one", [1, 1])
        q_stack = (w0_hi[:].rearrange("p e w d -> p (e w d)")[:, 0:G4 * L].rearrange("p (g t) -> p g t", g=G4),
                   w0_lo[:].rearrange("p e w d -> p (e w d)")[:, 0:G4 * L].rearrange("p (g t) -> p g t", g=G4))
        k_parts = [w[:].rearrange("p e w d -> p (e w d)")[:, G4 * L:(G4 + 2) * L].rearrange("p (g t) -> p g t", g=2)
                   for w in (w0_hi, w0_lo)]
        k_stack = [k_parts[g // 2][:, g % 2, :] for g in range(G4)]
        values = raw_w[:, 0:KB * H * VW].rearrange("p (k h v) -> p k h v", k=KB, h=H)
        def head_keys(b, g, j):
            flat = lambda t: t.rearrange("p e t -> p (e t)")
            return (xn_hi[:, L * b:L * (b + 1)], xn_lo[:, L * b:L * (b + 1)], score_all[:, 0:L],
                    score_all[:, L:2 * L], flat(act_hi[:, 0:2, :]), flat(act_lo[:, 0:2, :]),
                    flat(sel0_all[:])[:, 0:L], flat(sel0_all[:])[:, L:2 * L])[g % 2 * HG + j]

        probs = raw_w[:, E0 * 3 * D - NP * 2 * CH:].rearrange("p (n t) -> p n t", n=NP)
        qk_f = glu_s
        kv_f, lat_f, q_sq, k_sq = glu[:, 0, :], glu[0:LAT, 1, :], up[:, 0, :], up[:, 1, :]
        gen_small = sb("gen_small", [128, 3])
        head_max = sb("head_max", [128, NB, 2, QC])
        tops = sb("tops", [128, NB, 3])
        bound = sb("bound", [1, NB, 2])
        small_scores = sb("small_scores", [1, NB], mybir.dt.int32)
        minus_c = sb("minus_c", [128, NB])
        out_t = resid
        out_recip = sb("out_recip", [128, TPC, HG])

        flat = raw_w[:, E0 * 3 * D - NP * 2 * CH:]
        gen_s, gen_pt, gen_decays = flat[:, 0:L], flat[:, L:2 * L], flat[:, 2 * L:4 * L - 128]
        gen_k = act_hi[:, 0:2, :].rearrange("p a t -> p (a t)")
        gen_q = act_hi[:, 2, 0:128]
        gen_v = tmp[:].rearrange("p a t -> p (a t)")[:, 0:KB * HG * VW].rearrange("p (k h v) -> p k h v", k=KB, h=HG)
        gen_decay = up[:].rearrange("p a t -> p (a t)")
        gen_heads = tmp[:, 1, CH - HG * HD:]
        gen_unscale, gen_recip, gen_spare = gen_small[:, 0:1], gen_small[:, 1:2], gen_small[:, 2:3]

        bank = ctx.enter_context(nc.psum_tensor("bank", [128, 8, CH], F32))
        T1, T2, LG, ST = (0, 1), (2, 3), 4, 5
        Z, EW, OUT1 = 6, 3, 7
        G, U, S, O = (0, 1), (2, 3), (4, 5), (6, 7)

        names = """x_loaded0 x_loaded1 x_loaded2 x_loaded3 half_scaled w_loaded0 w_loaded1 w_loaded2 w_loaded3 small_loaded out_stored
            ident_loaded consts_ready x_ready tok_in t1_ready stats_step stats_ready eps_step
            rstd_ready offset_ready normalized inner_scaled t2_ready xn_hi_ready xn_ready w0_hi_ready w0_lo_ready
            small_hi_ready small_ready prep_step ab_ready
            logits_ready logit_step top_step taken_step shift_ready exp_ready pick_step
             share_ready score_psum_ready score_ready
            g_ready u_ready s_ready glu_ready up_ready glu_s_ready act_ready hi_ready lo_ready
            down_done
            ssm_step y_ready gelu_ready gelu_hi_ready gelu_lo_ready proj_ready resid_ready
            z_ready z_copied ew_ready zs_ready zs_hi_ready zs_lo_ready out1_ready fin_ready out_copied
            cast_loaded prep_loaded
            qkv_ready q_decayed q_sq_ready kv_copied lat_ready lat_copied kv_rec_ready k_sq_ready
            k_lo_ready v_copied q_hi_ready q_lo_ready norms_ready maxes_ready tops_ready
            tops_row bound_step bound_ready sqrt_ready minus_c_ready flag_ready neg_ready
            stack_ready stack_copied stack_copied_v ao_ready ao_t_ready ao_hi_ready ao_lo_ready attn_out""".split()
        names += [f"{n}{b}" for b in range(NB) for n in
                  ("keys_masked", "scored", "fixed", "exped", "pv_done", "ot_copied", "ot_ready", "recip_ready", "normed",
                   "gen_staged", "gen_scored", "gen_clipped", "gen_decayed", "gen_max", "gen_neg", "gen_probs",
                   "gen_t", "gen_tc", "gen_pv", "gen_recip", "gen_out", "gen_table")]
        s = {n: sem(n) for n in names}

        block = ctx.enter_context(nc.Block())

        def chunk(c):
            return slice(c * CH, (c + 1) * CH)

        def t2_bank(n, c):
            return T2[c % 2] if n < LN_FFN1A else T2[0]

        def skewed(stages, first=(), last=(), before={}):
            order = list(first) + [i for i in sorted(stages, reverse=True) if i not in first and i not in last]
            order += list(last)
            for step in range(NC + int(max(stages))):
                if step in before:
                    before[step]()
                for i in order:
                    if 0 <= step - int(i) < NC:
                        stages[i](step - int(i))

        UNITS = G4 * QC * KB * 2

        def unit(u):
            i = u // 2 % KB
            return u // (4 * KB), u // (2 * KB) % QC, i // 2 + i % 2 * (KB // 2), u % 2

        def fixes(u):
            g, qc, kb, hp = unit(u)
            return 2 * (CH // 128) * (u // (2 * KB)) + 2 * (kb % (CH // 128)) + hp + 1

        def stack_place(i, c):
            g, kind = i // 3, (i + 2) % 3
            at = slice(CH * (c % QC), CH * (c % QC + 1))
            return k_stack[g][:, at] if kind == 2 else q_stack[kind][:, g, at]

        SMALL = [(raw_r[:, 0:E0], "router_w"), (raw_r[:, E0:E0 + E1], "gate_w"),
                 (router_b[:], "router_b"), (raw_db[0:E0, :], "down_bias"), (raw_db[E0:2 * E0, :], "down_bias"),
                 (b_gate[:], "b_gate"), (b_up[:], "b_up"), (vecs[:], "vecs"), (raw_s[:], "squares")]
        LATER = [(w_down[:], "w_down"), (w_up[:], "w_up"), (same_head[:], "same_head"),
                 (head_rows[:], "head_rows"), (q_decay[:], "q_decay"), (k_decay[:], "k_decay"), (fix[:], "fix")]

        @block.sync
        def _(sp):
            x_rows = io["x"].rearrange("(n p) d -> p n d", p=128)
            sp.dma_start(ident[:], io["ident"]).then_inc(s["ident_loaded"], 16)
            for c in range(NC):
                sp.dma_start(x_tok[:, TPC * c:TPC * (c + 1), :], x_rows[:, TPC * c:TPC * (c + 1), :])\
                  .then_inc(s[f"x_loaded{c}"], 16)
            per = E0 // 4
            raw = raw_w[:].rearrange("p (e w d) -> p e w d", e=E0, w=3)
            for g in range(4):
                es = slice(per * g, per * (g + 1))
                sp.dma_start(raw[:, es, 0:2, :], io["gate_up"][:, es]).then_inc(s[f"w_loaded{g}"], 16)
                sp.dma_start(raw[:, es, 2, :], io["down"][:, es]).then_inc(s[f"w_loaded{g}"], 16)
            for dst, name in LATER:
                sp.dma_start(dst, io[name]).then_inc(s["prep_loaded"], 16)
            out_rows = io["out"].rearrange("(n p) d -> p n d", p=128)
            for c in range(NC):
                sp.wait_ge(s["out_copied"], c + 1)
                sp.dma_start(out_rows[:, TPC * c:TPC * (c + 1), :], x_tok[:, TPC * c:TPC * (c + 1), :])\
                  .then_inc(s["out_stored"], 16)
            sp.wait_ge(s["out_stored"], 16 * NC)

        @block.gpsimd
        def _(pool):
            for dst, name in SMALL:
                pool.dma_start(dst, io[name]).then_inc(s["small_loaded"], 16)
            for dst, name in ((sel0, "sel0"), (sel1, "sel1"), (sel_h, "sel_h")):
                pool.dma_start(dst[:], io[name]).then_inc(s["cast_loaded"], 16)
            pool.memset(half_pow[:], -0.5)
            pool.memset(minus_one[:], -1.0)
            pool.memset(half_one[:], 0.5)
            pool.memset(zero1[:], 0.0)
            pool.memset(raw_r[:, E0 + E1:], 0.0)
            pool.memset(logit[:, :, :, E0:20], SENTINEL)
            pool.memset(logit1[:, :, :, E1:16], SENTINEL)
            pool.memset(share_hl[:], 0.0)
            pool.memset(pw[:, 0:1], 1.0).then_inc(s["consts_ready"], 1)

            def norm(n, c):
                k = n * NC + c
                pool.wait_ge(s["stats_ready"], k + 1)
                if k >= 2:
                    pool.wait_ge(s["normalized"], k - 1)
                pool.tensor_scalar(var_eps[:, k % 2, :], mean_var[:, k % 2, :, 1], EPS, None, ALU.add)
                pool.tensor_scalar(minus_mean[:, k % 2, :], mean_var[:, k % 2, :, 0], -1.0, None, ALU.mult)\
                    .then_inc(s["eps_step"], 1)
                pool.wait_ge(s["eps_step"], k + 1)
                pool.tensor_tensor(rstd[:, k % 2, :], var_eps[:, k % 2, :], half_pow[:], ALU.pow)\
                    .then_inc(s["rstd_ready"], 1)
                pool.wait_ge(s["rstd_ready"], k + 1)
                pool.tensor_tensor(offset[:, k % 2, :], minus_mean[:, k % 2, :], rstd[:, k % 2, :], ALU.mult)\
                    .then_inc(s["offset_ready"], 1)

            def ssm_lo(c):
                pool.wait_ge(s["gelu_hi_ready"], c + 1)
                if c >= 2:
                    pool.wait_ge(s["proj_ready"], c - 1)
                pool.tensor_tensor(act_lo[:, c % 2, :], gelu[:, c % 2, :], act_hi[:, c % 2, :].bitcast(F32),
                                   ALU.subtract).then_inc(s["gelu_lo_ready"], 1)

            def experts(f):
                for j in range(f * NC * E0, (f + 1) * NC * E0):
                    pool.wait_ge(s["hi_ready"], j + 1)
                    if j >= NACT:
                        pool.wait_ge(s["down_done"], j - NACT + 1)
                    pool.tensor_tensor(act_lo[:, j % NACT, :], act[:, j % NACT, :],
                                       act_hi[:, j % NACT, :].bitcast(F32), ALU.subtract)\
                        .then_inc(s["lo_ready"], 1)

            skewed({0: lambda c: norm(LN_FFN0A, c)})
            experts(0)
            skewed({0: lambda c: norm(LN_SSM, c), 3: ssm_lo, 4: lambda c: norm(LN_INNER, c),
                    8: lambda c: norm(LN_FFN0B, c)})
            experts(1)
            skewed({0: lambda c: norm(LN_FFN1A, c), 8: lambda c: norm(LN_ATTN, c)})
            for b in range(NB):
                for c in range(QC * b, QC * (b + 1)):
                    if c == QC * (b + 1) - 1:
                        pool.wait_ge(s["bound_ready"], b + 1)
                        pool.tensor_tensor(bound[:, b, 1:2], bound[:, b, 0:1], half_one[:], ALU.pow)\
                            .then_inc(s["sqrt_ready"], 1)
                    pool.wait_ge(s["stack_copied"], 3 * G4 // 2 * c + 1)
                    at = slice(CH * (c % QC), CH * (c % QC + 1))
                    for j in range(HG):
                        pool.tensor_scalar(head_keys(b, 0, j)[:, at], k_stack[0][:, at].bitcast(F32),
                                           head_rows[:, j:j + 1], None, ALU.mult)\
                            .then_inc(s[f"keys_masked{b}"], 1)
                pool.wait_ge(s["minus_c_ready"], b + 1)
                pool.wait_ge(s["flag_ready"], b + 1)
                pool.wait_ge(s["stack_copied"], 3 * G4 // 2 * QC * (b + 1))
                pool.wait_ge(s["stack_copied_v"], 3 * G4 // 2 * QC * (b + 1))
                fast = pool.value_load(small_scores[0:1, b:b + 1], min_val=0, max_val=1)
                with pool.If(fast):
                    for g in range(1, G4):
                        if g >= 2:
                            pool.wait_ge(s[f"scored{b}"], UNITS // G4 * (g - 1))
                        for j in range(HG):
                            pool.tensor_scalar(head_keys(b, g, j), k_stack[g].bitcast(F32), head_rows[:, j:j + 1],
                                               None, ALU.mult).then_inc(s[f"keys_masked{b}"], 1)
            skewed({0: lambda c: norm(LN_FFN1B, c)})

        @block.scalar
        def _(eng):
            def split_small():
                eng.wait_ge(s["small_loaded"], 16 * len(SMALL))
                eng.wait_ge(s["consts_ready"], 1)
                eng.activation(raw_s[:, 1, :], raw_s[:, 1, :], ACT.Copy, scale=0.5).then_inc(s["half_scaled"], 1)
                eng.wait_ge(s["half_scaled"], 1)
                for dst, src in ((r_hi, raw_r), (db_hi, raw_db), (sq_hi, raw_s)):
                    eng.activation(dst[:], src[:], ACT.Copy).then_inc(s["small_hi_ready"], 1)
                eng.activation(ab[:, 0:1], vecs[:, 0:1], ACT.Exp, scale=-1.0).then_inc(s["small_hi_ready"], 1)

            def split_experts(g):
                raw = raw_w[:].rearrange("p (e w d) -> p e w d", e=E0, w=3)
                es = slice(E0 // 4 * g, E0 // 4 * (g + 1))
                eng.wait_ge(s[f"w_loaded{g}"], 32)
                eng.activation(w0_hi[:, es], raw[:, es], ACT.Copy).then_inc(s["w0_hi_ready"], 1)

            def norm_rows(n, c):
                k = n * NC + c
                b = k % 2
                tiles = (x_tok[:, TPC * c:TPC * (c + 1), :] if n == LN_FFN0A else
                         bank[:, T1[b], :].rearrange("p (t d) -> p t d", d=D))
                eng.wait_ge(s["offset_ready"], k + 1)
                if k >= 2:
                    eng.wait_ge(s["t2_ready"], k - 1)
                for t in range(TPC):
                    last = eng.activation(xt[:, b, t, :], tiles[:, t, :], ACT.Identity,
                                          bias=offset[:, b, t:t + 1], scale=rstd[:, b, t:t + 1])
                last.then_inc(s["normalized"], 1)

            def norm_hi(n, c):
                k = n * NC + c
                eng.wait_ge(s["t2_ready"], k + 1)
                dst = xn[:, chunk(c)] if n == LN_SSM else xn_hi[:, chunk(c)]
                eng.activation(dst, bank[:, t2_bank(n, c), :], ACT.Copy).then_inc(s["xn_hi_ready"], 1)

            def inner_scale(c):
                eng.wait_ge(s["t2_ready"], nth(LN_INNER, c))
                if c >= 2:
                    eng.wait_ge(s["x_ready"], nth(X_SSM, c - 2))
                eng.activation(tmp[:, c % 2, :], bank[:, t2_bank(LN_INNER, c), :], ACT.Identity,
                               bias=vecs[:, 6:7], scale=vecs[:, 5:6]).then_inc(s["inner_scaled"], 1)

            def router_exp(r, c):
                kr = r * NC + c
                eng.wait_ge(s["shift_ready"], kr + 1)
                ne = E0 if r < 2 else E1
                eng.activation(expd[:, kr % 2, :, 0:ne], shifted[:, kr % 2, :, 0:ne], ACT.Exp)\
                   .then_inc(s["exp_ready"], 1)

            def router_out(r, c):
                kr = r * NC + c
                nr = 2 * E0 if r < 2 else 2 * TRUE1
                eng.wait_ge(s["score_psum_ready"], kr + 1)
                eng.activation(score_t[0:nr, chunk(c)], bank[0:nr, ST, :], ACT.Copy)\
                   .then_inc(s["score_ready"], 1)

            def experts(f):
                first, last = f * NC * E0, (f + 1) * NC * E0
                for j in range(first, last + 1):
                    if j < last:
                        e = j % E0
                        eng.wait_ge(s["g_ready"], j + 1)
                        if j >= 2:
                            eng.wait_ge(s["glu_s_ready"], j - 1)
                        eng.activation(glu[:, j % 2, :], bank[:, G[j % 2], :], ACT.Gelu_apprx_sigmoid,
                                       bias=b_gate[:, e:e + 1]).then_inc(s["glu_ready"], 1)
                    if j > first:
                        i = j - 1
                        eng.wait_ge(s["act_ready"], i + 1)
                        if i >= NACT:
                            eng.wait_ge(s["down_done"], i - NACT + 1)
                        eng.activation(act_hi[:, i % NACT, :], act[:, i % NACT, :], ACT.Copy)\
                           .then_inc(s["hi_ready"], 1)

            def ssm_gelu(c):
                eng.wait_ge(s["y_ready"], c + 1)
                if c >= 2:
                    eng.wait_ge(s["gelu_lo_ready"], c - 1)
                eng.activation(gelu[:, c % 2, :], ssm_z[:, c % 2, :], ACT.Gelu).then_inc(s["gelu_ready"], 1)
                eng.wait_ge(s["gelu_ready"], c + 1)
                if c >= 2:
                    eng.wait_ge(s["proj_ready"], c - 1)
                eng.activation(act_hi[:, c % 2, :], gelu[:, c % 2, :], ACT.Copy).then_inc(s["gelu_hi_ready"], 1)

            def lora_z(r, c):
                k = (r - 2) * NC + c
                eng.wait_ge(s["z_ready"], k + 1)
                if k >= 2:
                    eng.wait_ge(s["zs_ready"], k - 1)
                eng.activation(glu[:, k % 2, :], bank[:, Z, :], ACT.Copy).then_inc(s["z_copied"], 1)

            def lora_hi(r, c):
                k = (r - 2) * NC + c
                eng.wait_ge(s["zs_ready"], k + 1)
                if k >= 2:
                    eng.wait_ge(s["out1_ready"], k - 1)
                eng.activation(act_hi[:, k % 2, :], act[:, k % 2, :], ACT.Copy).then_inc(s["zs_hi_ready"], 1)

            def attn_first(c):
                o = 4 * (c % 2)
                eng.wait_ge(s["qkv_ready"], c + 1)
                eng.activation(kv_f, bank[:, o + 1, :], ACT.Copy).then_inc(s["kv_copied"], 1)
                if c >= 1:
                    eng.wait_ge(s["norms_ready"], c)
                eng.wait_ge(s["q_decayed"], 2 * c + 2)
                eng.activation(q_sq, bank[:, o, :], ACT.Square, scale=SCALE).then_inc(s["q_sq_ready"], 1)

            def attn_second(c):
                o = 4 * (c % 2)
                eng.wait_ge(s["lat_ready"], c + 1)
                eng.activation(lat_f, bank[0:LAT, o + 2, :], ACT.Copy).then_inc(s["lat_copied"], 1)
                if c >= 1:
                    eng.wait_ge(s["stack_ready"], 3 * G4 * c)
                for i in range(2):
                    eng.wait_ge(s["q_decayed"], 2 * c + i + 1)
                    eng.activation(act_hi[:, i, :], qk_f[:, i, :], ACT.Copy).then_inc(s["q_hi_ready"], 1)
                eng.wait_ge(s["kv_rec_ready"], c + 1)
                eng.activation(act_hi[:, 2, :], bank[:, o + 3, :], ACT.Copy)
                eng.activation(k_sq, bank[:, o + 3, :], ACT.Square).then_inc(s["k_sq_ready"], 1)
                eng.activation(values[:, TPC * (c % QC):TPC * (c % QC + 1), :, 0:HD],
                               bank[:, o + 1, :].rearrange("p (t h d) -> p t h d", t=TPC, h=H), ACT.Copy)\
                   .then_inc(s["v_copied"], 1)

            def attn_stacks(c):
                for i in range(0, 3 * G4, 2):
                    n = c * 3 * G4 + i
                    eng.wait_ge(s["stack_ready"], n + 1)
                    eng.activation(stack_place(i, c), bank[:, i % 4, :], ACT.Copy).then_inc(s["stack_copied"], 1)

            def attn_fast(b):
                for u in range(UNITS):
                    g, qc, kb, hp = unit(u)
                    if kb // (CH // 128) == qc:
                        eng.wait_ge(s[f"fixed{b}"], fixes(u))
                    else:
                        eng.wait_ge(s[f"scored{b}"], u + 1)
                    if u >= NP:
                        eng.wait_ge(s[f"pv_done{b}"], (u - NP) // 2 + 1)
                    side = 1 if kb // (CH // 128) > qc else 0
                    pair = bank[:, 2 * (u % 3):2 * (u % 3) + 2, :].rearrange("p a q -> p (a q)")
                    eng.activation(probs[:, u % NP, :], pair, ACT.Exp, bias=minus_c[:, b:b + 1],
                                   scale=k_decay[:, side, kb:kb + 1]).then_inc(s[f"exped{b}"], 1)

            def attn_out(b):
                for c in range(QC * b, QC * (b + 1)):
                    eng.wait_ge(s["ao_t_ready"], c + 1)
                    eng.activation(act_hi[:, c % 2, :], bank[:, 4 + c % 2, :], ACT.Copy).then_inc(s["ao_hi_ready"], 1)

            def attention():
                for b in range(NB):
                    attn_first(QC * b)
                    attn_second(QC * b)
                    for c in range(QC * b, QC * (b + 1)):
                        if c + 1 < QC * (b + 1):
                            attn_first(c + 1)
                        attn_stacks(c)
                        if c + 1 < QC * (b + 1):
                            attn_second(c + 1)
                    eng.wait_ge(s["neg_ready"], b + 1)
                    eng.activation(minus_c[:, b:b + 1], bank[:, 7, 0:1], ACT.Copy).then_inc(s["minus_c_ready"], 1)
                    eng.wait_ge(s["minus_c_ready"], b + 1)
                    eng.wait_ge(s["flag_ready"], b + 1)
                    fast = eng.value_load(small_scores[0:1, b:b + 1], min_val=0, max_val=1)
                    with eng.If(fast):
                        attn_fast(b)
                    with eng.Else():
                        attn_general(b)
                    attn_out(b)

            def attn_general(b):
                eng.dma_start(gen_decays, io["decay"]).then_inc(s[f"gen_table{b}"], 16)
                with eng.Fori(0, G4 * KB) as block_of_queries:
                    for j in range(HG):
                        n = block_of_queries * HG + j
                        eng.wait_ge(s[f"gen_neg{b}"], n + 1)
                        eng.activation(gen_s, gen_s, ACT.Exp, bias=tops[:, b, 1:2],
                                       accum_out=tops[:, b, 2:3]).then_inc(s[f"gen_probs{b}"], 1)
                        eng.wait_ge(s[f"gen_t{b}"], n + 1)
                        eng.activation(gen_pt, bank[:, 2:4, :].rearrange("p a q -> p (a q)"), ACT.Copy)\
                           .then_inc(s[f"gen_tc{b}"], 1)

            def routed_norm(n, r, at=0):
                return {at + 1: lambda c: norm_rows(n, c), at + 2: lambda c: norm_hi(n, c),
                        at + 3: lambda c: router_exp(r, c), at + 5: lambda c: router_out(r, c)}

            def lora_stages(n, r):
                stages = routed_norm(n, r)

                def scores_and_z(c):
                    router_out(r, c)
                    lora_z(r, c)
                return {**stages, 5: scores_and_z, 6: lambda c: lora_hi(r, c)}

            def out_copy(c):
                eng.wait_ge(s["fin_ready"], c + 1)
                eng.activation(x_tok[:, TPC * c:TPC * (c + 1), :],
                               bank[:, T1[c % 2], :].rearrange("p (t d) -> p t d", d=D), ACT.Copy)\
                   .then_inc(s["out_copied"], 1)

            skewed(routed_norm(LN_FFN0A, 0), last=(2, 1, 3),
                   before={2: split_small, 5: lambda: split_experts(0), 6: lambda: split_experts(1)})
            for g in range(2, 4):
                split_experts(g)
            experts(0)
            skewed({1: lambda c: norm_rows(LN_SSM, c), 2: lambda c: norm_hi(LN_SSM, c), 3: ssm_gelu,
                    5: lambda c: norm_rows(LN_INNER, c), 6: inner_scale, **routed_norm(LN_FFN0B, 1, 8)},
                   last=(10, 9, 11))
            experts(1)
            skewed({**lora_stages(LN_FFN1A, 2), 9: lambda c: norm_rows(LN_ATTN, c),
                    10: lambda c: norm_hi(LN_ATTN, c)}, last=(2, 1, 3))
            attention()
            skewed({**lora_stages(LN_FFN1B, 3), 9: out_copy}, last=(2, 1, 3))

        @block.vector
        def _(eng):
            def take_in(c):
                eng.wait_ge(s["tok_in"], c + 1)
                eng.tensor_copy(x[:, chunk(c)], bank[:, O[c % 2], :]).then_inc(s["x_ready"], 1)

            def norm_stats(n, c):
                k = n * NC + c
                b = k % 2
                if n == LN_FFN0A:
                    eng.wait_ge(s[f"x_loaded{c}"], 16)
                    if c >= 2:
                        eng.wait_ge(s["normalized"], k - 1)
                    tiles = x_tok[:, TPC * c:TPC * (c + 1), :]
                else:
                    eng.wait_ge(s["t1_ready"], k + 1 - NC)
                    tiles = bank[:, T1[b], :].rearrange("p (t d) -> p t d", d=D)
                for t in range(TPC):
                    last = eng.bn_stats(stats[:, b, t, :], tiles[:, t, :])
                last.then_inc(s["stats_step"], 1)
                eng.wait_ge(s["stats_step"], k + 1)
                for t in range(TPC):
                    last = eng.bn_aggr(mean_var[:, b, t, :], stats[:, b, t, :])
                last.then_inc(s["stats_ready"], 1)

            def norm_lo(n, c):
                k = n * NC + c
                eng.wait_ge(s["xn_hi_ready"], nth_hi(n, c))
                eng.tensor_tensor(xn_lo[:, chunk(c)], bank[:, t2_bank(n, c), :],
                                  xn_hi[:, chunk(c)].bitcast(F32), ALU.subtract).then_inc(s["xn_ready"], 1)

            def router_pick(r, c):
                kr, b = r * NC + c, (r * NC + c) % 2
                moe = r < 2
                ne, sent = (E0, 20 - E0) if moe else (E1, 16 - E1)
                lg = logit if moe else logit1
                width = ne + sent
                eng.wait_ge(s["logits_ready"], kr + 1)
                src = bank[:, LG, 0:TPC * 16].rearrange("p (t e) -> p t e", e=16)[:, :, 0:ne]
                if moe:
                    eng.tensor_tensor(lg[:, b, :, 0:ne], src, router_b[:, None, :].to_broadcast([128, TPC, E0]),
                                      ALU.add).then_inc(s["logit_step"], 1)
                else:
                    eng.tensor_copy(lg[:, b, :, 0:ne], src).then_inc(s["logit_step"], 1)
                eng.wait_ge(s["logit_step"], kr + 1)
                for t in range(TPC):
                    last = eng.max(top8[:, b, t, :], lg[:, b, t, :])
                last.then_inc(s["top_step"], 1)
                eng.wait_ge(s["top_step"], kr + 1)
                for t in range(TPC):
                    last = eng.match_replace(out=taken[:, b, t, 0:width], in_to_replace=top8[:, b, t, :],
                                      in_values=lg[:, b, t, :], imm_value=TAKEN)
                last.then_inc(s["taken_step"], 1)
                eng.tensor_tensor(shifted[:, b, :, 0:ne], lg[:, b, :, 0:ne],
                                  top8[:, b, :, sent:sent + 1].to_broadcast([128, TPC, ne]), ALU.subtract)\
                    .then_inc(s["shift_ready"], 1)

            def router_share(r, c):
                kr, b = r * NC + c, (r * NC + c) % 2
                moe = r < 2
                ne = E0 if moe else TRUE1
                eng.wait_ge(s["exp_ready"], kr + 1)
                eng.wait_ge(s["taken_step"], kr + 1)
                step = PICK_STEPS * kr

                def then(ins):
                    nonlocal step
                    step += 1
                    ins.then_inc(s["pick_step"], 1)
                    eng.wait_ge(s["pick_step"], step)

                then(eng.scalar_tensor_tensor(out=picked[:, b, :, 0:ne], in0=taken[:, b, :, 0:ne], scalar=TAKEN,
                                              in1=expd[:, b, :, 0:ne], op0=ALU.is_equal, op1=ALU.mult))
                then(eng.tensor_reduce(denom[:, b, :], picked[:, b, :, 0:ne], axis=AX.X, op=ALU.add))
                then(eng.scalar_tensor_tensor(out=denom1[:, b, :], in0=denom[:, b, :], scalar=0.0,
                                              in1=denom[:, b, :], op0=ALU.is_equal, op1=ALU.add))
                then(eng.reciprocal(recip[:, b, :], denom1[:, b, :]))
                if kr >= 2:
                    eng.wait_ge(s["score_psum_ready"], kr - 1)
                for dst in (share[:, b, :, 0:ne], share_hl[:, b, :, 0:ne].bitcast(F32R)):
                    ins = eng.scalar_tensor_tensor(out=dst, in0=picked[:, b, :, 0:ne],
                                                   scalar=0.5 if moe else 1.0,
                                                   in1=recip[:, b, :, None].to_broadcast([128, TPC, ne]),
                                                   op0=ALU.mult, op1=ALU.mult)
                then(ins)
                eng.tensor_tensor(share_hl[:, b, :, ne:2 * ne].bitcast(F32R), share[:, b, :, 0:ne],
                                  share_hl[:, b, :, 0:ne], ALU.subtract).then_inc(s["share_ready"], 1)

            def split_small():
                eng.wait_ge(s["small_hi_ready"], 4)
                for dst, src, hi in ((r_lo, raw_r, r_hi), (db_lo, raw_db, db_hi), (sq_lo, raw_s, sq_hi)):
                    eng.tensor_tensor(dst[:], src[:], hi[:].bitcast(F32), ALU.subtract)
                eng.tensor_scalar(b_up1[:], b_up[:], 1.0, None, ALU.add).then_inc(s["small_ready"], 1)

            def ssm_powers():
                step = 0

                def then(ins):
                    nonlocal step
                    step += 1
                    ins.then_inc(s["prep_step"], 1)
                    eng.wait_ge(s["prep_step"], step)

                then(eng.tensor_scalar(ab[:, 1:2], ab[:, 0:1], 1.0, None, ALU.add))
                then(eng.reciprocal(ab[:, 2:3], ab[:, 1:2]))
                then(eng.tensor_tensor(ab[:, 3:4], vecs[:, 2:3], vecs[:, 1:2], ALU.mult))
                then(eng.tensor_scalar(ab[:, 4:5], vecs[:, 7:8], 0.5, None, ALU.mult))
                eng.tensor_tensor_scan(pw[:, 1:L], ab[:, 2:3].to_broadcast([128, L - 1]),
                                       zero1[:, 0:1].to_broadcast([128, L - 1]), 1.0, ALU.mult, ALU.add)\
                    .then_inc(s["ab_ready"], 1)

            def split_experts(g):
                raw = raw_w[:].rearrange("p (e w d) -> p e w d", e=E0, w=3)
                es = slice(E0 // 4 * g, E0 // 4 * (g + 1))
                eng.wait_ge(s["w0_hi_ready"], g + 1)
                eng.tensor_tensor(w0_lo[:, es], raw[:, es], w0_hi[:, es].bitcast(F32), ALU.subtract)\
                    .then_inc(s["w0_lo_ready"], 1)

            def experts(f):
                for j in range(f * NC * E0, (f + 1) * NC * E0):
                    e, c = j % E0, j // E0 % NC
                    eng.wait_ge(s["u_ready"], j + 1)
                    eng.tensor_scalar(up[:, j % 2, :], bank[:, U[j % 2], :], b_up1[:, e:e + 1], 1.0 - LIMIT,
                                      ALU.add, ALU.max).then_inc(s["up_ready"], 1)
                    eng.wait_ge(s["glu_ready"], j + 1)
                    eng.wait_ge(s["s_ready"], j + 1)
                    eng.scalar_tensor_tensor(out=glu_s[:, j % 2, :], in0=glu[:, j % 2, :], scalar=GLU_AT_LIMIT,
                                             in1=bank[:, S[j % 2], :], op0=ALU.min, op1=ALU.mult)\
                        .then_inc(s["glu_s_ready"], 1)
                    eng.wait_ge(s["glu_s_ready"], j + 1)
                    if j >= NACT:
                        eng.wait_ge(s["lo_ready"], j - NACT + 1)
                    eng.scalar_tensor_tensor(out=act[:, j % NACT, :], in0=up[:, j % 2, :], scalar=1.0 + LIMIT,
                                             in1=glu_s[:, j % 2, :], op0=ALU.min, op1=ALU.mult)\
                        .then_inc(s["act_ready"], 1)
                    if e == 2 and c > 0:
                        add_out(f, c - 1)
                add_out(f, NC - 1)

            def add_out(f, c):
                eng.wait_ge(s["down_done"], E0 * nth(f, c))
                eng.tensor_tensor(x[:, chunk(c)], bank[:, O[c % 2], :], x[:, chunk(c)], ALU.add)\
                    .then_inc(s["x_ready"], 1)

            def ssm_scan(c):
                n = LN_SSM
                at = c * CH % L
                b = c % 2
                step = 2 * c
                eng.wait_ge(s["xn_hi_ready"], nth_hi(LN_SSM, c))
                eng.wait_ge(s["ab_ready"], 1)
                eng.tensor_tensor(ssm_in[:, b * CH:(b + 1) * CH], bank[:, t2_bank(n, c), :], pw[:, at:at + CH],
                                  ALU.mult).then_inc(s["xn_ready"], 1)
                eng.wait_ge(s["xn_ready"], nth_hi(n, c))
                first = 0.0 if at == 0 else ssm_sum[:, (1 - b) * CH + CH - 1:(1 - b) * CH + CH]
                eng.tensor_tensor_scan(ssm_sum[:, b * CH:(b + 1) * CH], ssm_in[:, b * CH:(b + 1) * CH],
                                       zero1[:, 0:1].to_broadcast([128, CH]), first, ALU.add, ALU.add)\
                    .then_inc(s["ssm_step"], 1)
                eng.wait_ge(s["ssm_step"], step + 1)
                hi = L - 1 - at
                back = pw[:, hi - CH + 1:hi + 1][:, ::-1]
                eng.scalar_tensor_tensor(out=ssm_y[:, b, :], in0=ssm_sum[:, b * CH:(b + 1) * CH],
                                         scalar=ab[:, 3:4], in1=back, op0=ALU.mult, op1=ALU.mult)\
                    .then_inc(s["ssm_step"], 1)
                eng.wait_ge(s["ssm_step"], step + 2)
                if c >= 2:
                    eng.wait_ge(s["gelu_ready"], c - 1)
                eng.scalar_tensor_tensor(out=ssm_z[:, b, :], in0=xn[:, chunk(c)], scalar=vecs[:, 3:4],
                                         in1=ssm_y[:, b, :], op0=ALU.mult, op1=ALU.add).then_inc(s["y_ready"], 1)

            def ssm_resid(c):
                eng.wait_ge(s["proj_ready"], c + 1)
                k = LN_INNER * NC + c
                if c >= 2:
                    eng.wait_ge(s["t1_ready"], k - 1 - NC)
                eng.scalar_tensor_tensor(out=resid[:, c % 2, :], in0=bank[:, O[c % 2], :], scalar=vecs[:, 4:5],
                                         in1=xn[:, chunk(c)], op0=ALU.add, op1=ALU.add)\
                    .then_inc(s["resid_ready"], 1)

            def ssm_out(c):
                eng.wait_ge(s["inner_scaled"], c + 1)
                eng.tensor_tensor(x[:, chunk(c)], tmp[:, c % 2, :], x[:, chunk(c)], ALU.add)\
                    .then_inc(s["x_ready"], 1)

            def lora_scaled(r, c):
                k = (r - 2) * NC + c
                eng.wait_ge(s["z_copied"], k + 1)
                eng.wait_ge(s["ew_ready"], k + 1)
                if k >= 2:
                    eng.wait_ge(s["zs_lo_ready"], k - 1)
                eng.tensor_tensor(act[:, k % 2, :], glu[:, k % 2, :], bank[:, EW, :], ALU.mult)\
                    .then_inc(s["zs_ready"], 1)

            def lora_lo(r, c):
                k = (r - 2) * NC + c
                eng.wait_ge(s["zs_hi_ready"], k + 1)
                if k >= 2:
                    eng.wait_ge(s["out1_ready"], k - 1)
                eng.tensor_tensor(act_lo[:, k % 2, :], act[:, k % 2, :], act_hi[:, k % 2, :].bitcast(F32),
                                  ALU.subtract).then_inc(s["zs_lo_ready"], 1)

            def lora_out(r, c):
                k = (r - 2) * NC + c
                eng.wait_ge(s["out1_ready"], k + 1)
                eng.scalar_tensor_tensor(out=x[:, chunk(c)], in0=bank[:, OUT1, :], scalar=ab[:, 4:5],
                                         in1=x[:, chunk(c)], op0=ALU.add, op1=ALU.add)\
                    .then_inc(s["x_ready"], 1)

            def routed_norm(n, r, at=0):
                return {at: lambda c: norm_stats(n, c), at + 2: lambda c: norm_lo(n, c),
                        at + 3: lambda c: router_pick(r, c), at + 4: lambda c: router_share(r, c)}

            def lora_stages(n, r):
                return {**routed_norm(n, r), 5: lambda c: lora_scaled(r, c), 6: lambda c: lora_lo(r, c),
                        7: lambda c: lora_out(r, c)}

            def attn_first(c):
                o = 4 * (c % 2)
                eng.wait_ge(s["qkv_ready"], c + 1)
                if c == 0:
                    eng.wait_ge(s["prep_loaded"], 16 * len(LATER))
                else:
                    eng.wait_ge(s["q_lo_ready"], 2 * c)
                at = slice(c % QC * CH, (c % QC + 1) * CH)
                for i in range(2):
                    eng.tensor_tensor(qk_f[:, i, :], bank[:, o, :], q_decay[:, i, at], ALU.mult)\
                        .then_inc(s["q_decayed"], 1)

            def attn_second(c):
                o = 4 * (c % 2)
                for i in range(2):
                    eng.wait_ge(s["q_hi_ready"], 2 * c + i + 1)
                    eng.tensor_tensor(act_lo[:, i, :], qk_f[:, i, :], act_hi[:, i, :].bitcast(F32), ALU.subtract)\
                        .then_inc(s["q_lo_ready"], 1)
                eng.wait_ge(s["k_sq_ready"], c + 1)
                eng.tensor_tensor(act_lo[:, 2, :], bank[:, o + 3, :], act_hi[:, 2, :].bitcast(F32), ALU.subtract)\
                    .then_inc(s["k_lo_ready"], 1)
                b = c // QC
                eng.wait_ge(s["norms_ready"], c + 1)
                eng.reduce_max(head_max[:, b, 0, c % QC:c % QC + 1], bank[:, o, :], axis=AX.X)
                eng.reduce_max(head_max[:, b, 1, c % QC:c % QC + 1], bank[:, o + 2, :], axis=AX.X)\
                    .then_inc(s["maxes_ready"], 1)

            def attn_stacks(c):
                for i in range(1, 3 * G4, 2):
                    n = c * 3 * G4 + i
                    eng.wait_ge(s["stack_ready"], n + 1)
                    eng.tensor_copy(stack_place(i, c), bank[:, i % 4, :]).then_inc(s["stack_copied_v"], 1)

            def attn_bound(b):
                eng.wait_ge(s["maxes_ready"], QC * (b + 1))
                eng.tensor_reduce(tops[:, b, 0:2], head_max[:, b], axis=AX.X, op=ALU.max)\
                    .then_inc(s["bound_step"], 1)
                eng.wait_ge(s["bound_step"], b + 1)
                eng.tensor_tensor(tops[:, b, 2:3], tops[:, b, 0:1], tops[:, b, 1:2], ALU.mult)\
                    .then_inc(s["tops_ready"], 1)
                eng.wait_ge(s["tops_row"], b + 1)
                eng.reduce_max(bound[:, b, 0:1], bank[0:1, 7, 0:128], axis=AX.X).then_inc(s["bound_ready"], 1)
                eng.wait_ge(s["bound_ready"], b + 1)
                eng.tensor_scalar(small_scores[:, b:b + 1], bound[:, b, 0:1], SAFE_BOUND ** 2, None, ALU.is_le)\
                    .then_inc(s["flag_ready"], 1)
                eng.wait_ge(s["flag_ready"], b + 1)

            def attn_fast(b):
                def take_out(n):
                    g, qc = n // QC, n % QC
                    o = 6 + n % 2
                    eng.wait_ge(s[f"pv_done{b}"], KB * (n + 1))
                    if n >= 2:
                        eng.wait_ge(s[f"ot_ready{b}"], n - 1)
                    eng.tensor_copy(out_t[:, n % 2, :], bank[:, o, :]).then_inc(s[f"ot_copied{b}"], 1)

                def normalize(n):
                    g, qc = n // QC, n % QC
                    rows = bank[:, 6 + n % 2, :].rearrange("p (t j m) -> p t j m", t=TPC, j=HG)
                    eng.wait_ge(s[f"ot_ready{b}"], n + 1)
                    eng.reciprocal(out_recip[:], rows[:, :, :, HD]).then_inc(s[f"recip_ready{b}"], 1)
                    eng.wait_ge(s[f"recip_ready{b}"], n + 1)
                    at = KB * b + TPC * qc
                    place = x_tok[:, at:at + TPC, HG * HD * g:HG * HD * (g + 1)]
                    ins = eng.tensor_tensor(place.rearrange("p t (j d) -> p t j d", j=HG), rows[:, :, :, 0:HD],
                                            out_recip[:, :, :, None].to_broadcast([128, TPC, HG, HD]), ALU.mult)
                    ins.then_inc(s[f"normed{b}"], 1)

                for u in range(UNITS):
                    g, qc, kb, hp = unit(u)
                    if kb // (CH // 128) == qc:
                        i = kb % (CH // 128)
                        w = 128 * (i + 1)
                        turned = fix[:, None, CH - w:CH].to_broadcast([128, 2, w])
                        pair = bank[:, 2 * (u % 3):2 * (u % 3) + 2, 0:w]
                        eng.wait_ge(s[f"scored{b}"], u + 1)
                        eng.tensor_tensor(pair, pair, turned, ALU.mult)\
                            .then_inc(s[f"fixed{b}"], 1)
                    n = u // (2 * KB)
                    if u % (2 * KB) == 4 and n > 0:
                        take_out(n - 1)
                    if u % (2 * KB) == 8 and n > 0:
                        normalize(n - 1)
                take_out(G4 * QC - 1)
                normalize(G4 * QC - 1)

            def attn_general(b):
                eng.wait_ge(s[f"gen_table{b}"], 16)
                for half in range(2):
                    with eng.Fori(0, 2) as gl:
                        with eng.Fori(0, KB) as qb:
                            eng.tensor_copy(gen_k, k_parts[half][:, bass.ds(gl, 1), :].bitcast(F32)
                                            .rearrange("p a t -> p (a t)"))
                            eng.tensor_copy(gen_q, q_stack[0][:, bass.ds(2 * half + gl, 1), bass.ds(128 * qb, 128)]
                                            .bitcast(F32).rearrange("p a t -> p (a t)"))
                            eng.tensor_copy(gen_unscale, k_decay[:, 0, bass.ds(qb, 1)])
                            eng.tensor_copy(gen_decay, gen_decays[:, bass.ds(L - 128 - 128 * qb, L)])
                            eng.tensor_copy(gen_v, values[:, :, bass.ds(HG * (2 * half + gl), HG), :])\
                                .then_inc(s[f"gen_staged{b}"], 1)
                            for j in range(HG):
                                n = (2 * half * KB + gl * KB + qb) * HG + j
                                eng.wait_ge(s[f"gen_scored{b}"], n + 1)
                                eng.tensor_scalar(gen_s, bank[:, 0:2, :].rearrange("p a q -> p (a q)"), gen_unscale,
                                                  -CLAMP, ALU.mult, ALU.max).then_inc(s[f"gen_clipped{b}"], 1)
                                eng.wait_ge(s[f"gen_clipped{b}"], n + 1)
                                eng.scalar_tensor_tensor(out=gen_s, in0=gen_s, scalar=CLAMP,
                                                         in1=gen_decay,
                                                         op0=ALU.min, op1=ALU.mult).then_inc(s[f"gen_decayed{b}"], 1)
                                eng.wait_ge(s[f"gen_decayed{b}"], n + 1)
                                eng.reduce_max(tops[:, b, 0:1], gen_s, axis=AX.X).then_inc(s[f"gen_max{b}"], 1)
                                eng.wait_ge(s[f"gen_max{b}"], n + 1)
                                eng.tensor_scalar(tops[:, b, 1:2], tops[:, b, 0:1], -1.0, None, ALU.mult)\
                                    .then_inc(s[f"gen_neg{b}"], 1)
                                eng.wait_ge(s[f"gen_pv{b}"], n + 1)
                                eng.reciprocal(gen_recip, tops[:, b, 2:3]).then_inc(s[f"gen_recip{b}"], 1)
                                eng.wait_ge(s[f"gen_recip{b}"], n + 1)
                                eng.tensor_scalar(gen_heads[:, HD * j:HD * (j + 1)], bank[:, 4, 0:HD], gen_recip,
                                                  None, ALU.mult).then_inc(s[f"gen_out{b}"], 1)
                            eng.wait_ge(s[f"gen_out{b}"], (2 * half * KB + gl * KB + qb + 1) * HG)
                            eng.tensor_copy(gen_spare, gen_recip)
                            eng.tensor_copy(x_tok[:, bass.ds(KB * b + qb, 1), bass.ds(HG * HD * (2 * half + gl), HG * HD)]
                                            .rearrange("p a d -> p (a d)"), gen_heads)

            def attn_out(b):
                for c in range(QC * b, QC * (b + 1)):
                    eng.wait_ge(s["ao_hi_ready"], c + 1)
                    eng.tensor_tensor(act_lo[:, c % 2, :], bank[:, 4 + c % 2, :], act_hi[:, c % 2, :].bitcast(F32),
                                      ALU.subtract).then_inc(s["ao_lo_ready"], 1)
                for c in range(QC * b, QC * (b + 1)):
                    eng.wait_ge(s["attn_out"], c + 1)
                    eng.tensor_tensor(x[:, chunk(c)], bank[:, 6 + c % 2, :], x[:, chunk(c)], ALU.add)\
                        .then_inc(s["x_ready"], 1)

            def attention():
                eng.memset(values[:, :, :, HD:VW], 1.0)
                for b in range(NB):
                    attn_first(QC * b)
                    attn_second(QC * b)
                    for c in range(QC * b, QC * (b + 1)):
                        if c + 1 < QC * (b + 1):
                            attn_first(c + 1)
                        else:
                            attn_bound(b)
                        attn_stacks(c)
                        if c + 1 < QC * (b + 1):
                            attn_second(c + 1)
                    fast = eng.value_load(small_scores[0:1, b:b + 1], min_val=0, max_val=1)
                    with eng.If(fast):
                        attn_fast(b)
                    with eng.Else():
                        attn_general(b)
                    eng.memset(tops[:, b, 0:1], 0.0).then_inc(s["ao_ready"], 1)
                    attn_out(b)

            eng.wait_ge(s["consts_ready"], 1)
            def take_in_and_stats(c):
                norm_stats(LN_FFN0A, c)
                take_in(c)

            skewed({**routed_norm(LN_FFN0A, 0), 0: take_in_and_stats},
                   before={2: split_small, 3: ssm_powers, 5: lambda: split_experts(0),
                           6: lambda: split_experts(1)})
            for g in range(2, 4):
                split_experts(g)
            experts(0)
            skewed({0: lambda c: norm_stats(LN_SSM, c), 2: ssm_scan, 4: ssm_resid,
                    4.5: lambda c: norm_stats(LN_INNER, c), 7: ssm_out, **routed_norm(LN_FFN0B, 1, 8)},
                   last=(0, 4.5))
            experts(1)
            skewed({**lora_stages(LN_FFN1A, 2), 8: lambda c: norm_stats(LN_ATTN, c),
                    10: lambda c: norm_lo(LN_ATTN, c)}, last=(5, 8, 0))
            attention()
            skewed(lora_stages(LN_FFN1B, 3), last=(5, 0))

        @block.tensor
        def _(pe):
            def split_matmul(out, w_hi, w_lo, v_hi, v_lo, start, stop):
                pe.matmul(out, w_hi, v_hi, start=start, stop=False)
                pe.matmul(out, w_lo, v_hi, start=False, stop=False)
                return pe.matmul(out, w_hi, v_lo, start=False, stop=stop)

            def take_in(c):
                pe.wait_ge(s[f"x_loaded{c}"], 16)
                if c >= 2:
                    pe.wait_ge(s["x_ready"], nth(X_IN, c - 2))
                for t in range(TPC):
                    last = pe.transpose(bank[:, O[c % 2], 128 * t:128 * (t + 1)], x_tok[:, TPC * c + t, :], ident[:])
                last.then_inc(s["tok_in"], 1)

            def norm_in(n, c, version):
                k = n * NC + c
                b = k % 2
                if n == LN_INNER:
                    pe.wait_ge(s["resid_ready"], c + 1)
                else:
                    pe.wait_ge(s["x_ready"], nth(version, c))
                pe.wait_ge(s["normalized"], k - 1)
                for t in range(TPC):
                    src = (resid[:, c % 2, 128 * t:128 * (t + 1)] if n == LN_INNER else
                           x[:, c * CH + 128 * t:c * CH + 128 * (t + 1)])
                    last = pe.transpose(bank[:, T1[b], 128 * t:128 * (t + 1)], src, ident[:])
                last.then_inc(s["t1_ready"], 1)

            def norm_out(n, c):
                k = n * NC + c
                b = k % 2
                pe.wait_ge(s["normalized"], k + 1)
                last_n, last_c = divmod(k - (2 if n < LN_FFN1A else 1), NC)
                if last_n == LN_INNER:
                    pe.wait_ge(s["inner_scaled"], last_c + 1)
                elif k >= 2:
                    pe.wait_ge(s["xn_ready"], nth_hi(last_n, last_c))
                for t in range(TPC):
                    last = pe.transpose(bank[:, t2_bank(n, c), 128 * t:128 * (t + 1)], xt[:, b, t, :], ident[:])
                last.then_inc(s["t2_ready"], 1)

            def router_logits(r, n, c):
                kr = r * NC + c
                w_hi, w_lo = (r_hi[:, 0:16], r_lo[:, 0:16]) if r < 2 else (r_hi[:, 16:32], r_lo[:, 16:32])
                pe.wait_ge(s["xn_ready"], nth_hi(n, c))
                pe.wait_ge(s["small_ready"], 1)
                if kr >= 1:
                    pe.wait_ge(s["logit_step"], kr)
                for t in range(TPC):
                    at = slice(c * CH + 128 * t, c * CH + 128 * (t + 1))
                    out = bank[:, LG, 16 * t:16 * (t + 1)]
                    last = split_matmul(out, xn_hi[:, at], xn_lo[:, at], w_hi, w_lo, True, True)
                last.then_inc(s["logits_ready"], 1)

            def router_scores(r, c):
                kr = r * NC + c
                nr = 2 * E0 if r < 2 else 2 * TRUE1
                pe.wait_ge(s["share_ready"], kr + 1)
                if kr >= 1:
                    pe.wait_ge(s["score_ready"], kr)
                for t in range(TPC):
                    last = pe.transpose(bank[0:nr, ST, 128 * t:128 * (t + 1)], share_hl[:, kr % 2, t, 0:nr], ident[:])
                last.then_inc(s["score_psum_ready"], 1)

            def experts(f):
                def down(j):
                    e, c, slot = j % E0, j // E0 % NC, j % NACT
                    out = bank[:, O[c % 2], :]
                    if e == 0:
                        if c >= 2:
                            pe.wait_ge(s["x_ready"], nth(X_FFN0A if f == 0 else X_FFN0B, c - 2))
                        pe.matmul(out, db_hi[:], score_t[:, chunk(c)], start=True, stop=False)
                        pe.matmul(out, db_lo[:], score_t[:, chunk(c)], start=False, stop=False)
                    pe.wait_ge(s["hi_ready"], j + 1)
                    pe.matmul(out, w0_hi[:, e, 2, :], act_hi[:, slot, :], start=False, stop=False)
                    pe.matmul(out, w0_lo[:, e, 2, :], act_hi[:, slot, :], start=False, stop=False)
                    pe.wait_ge(s["lo_ready"], j + 1)
                    last = pe.matmul(out, w0_hi[:, e, 2, :], act_lo[:, slot, :], start=False, stop=e == E0 - 1)
                    last.then_inc(s["down_done"], 1)

                first, end = f * NC * E0, (f + 1) * NC * E0
                pe.wait_ge(s["cast_loaded"], 48)
                for j in range(first, end + 2):
                    if j < end:
                        e, c, b = j % E0, j // E0 % NC, j % 2
                        at = chunk(c)
                        if f == 0 and c == 0 and e % 4 == 0:
                            pe.wait_ge(s["w0_lo_ready"], e // 4 + 1)
                        if j >= 2:
                            pe.wait_ge(s["glu_ready"], j - 1)
                        split_matmul(bank[:, G[b], :], w0_hi[:, e, 0, :], w0_lo[:, e, 0, :],
                                     xn_hi[:, at], xn_lo[:, at], True, True).then_inc(s["g_ready"], 1)
                        if j >= 2:
                            pe.wait_ge(s["up_ready"], j - 1)
                        split_matmul(bank[:, U[b], :], w0_hi[:, e, 1, :], w0_lo[:, e, 1, :],
                                     xn_hi[:, at], xn_lo[:, at], True, True).then_inc(s["u_ready"], 1)
                        if j >= 2:
                            pe.wait_ge(s["glu_s_ready"], j - 1)
                        if j == first:
                            pe.wait_ge(s["score_ready"], nth(f, NC - 1))
                        pe.matmul(bank[:, S[b], :], sel0[:, e, :], score_t[:, at], start=True, stop=True)\
                          .then_inc(s["s_ready"], 1)
                    if j - 2 >= first:
                        down(j - 2)

            def ssm_proj(c):
                pe.wait_ge(s["gelu_lo_ready"], c + 1)
                if c >= 2:
                    pe.wait_ge(s["resid_ready"], c - 1)
                split_matmul(bank[:, O[c % 2], :], sq_hi[:, 0, :], sq_lo[:, 0, :], act_hi[:, c % 2, :],
                             act_lo[:, c % 2, :], True, True).then_inc(s["proj_ready"], 1)

            def lora_front(r, c):
                k = (r - 2) * NC + c
                at = chunk(c)
                if k >= 1:
                    pe.wait_ge(s["z_copied"], k)
                split_matmul(bank[:, Z, :], sq_hi[:, 2, :], sq_lo[:, 2, :], xn_hi[:, at], xn_lo[:, at],
                             True, True).then_inc(s["z_ready"], 1)
                if k >= 1:
                    pe.wait_ge(s["zs_ready"], k)
                pe.wait_ge(s["score_ready"], nth(r, c))
                pe.matmul(bank[:, EW, :], sel1[:], score_t[0:2 * TRUE1, at], start=True, stop=True)\
                  .then_inc(s["ew_ready"], 1)

            def lora_back(r, c):
                k = (r - 2) * NC + c
                at = chunk(c)
                if c >= 1:
                    pe.wait_ge(s["x_ready"], nth(X_FFN1A if r == 2 else X_FFN1B, c - 1))
                split_matmul(bank[:, OUT1, :], sq_hi[:, 1, :], sq_lo[:, 1, :], xn_hi[:, at], xn_lo[:, at],
                             True, False)
                pe.wait_ge(s["zs_lo_ready"], k + 1)
                split_matmul(bank[:, OUT1, :], sq_hi[:, 3, :], sq_lo[:, 3, :], act_hi[:, k % 2, :],
                             act_lo[:, k % 2, :], False, True).then_inc(s["out1_ready"], 1)

            def routed_norm(n, r, version, at=0):
                return {at: lambda c: norm_in(n, c, version), at + 1: lambda c: norm_out(n, c),
                        at + 2: lambda c: router_logits(r, n, c), at + 4: lambda c: router_scores(r, c)}

            def lora_stages(n, r, version):
                return {**routed_norm(n, r, version), 5: lambda c: lora_front(r, c), 6: lambda c: lora_back(r, c)}

            def attn_first(c):
                o = 4 * (c % 2)
                at = chunk(c)
                pe.wait_ge(s["xn_ready"], nth_hi(LN_ATTN, c))
                if c == 0:
                    pe.wait_ge(s["xn_ready"], nth_hi(LN_ATTN, NC - 1))
                elif c == QC:
                    pe.wait_ge(s["x_ready"], nth(X_ATTN, QC - 1))
                split_matmul(bank[:, o, :], sq_hi[:, WQ, :], sq_lo[:, WQ, :], xn_hi[:, at], xn_lo[:, at], True, True)
                split_matmul(bank[:, o + 1, :], sq_hi[:, WK, :], sq_lo[:, WK, :], xn_hi[:, at], xn_lo[:, at],
                             True, False)
                split_matmul(bank[:, o + 1, :], sq_hi[:, WV, :], sq_lo[:, WV, :], xn_hi[:, at], xn_lo[:, at],
                             False, True).then_inc(s["qkv_ready"], 1)

            def attn_second(c):
                o = 4 * (c % 2)
                pe.wait_ge(s["prep_loaded"], 16 * len(LATER))
                pe.wait_ge(s["kv_copied"], c + 1)
                pe.matmul(bank[0:LAT, o + 2, :], w_down[:], kv_f, start=True, stop=True).then_inc(s["lat_ready"], 1)
                pe.wait_ge(s["lat_copied"], c + 1)
                pe.matmul(bank[:, o + 3, :], w_up[:, 0, :], lat_f, start=True, stop=True)
                for t in range(TPC):
                    last = pe.matmul(bank[:, o + 1, 128 * t:128 * (t + 1)], lat_f[:, 128 * t:128 * (t + 1)],
                                     w_up[:, 1, :], start=True, stop=True)
                last.then_inc(s["kv_rec_ready"], 1)
                pe.wait_ge(s["q_decayed"], 2 * c + 2)
                pe.wait_ge(s["k_sq_ready"], c + 1)
                pe.matmul(bank[:, o, :], same_head[:], q_sq, start=True, stop=True)
                pe.matmul(bank[:, o + 2, :], same_head[:], k_sq, start=True, stop=True)\
                  .then_inc(s["norms_ready"], 1)

            def attn_stacks(c):
                pe.wait_ge(s["cast_loaded"], 48)
                pe.wait_ge(s["maxes_ready"], c + 1)
                pe.wait_ge(s["k_lo_ready"], c + 1)
                pe.wait_ge(s["v_copied"], c + 1)
                for i in range(3 * G4):
                    n = c * 3 * G4 + i
                    g, kind = i // 3, (i + 2) % 3
                    if n >= 4:
                        pe.wait_ge(s["stack_copied"] if i % 2 == 0 else s["stack_copied_v"], (n - 4) // 2 + 1)
                    part = 2 if kind == 2 else 0
                    out = bank[:, i % 4, :]
                    pe.matmul(out, sel_h[:, g, part, :], act_hi[:, kind, :], start=True, stop=False)
                    pe.matmul(out, sel_h[:, g, part + 1, :], act_lo[:, kind, :], start=False, stop=True)\
                      .then_inc(s["stack_ready"], 1)

            def attn_bound(b):
                pe.wait_ge(s["k_lo_ready"], QC * (b + 1))
                pe.wait_ge(s["tops_ready"], b + 1)
                pe.transpose(bank[0:1, 7, 0:128], tops[:, b, 2:3], ident[:]).then_inc(s["tops_row"], 1)

            def attn_spread(b):
                pe.wait_ge(s["sqrt_ready"], b + 1)
                pe.wait_ge(s["flag_ready"], b + 1)
                pe.matmul(bank[:, 7, 0:1], minus_one[:], bound[:, b, 1:2], start=True, stop=True)\
                  .then_inc(s["neg_ready"], 1)
                pe.wait_ge(s[f"keys_masked{b}"], HG * QC)
                pe.wait_ge(s["stack_copied"], 3 * G4 // 2 * QC * (b + 1))
                pe.wait_ge(s["stack_copied_v"], 3 * G4 // 2 * QC * (b + 1))
                pe.wait_ge(s["minus_c_ready"], b + 1)

            def attn_fast(b):
                def scores(u):
                    g, qc, kb, hp = unit(u)
                    side = 1 if kb // (CH // 128) > qc else 0
                    if u >= 3:
                        pe.wait_ge(s[f"exped{b}"], u - 2)
                    if g >= 1 and qc == 0 and kb == 0:
                        pe.wait_ge(s[f"keys_masked{b}"], HG * (QC + g - 1) + 2 * hp + 2)
                    for a in range(2):
                        j = 2 * hp + a
                        last = pe.matmul(bank[:, 2 * (u % 3) + a, :], head_keys(b, g, j)[:, 128 * kb:128 * (kb + 1)],
                                         q_stack[side][:, g, CH * qc:CH * (qc + 1)], start=True, stop=True)
                    last.then_inc(s[f"scored{b}"], 1)

                def weigh(t):
                    n, i = t // KB, t % KB
                    g, _, kb, _ = unit(2 * t)
                    if i == 0 and n >= 2:
                        pe.wait_ge(s[f"normed{b}"], n - 1)
                    for j in range(HG):
                        u = 2 * t + j // 2
                        pe.wait_ge(s[f"exped{b}"], u + 1)
                        last = pe.matmul(bank[32 * j:32 * j + VW, 6 + n % 2, :], values[:, kb, HG * g + j, :],
                                         probs[:, u % NP, CH * (j % 2):CH * (j % 2 + 1)],
                                         start=i == 0, stop=i == KB - 1, tile_position=(0, 32 * j))
                    last.then_inc(s[f"pv_done{b}"], 1)

                def turn(n):
                    pe.wait_ge(s[f"ot_copied{b}"], n + 1)
                    for t in range(TPC):
                        last = pe.transpose(bank[:, 6 + n % 2, 128 * t:128 * (t + 1)],
                                            out_t[:, n % 2, 128 * t:128 * (t + 1)], ident[:])
                    last.then_inc(s[f"ot_ready{b}"], 1)

                steps = UNITS // 2
                for t in range(steps + 1):
                    if t < steps:
                        scores(2 * t)
                        scores(2 * t + 1)
                    if t >= 1:
                        weigh(t - 1)
                    if t % KB == 4 and t >= KB:
                        turn(t // KB - 1)
                turn(G4 * QC - 1)

            def attn_general(b):
                with pe.Fori(0, G4 * KB) as block_of_queries:
                    pe.wait_ge(s[f"gen_staged{b}"], block_of_queries + 1)
                    for j in range(HG):
                        n = block_of_queries * HG + j
                        rows = slice(32 * j, 32 * (j + 1))
                        for a in range(2):
                            last = pe.matmul(bank[:, a, :], act_hi[rows, 2, 0:128], act_hi[rows, a, :],
                                             start=True, stop=True)
                        last.then_inc(s[f"gen_scored{b}"], 1)
                        pe.wait_ge(s[f"gen_probs{b}"], n + 1)
                        for kb in range(KB):
                            last = pe.transpose(bank[:, 2 + kb // 4, 128 * (kb % 4):128 * (kb % 4 + 1)],
                                                gen_s[:, 128 * kb:128 * (kb + 1)], ident[:])
                        last.then_inc(s[f"gen_t{b}"], 1)
                        pe.wait_ge(s[f"gen_tc{b}"], n + 1)
                        for kb in range(KB):
                            last = pe.matmul(bank[:, 4, 0:HD], gen_pt[:, 128 * kb:128 * (kb + 1)],
                                             gen_v[:, kb, j, 0:HD], start=kb == 0, stop=kb == KB - 1)
                        last.then_inc(s[f"gen_pv{b}"], 1)

            def attn_out(b):
                pe.wait_ge(s["ao_ready"], b + 1)
                for c in range(QC * b, QC * (b + 1)):
                    for t in range(TPC):
                        last = pe.transpose(bank[:, 4 + c % 2, 128 * t:128 * (t + 1)], x_tok[:, TPC * c + t, :],
                                            ident[:])
                    last.then_inc(s["ao_t_ready"], 1)
                for c in range(QC * b, QC * (b + 1)):
                    pe.wait_ge(s["ao_lo_ready"], c + 1)
                    split_matmul(bank[:, 6 + c % 2, :], sq_hi[:, WO, :], sq_lo[:, WO, :], act_hi[:, c % 2, :],
                                 act_lo[:, c % 2, :], True, True).then_inc(s["attn_out"], 1)

            def attention():
                for b in range(NB):
                    attn_first(QC * b)
                    attn_second(QC * b)
                    for c in range(QC * b, QC * (b + 1)):
                        if c + 1 < QC * (b + 1):
                            attn_first(c + 1)
                        else:
                            attn_bound(b)
                        attn_stacks(c)
                        if c + 1 < QC * (b + 1):
                            attn_second(c + 1)
                    attn_spread(b)
                    fast = pe.value_load(small_scores[0:1, b:b + 1], min_val=0, max_val=1)
                    with pe.If(fast):
                        attn_fast(b)
                    with pe.Else():
                        attn_general(b)
                    attn_out(b)

            pe.wait_ge(s["ident_loaded"], 16)
            skewed({**routed_norm(LN_FFN0A, 0, None), 0: take_in}, first=(0,))
            experts(0)
            skewed({0: lambda c: norm_in(LN_SSM, c, X_FFN0A), 1: lambda c: norm_out(LN_SSM, c), 3: ssm_proj,
                    4: lambda c: norm_in(LN_INNER, c, None), 5: lambda c: norm_out(LN_INNER, c),
                    **routed_norm(LN_FFN0B, 1, X_SSM, 8)}, first=(8, 0))
            experts(1)
            skewed({**lora_stages(LN_FFN1A, 2, X_FFN0B), 8: lambda c: norm_in(LN_ATTN, c, X_FFN1A),
                    9: lambda c: norm_out(LN_ATTN, c)}, first=(8, 0))
            attention()

            def turn_back(c):
                pe.wait_ge(s["x_ready"], nth(X_FFN1B, c))
                if c >= 2:
                    pe.wait_ge(s["out_copied"], c - 1)
                for t in range(TPC):
                    at = slice(c * CH + 128 * t, c * CH + 128 * (t + 1))
                    last = pe.transpose(bank[:, T1[c % 2], 128 * t:128 * (t + 1)], x[:, at], ident[:])
                last.then_inc(s["fin_ready"], 1)

            skewed({**lora_stages(LN_FFN1B, 3, X_ATTN), 8: turn_back}, first=(8, 0))


def position_tables():
    t = np.arange(L, dtype=np.float64)
    side = np.array([-1.0, 1.0])
    grow = np.exp(-DECAY * side[:, None] * (t - L // 2))
    p, q = np.arange(128)[:, None], np.arange(CH)[None, :]
    row = np.arange(128)
    col_head, col_slot, col_d = row // 32, row % 32 // HD, row % HD
    sel = np.zeros((128, G4, 4, 128))
    for g in range(G4):
        same = row[:, None] == (HG * g + col_head[None, :]) * HD + col_d[None, :]
        for part, slots in enumerate(((0, 1), (2, 3), (0, 2), (1, 3))):
            sel[:, g, part, :] = same & np.isin(col_slot, slots)[None, :]
    tables = {
        "q_decay": np.broadcast_to(SCALE * grow[::-1][None], (128, 2, L)),
        "k_decay": grow.reshape(2, KB, 128).transpose(2, 0, 1),
        "fix": np.exp(-2 * DECAY * np.maximum(CH - 128 + p - q, 0)),
        "decay": np.exp(-DECAY * np.abs(np.arange(128)[:, None] - (np.arange(2 * L - 128) - (L - 128))[None, :])),
        "same_head": row[:, None] // HD == row[None, :] // HD,
        "sel_h": sel,
        "head_rows": row[:, None] // 32 == np.arange(HG)[None, :],
    }
    return {k: v.astype(np.float32) for k, v in tables.items()}


def kernel(**inputs):
    import concourse.bacc as bacc
    from concourse.bass_utils import run_bass_kernel_spmd

    a = {k: np.asarray(v) for k, v in inputs.items()}
    p = "L0_ffn_"
    gate_up = a[p + "gate_up_proj"].reshape(E0, D, D, 2)
    bias = a[p + "gate_up_bias"].reshape(E0, D, 2)
    k32, m128 = np.arange(2 * E0), np.arange(128)
    host = {
        "x": a["L0_attn_x"].reshape(T, D),
        "gate_up": gate_up.transpose(1, 0, 3, 2),
        "down": a[p + "down_proj"].transpose(1, 0, 2),
        "down_bias": a[p + "down_bias"],
        "router_w": a[p + "router_w"],
        "router_b": np.broadcast_to(a[p + "router_b"], (128, E0)),
        "gate_w": a["L1_ffn_gate_w"].T,
        "b_gate": bias[:, :, 0].T,
        "b_up": bias[:, :, 1].T,
        "vecs": np.stack([a["L0_attn_" + n] for n in ("A_param", "B_vec", "C_vec", "D_vec", "b_proj", "gamma",
                                                      "beta")] + [a["L1_ffn_base_b"]], axis=1),
        "squares": np.stack([a["L0_attn_W_proj"].T, a["L1_ffn_base_w"].T,
                             a["L1_ffn_lora_A"].reshape(TRUE1 * RANK, D).T,
                             a["L1_ffn_lora_B"].transpose(0, 2, 1).reshape(TRUE1 * RANK, D),
                             a["L1_attn_Wq"], a["L1_attn_Wk"], a["L1_attn_Wv"], a["L1_attn_Wo"]], axis=1),
        "w_down": a["L1_attn_W_down_kv"],
        "w_up": np.stack([a["L1_attn_W_up_k"], a["L1_attn_W_up_v"]], axis=1),
        **position_tables(),
        "ident": np.eye(128, dtype=np.float32),
        "sel0": np.broadcast_to((k32[:, None] % E0 == np.arange(E0))[:, :, None], (2 * E0, E0, 128))
                  .astype(np.float32),
        "sel1": (np.arange(2 * TRUE1)[:, None] % TRUE1 == m128 // RANK).astype(np.float32),
    }
    nc = bacc.Bacc("TRN2", target_bir_lowering=False, num_devices=1)
    arrays, io = {}, {}
    for name, v in host.items():
        v = np.ascontiguousarray(v)
        arrays[f"in_{name}"] = v
        io[name] = nc.dram_tensor(f"in_{name}", v.shape, mybir.dt.from_np(v.dtype), kind="ExternalInput").ap()
    io["out"] = nc.dram_tensor("out_0", (T, D), F32, kind="ExternalOutput").ap()
    build(nc, io)
    result = run_bass_kernel_spmd(nc, [arrays], core_ids=[0])
    return result.results[0]["out_0"].reshape(NB, L, D)
```

```python
import numpy as np
import concourse.bass as bass
from concourse import mybir
from contextlib import ExitStack

F32 = mybir.dt.float32
F32R = mybir.dt.float32r
ALU = mybir.AluOpType
ACT = mybir.ActivationFunctionType
AX = mybir.AxisListType

D = 128
NB, L = 2, 1024
T = NB * L
CH = 512
NC = T // CH
TPC = CH // 128
EPS = 1e-5
E0, TOP0 = 16, 4
E1, TOP1, TRUE1, RANK = 10, 2, 8, 16
LIMIT, ALPHA = 7.0, 1.702
GLU_AT_LIMIT = LIMIT / (1.0 + float(np.exp(-ALPHA * LIMIT)))
SENTINEL, TAKEN = 3.0e38, -3.0e38

LN_FFN0A, LN_SSM, LN_INNER, LN_FFN0B, LN_FFN1A, LN_ATTN, LN_FFN1B = range(7)
X_IN, X_FFN0A, X_SSM, X_FFN0B, X_FFN1A, X_ATTN, X_FFN1B = range(7)

H, HD = 16, 8
LAT = 32
G4, HG = 4, 4
KB = L // 128
QC = L // CH
SCALE = float(np.float32(1.0) / (np.sqrt(np.float32(D)) + np.float32(1e-8)))
CLAMP = 1.0e4
DECAY = 0.01 * 0.01
VW = HD + 1
NP = 4
SAFE_BOUND = 40.0
WQ, WK, WV, WO = 4, 5, 6, 7

STAGES = {
    "ffn0a": {"norm": 0, "take_in": 0, "stats": 0, "rows": 1, "t2": 1, "hi": 2, "lo": 2, "logits": 2, "pick": 3,
              "exp": 3, "share": 4, "scores": 4, "out": 5, "split": 5},
    "ssm": {"t1": 1, "stats": 1, "norm": 1, "rows": 2, "t2": 2, "copy": 3, "scan": 3, "gelu": 4, "gelu_lo": 4,
            "proj": 5, "resid": 5, "inner_t1": 5, "inner_stats": 5, "inner_norm": 5, "inner_rows": 6,
            "inner_t2": 6, "scale": 7, "add": 7, "b_t1": 9, "b_stats": 9, "b_norm": 9, "b_rows": 10, "b_t2": 10,
            "hi": 11, "lo": 11, "logits": 11, "pick": 12, "exp": 12, "share": 13, "scores": 13, "out": 14},
    "ffn1a": {"norm": 0, "t1": 0, "stats": 0, "rows": 1, "t2": 1, "hi": 2, "lo": 2, "logits": 2, "pick": 3,
              "exp": 3, "share": 4, "scores": 4, "out": 5, "z": 5, "z_copy": 5, "zs": 5, "zs_hi": 6, "zs_lo": 6,
              "back": 6, "add": 7, "b_t1": 8, "b_stats": 8, "b_norm": 8, "b_rows": 9, "b_t2": 9, "b_hi": 10,
              "b_lo": 10},
    "ffn1b": {"norm": 0, "t1": 0, "stats": 0, "rows": 1, "t2": 1, "hi": 2, "lo": 2, "logits": 2, "pick": 3,
              "exp": 3, "share": 4, "scores": 4, "out": 5, "z": 5, "z_copy": 5, "zs": 5, "zs_hi": 7, "zs_lo": 7,
              "back": 7, "add": 8, "turn": 9, "copy": 10},
}
ONCE = {"ffn0a": {"split_small": 2, "powers": 3, "split_squares": 7}, "ffn1a": {"first": 11, "second": 12}}
ORDERS = {
    "ffn0a": {
        "pe": ["scores", "take_in", "t2", "logits"],
        "act": ["split", "out", "hi", "rows", "exp"],
        "dve": ["share", "split", "pick", "lo", "stats"],
        "pool": ["norm"],
    },
    "ssm": {
        "pe": ["b_t1", "scores", "logits", "proj", "inner_t1", "inner_t2", "t1", "b_t2", "t2"],
        "act": ["out", "scale", "copy", "gelu", "rows", "b_rows", "inner_rows", "hi", "exp"],
        "dve": ["share", "pick", "lo", "stats", "b_stats", "scan", "resid", "add", "inner_stats"],
        "pool": ["b_norm", "gelu_lo", "inner_norm", "norm"],
    },
    "ffn1a": {
        "pe": ["b_t1", "t1", "b_t2", "back", "z", "scores", "logits", "t2"],
        "act": ["b_hi", "b_rows", "zs_hi", "out", "z_copy", "hi", "rows", "exp"],
        "dve": ["b_lo", "add", "zs_lo", "share", "pick", "lo", "zs", "b_stats", "stats"],
        "pool": ["b_norm", "norm"],
    },
    "ffn1b": {
        "pe": ["turn", "z", "back", "scores", "t1", "logits", "t2"],
        "act": ["copy", "zs_hi", "out", "hi", "rows", "exp", "z_copy"],
        "dve": ["add", "zs_lo", "share", "pick", "lo", "zs", "stats"],
        "pool": ["norm"],
    },
}
HEADS = {"ffn0a": {7: 2}, "ssm": {16: 2}}


def nth(group, c):
    return group * NC + c + 1


def nth_hi(n, c):
    return nth(n - (n > LN_INNER), c)


def build(nc, io):
    ctx = ExitStack()
    with ctx:
        def sb(name, shape, dt=F32):
            return ctx.enter_context(nc.sbuf_tensor(name, shape, dt))

        def sem(name):
            return ctx.enter_context(nc.semaphore(name))

        x = sb("x", [D, T])
        x_tok = sb("x_tok", [128, T // 128, D])
        xn_hi = sb("xn_hi", [D, T], F32R)
        xn_lo = sb("xn_lo", [D, T], F32R)
        ident = sb("ident", [128, 128])
        raw_w = sb("raw_w", [128, E0 * 3 * D])
        w0_hi = sb("w0_hi", [128, E0, 3, D], F32R)
        w0_lo = sb("w0_lo", [128, E0, 3, D], F32R)
        b_gate = sb("b_gate", [128, E0])
        b_up = sb("b_up", [128, E0])
        b_up1 = sb("b_up1", [128, E0])
        raw_s = sb("raw_s", [128, 8, D])
        sq_hi = sb("sq_hi", [128, 8, D], F32R)
        sq_lo = sb("sq_lo", [128, 8, D], F32R)
        raw_r = sb("raw_r", [128, E0 + 16])
        r_split = sb("r_split", [128, 2, 2, 16], F32R)
        raw_db = sb("raw_db", [2 * E0, D])
        db_hi = sb("db_hi", [2 * E0, D], F32R)
        db_lo = sb("db_lo", [2 * E0, D], F32R)
        router_b = sb("router_b", [128, E0])
        sel0_all = sb("sel0", [128, E0, 128], F32R)
        sel0 = sel0_all[0:2 * E0]
        sel1 = sb("sel1", [2 * TRUE1, 128], F32R)
        vecs = sb("vecs", [128, 8])
        ab = sb("ab", [128, 8])
        pw = sb("pw", [128, L])
        zero1 = sb("zero1", [128, 1])
        half_pow = sb("half_pow", [128, TPC])

        stats = sb("stats", [128, 2, TPC, 6])
        mean_var = sb("mean_var", [128, 2, TPC, 2])
        var_eps = sb("var_eps", [128, 2, TPC])
        rstd = sb("rstd", [128, 2, TPC])
        minus_mean = sb("minus_mean", [128, 2, TPC])
        offset = sb("offset", [128, 2, TPC])
        xt = sb("xt", [128, 2, TPC, D])

        logit = sb("logit", [128, 2, TPC, 20])
        logit1 = sb("logit1", [128, 2, TPC, 16])
        top8 = sb("top8", [128, 2, TPC, 8])
        taken = sb("taken", [128, 2, TPC, 20])
        shifted = sb("shifted", [128, 2, TPC, 16])
        expd = sb("expd", [128, 2, TPC, 16])
        picked = sb("picked", [128, 2, TPC, 16])
        denom = sb("denom", [128, 2, TPC])
        denom1 = sb("denom1", [128, 2, TPC])
        recip = sb("recip", [128, 2, TPC])
        share = sb("share", [128, 2, TPC, 16])
        share_hl = sb("share_hl", [128, 2, TPC, 2 * E0])
        score_all = sb("score_t", [128, T], F32R)
        score_t = score_all[0:2 * E0]

        NACT = 3
        glu = sb("glu", [128, 2, CH])
        up = sb("up", [128, 2, CH])
        glu_s = sb("glu_s", [128, 2, CH])
        act = sb("act", [128, NACT, CH])
        act_hi = sb("act_hi", [128, NACT, CH], F32R)
        act_lo = sb("act_lo", [128, NACT, CH], F32R)

        xn = raw_w[:, 0:T]
        ssm_in = raw_w[:, T:T + 2 * CH]
        ssm_sum = raw_w[:, 2 * T - 2 * CH:2 * T]
        ssm_y = glu
        ssm_z = up
        gelu = glu_s
        resid = sb("resid", [128, 2, CH])
        tmp = sb("tmp", [128, 2, CH])

        w_down = sb("w_down", [D, LAT])
        w_up = sb("w_up", [LAT, 2, D])
        sel_h = sb("sel_h", [128, G4, 4, 128], F32R)
        head_rows = sb("head_rows", [128, HG])
        same_head = sb("same_head", [128, 128], F32R)
        q_decay = sb("q_decay", [128, 2, L])
        k_decay = sb("k_decay", [128, 2, KB])
        fix = sb("fix", [128, CH])
        minus_one = sb("minus_one", [1, 128])
        half_one = sb("half_one", [1, 1])
        q_stack = (w0_hi[:].rearrange("p e w d -> p (e w d)")[:, 0:G4 * L].rearrange("p (g t) -> p g t", g=G4),
                   w0_lo[:].rearrange("p e w d -> p (e w d)")[:, 0:G4 * L].rearrange("p (g t) -> p g t", g=G4))
        k_parts = [w[:].rearrange("p e w d -> p (e w d)")[:, G4 * L:(G4 + 2) * L].rearrange("p (g t) -> p g t", g=2)
                   for w in (w0_hi, w0_lo)]
        k_stack = [k_parts[g // 2][:, g % 2, :] for g in range(G4)]
        values = raw_w[:, 0:KB * H * VW].rearrange("p (k h v) -> p k h v", k=KB, h=H)
        def head_keys(b, g, j):
            flat = lambda t: t.rearrange("p e t -> p (e t)")
            return (xn_hi[:, L * b:L * (b + 1)], xn_lo[:, L * b:L * (b + 1)], score_all[:, 0:L],
                    score_all[:, L:2 * L], flat(act_hi[:, 0:2, :]), flat(act_lo[:, 0:2, :]),
                    flat(sel0_all[:])[:, 0:L], flat(sel0_all[:])[:, L:2 * L])[g % 2 * HG + j]

        probs = raw_w[:, E0 * 3 * D - NP * 2 * CH:].rearrange("p (n t) -> p n t", n=NP)
        qk_f = glu_s
        kv_f, lat_f = glu[:, 0, :], glu[0:LAT, 1, :]

        def squares(c):
            at = CH * (c % QC)
            return score_all[:, at:at + CH], score_all[:, L + at:L + at + CH]

        gen_small = sb("gen_small", [128, 3])
        head_max = sb("head_max", [128, NB, 2, QC])
        tops = sb("tops", [128, NB, 3])
        bound = sb("bound", [1, NB, 2])
        small_scores = sb("small_scores", [1, NB], mybir.dt.int32)
        minus_c = sb("minus_c", [128, NB])
        out_t = resid
        out_recip = sb("out_recip", [128, TPC, HG])

        flat = raw_w[:, E0 * 3 * D - NP * 2 * CH:]
        gen_s, gen_pt, gen_decays = flat[:, 0:L], flat[:, L:2 * L], flat[:, 2 * L:4 * L - 128]
        gen_k = act_hi[:, 0:2, :].rearrange("p a t -> p (a t)")
        gen_q = act_hi[:, 2, 0:128]
        gen_v = tmp[:].rearrange("p a t -> p (a t)")[:, 0:KB * HG * VW].rearrange("p (k h v) -> p k h v", k=KB, h=HG)
        gen_decay = up[:].rearrange("p a t -> p (a t)")
        gen_heads = tmp[:, 1, CH - HG * HD:]
        gen_unscale, gen_recip, gen_spare = gen_small[:, 0:1], gen_small[:, 1:2], gen_small[:, 2:3]

        bank = ctx.enter_context(nc.psum_tensor("bank", [128, 8, CH], F32))
        T1, T2, LG, ST = (0, 1), (2, 3), 5, 7
        Z, EW, OUT1 = 6, 3, 4
        G, U, S, O = (0, 1), (2, 3), (4, 5), (6, 7)

        names = """x_loaded0 x_loaded1 x_loaded2 x_loaded3
            squares_loaded half_scaled squares_hi_ready squares_ready w_loaded0 w_loaded1 w_loaded2 w_loaded3
            small_loaded out_stored
            ident_loaded consts_ready x_ready tok_in t1_ready stats_step stats_ready eps_step
            rstd_ready offset_ready normalized inner_scaled t2_ready xn_hi_ready xn_ready w0_hi_ready w0_lo_ready
            small_hi_ready small_ready prep_step ab_ready
            logits_ready logit_half logit_step top_step taken_step shift_ready exp_ready pick_step
             share_ready score_psum_ready score_ready
            g_ready u_ready s_ready glu_ready up_ready glu_s_ready act_ready hi_ready lo_ready
            down_done
            ssm_step y_ready gelu_ready gelu_hi_ready gelu_lo_ready proj_ready resid_ready
            z_ready z_copied ew_ready zs_ready zs_hi_ready zs_lo_ready out1_ready fin_ready out_copied
            cast_loaded prep_loaded
            qkv_ready q_decayed  kv_copied lat_ready lat_copied kv_rec_ready k_sq_ready
            k_lo_ready v_copied q_hi_ready q_lo_ready norms_ready maxes_ready tops_ready
            tops_row bound_step bound_ready sqrt_ready minus_c_ready flag_ready neg_ready
            stack_ready stack_copied stack_copied_v ao_ready ao_t_ready ao_hi_ready ao_lo_ready attn_out""".split()
        names += [f"{n}{b}" for b in range(NB) for n in
                  ("keys_masked", "first_masked", "scored", "fixed", "exped", "pv_done", "ot_copied", "ot_ready",
                   "recip_ready", "normed",
                   "gen_staged", "gen_scored", "gen_clipped", "gen_decayed", "gen_max", "gen_neg", "gen_probs",
                   "gen_t", "gen_tc", "gen_pv", "gen_recip", "gen_out", "gen_table")]
        s = {n: sem(n) for n in names}

        block = ctx.enter_context(nc.Block())

        def chunk(c):
            return slice(c * CH, (c + 1) * CH)

        def t2_bank(n, c):
            return T2[c % 2] if n < LN_FFN1A else T2[0]

        def skewed(phase, engine, ops, once={}, head=None):
            stage, order, at = STAGES[phase], ORDERS[phase][engine], ONCE.get(phase, {})
            for step in range(NC + max(stage.values())):
                for name in once:
                    if at[name] == step:
                        once[name]()
                for name in order:
                    if 0 <= step - stage[name] < NC:
                        ops[name](step - stage[name])
                if head and step in HEADS[phase]:
                    head(HEADS[phase][step])

        def attn_banks(c):
            return 4 * ((c + c // QC + 1) % 2)

        def bound_bank(b):
            return attn_banks(QC * b) + 3

        def pieces(experts, f):
            done = [0]

            def upto(n):
                experts(f, done[0], n)
                done[0] = n
            return upto

        UNITS = G4 * QC * KB * 2

        def unit(u):
            i = u // 2 % KB
            return u // (4 * KB), u // (2 * KB) % QC, i // 2 + i % 2 * (KB // 2), u % 2

        def fixes(u):
            g, qc, kb, hp = unit(u)
            return 2 * (CH // 128) * (u // (2 * KB)) + 2 * (kb % (CH // 128)) + hp + 1

        def stack_place(i, c):
            g, kind = i // 3, (i + 2) % 3
            at = slice(CH * (c % QC), CH * (c % QC + 1))
            return k_stack[g][:, at] if kind == 2 else q_stack[kind][:, g, at]

        SMALL = [(raw_r[:, 0:E0], "router_w"), (raw_r[:, E0:E0 + E1], "gate_w"),
                 (router_b[:], "router_b"), (raw_db[0:E0, :], "down_bias"), (raw_db[E0:2 * E0, :], "down_bias"),
                 (b_gate[:], "b_gate"), (b_up[:], "b_up"), (vecs[:], "vecs")]
        LATER = [(w_down[:], "w_down"), (w_up[:], "w_up"),
                 (head_rows[:], "head_rows"), (q_decay[:], "q_decay"), (k_decay[:], "k_decay"), (fix[:], "fix")]

        @block.sync
        def _(sp):
            x_rows = io["x"].rearrange("(n p) d -> p n d", p=128)
            sp.dma_start(ident[:], io["ident"]).then_inc(s["ident_loaded"], 16)
            for c in range(NC):
                sp.dma_start(x_tok[:, TPC * c:TPC * (c + 1), :], x_rows[:, TPC * c:TPC * (c + 1), :])\
                  .then_inc(s[f"x_loaded{c}"], 16)
            per = E0 // 4
            raw = raw_w[:].rearrange("p (e w d) -> p e w d", e=E0, w=3)
            for g in range(4):
                es = slice(per * g, per * (g + 1))
                sp.dma_start(raw[:, es, 0:2, :], io["gate_up"][:, es]).then_inc(s[f"w_loaded{g}"], 16)
                sp.dma_start(raw[:, es, 2, :], io["down"][:, es]).then_inc(s[f"w_loaded{g}"], 16)
            sp.dma_start(raw_s[:], io["squares"]).then_inc(s["squares_loaded"], 16)
            for dst, name in LATER:
                sp.dma_start(dst, io[name]).then_inc(s["prep_loaded"], 16)
            out_rows = io["out"].rearrange("(n p) d -> p n d", p=128)
            for c in range(NC):
                sp.wait_ge(s["out_copied"], c + 1)
                sp.dma_start(out_rows[:, TPC * c:TPC * (c + 1), :], x_tok[:, TPC * c:TPC * (c + 1), :])\
                  .then_inc(s["out_stored"], 16)
            sp.wait_ge(s["out_stored"], 16 * NC)

        @block.gpsimd
        def _(pool):
            pool.memset(half_pow[:], -0.5)
            pool.memset(minus_one[:], -1.0)
            pool.memset(half_one[:], 0.5)
            pool.memset(zero1[:], 0.0)
            pool.memset(raw_r[:, E0 + E1:], 0.0)
            pool.memset(logit[:, :, :, E0:20], SENTINEL)
            pool.memset(logit1[:, :, :, E1:16], SENTINEL)
            pool.memset(share_hl[:], 0.0)
            pool.memset(pw[:, 0:1], 1.0).then_inc(s["consts_ready"], 1)
            for dst, name in ((sel0, "sel0"), (sel1, "sel1"), (sel_h, "sel_h"),
                              (same_head, "same_head")):
                pool.dma_start(dst[:], io[name]).then_inc(s["cast_loaded"], 16)

            def norm(n, c):
                k = n * NC + c
                pool.wait_ge(s["stats_ready"], k + 1)
                if k >= 2:
                    pool.wait_ge(s["normalized"], k - 1)
                pool.tensor_scalar(var_eps[:, k % 2, :], mean_var[:, k % 2, :, 1], EPS, None, ALU.add)\
                    .then_inc(s["eps_step"], 1)
                pool.wait_ge(s["eps_step"], 2 * k + 1)
                pool.tensor_tensor(rstd[:, k % 2, :], var_eps[:, k % 2, :], half_pow[:], ALU.pow)\
                    .then_inc(s["rstd_ready"], 1)
                pool.tensor_scalar(minus_mean[:, k % 2, :], mean_var[:, k % 2, :, 0], -1.0, None, ALU.mult)\
                    .then_inc(s["eps_step"], 1)
                pool.wait_ge(s["rstd_ready"], k + 1)
                pool.wait_ge(s["eps_step"], 2 * k + 2)
                pool.tensor_tensor(offset[:, k % 2, :], minus_mean[:, k % 2, :], rstd[:, k % 2, :], ALU.mult)\
                    .then_inc(s["offset_ready"], 1)

            def ssm_lo(c):
                pool.wait_ge(s["gelu_hi_ready"], c + 1)
                if c >= 2:
                    pool.wait_ge(s["proj_ready"], c - 1)
                pool.tensor_tensor(act_lo[:, c % 2, :], gelu[:, c % 2, :], act_hi[:, c % 2, :].bitcast(F32),
                                   ALU.subtract).then_inc(s["gelu_lo_ready"], 1)

            def experts(f):
                for j in range(f * NC * E0, (f + 1) * NC * E0):
                    pool.wait_ge(s["hi_ready"], j + 1)
                    if j >= NACT:
                        pool.wait_ge(s["down_done"], j - NACT + 1)
                    pool.tensor_tensor(act_lo[:, j % NACT, :], act[:, j % NACT, :],
                                       act_hi[:, j % NACT, :].bitcast(F32), ALU.subtract)\
                        .then_inc(s["lo_ready"], 1)

            skewed("ffn0a", "pool", {"norm": lambda c: norm(LN_FFN0A, c)})
            experts(0)
            skewed("ssm", "pool", {"norm": lambda c: norm(LN_SSM, c), "gelu_lo": ssm_lo,
                                   "inner_norm": lambda c: norm(LN_INNER, c), "b_norm": lambda c: norm(LN_FFN0B, c)})
            experts(1)
            skewed("ffn1a", "pool", {"norm": lambda c: norm(LN_FFN1A, c), "b_norm": lambda c: norm(LN_ATTN, c)})
            for b in range(NB):
                for c in range(QC * b, QC * (b + 1)):
                    if c == QC * (b + 1) - 1:
                        pool.wait_ge(s["bound_ready"], b + 1)
                        pool.tensor_tensor(bound[:, b, 1:2], bound[:, b, 0:1], half_one[:], ALU.pow)\
                            .then_inc(s["sqrt_ready"], 1)
                    pool.wait_ge(s["stack_copied"], 3 * G4 // 2 * c + 1)
                    at = slice(CH * (c % QC), CH * (c % QC + 1))
                    for j in range(HG // 2):
                        pool.tensor_scalar(head_keys(b, 0, j)[:, at], k_stack[0][:, at].bitcast(F32),
                                           head_rows[:, j:j + 1], None, ALU.mult)\
                            .then_inc(s[f"keys_masked{b}"], 1)
                pool.wait_ge(s["minus_c_ready"], b + 1)
                pool.wait_ge(s["flag_ready"], b + 1)
                pool.wait_ge(s["stack_copied"], 3 * G4 // 2 * QC * (b + 1))
                pool.wait_ge(s["stack_copied_v"], 3 * G4 // 2 * QC * (b + 1))
                fast = pool.value_load(small_scores[0:1, b:b + 1], min_val=0, max_val=1)
                with pool.If(fast):
                    for g in range(1, G4):
                        if g >= 2:
                            pool.wait_ge(s[f"scored{b}"], UNITS // G4 * (g - 1))
                        for j in range(HG):
                            pool.tensor_scalar(head_keys(b, g, j), k_stack[g].bitcast(F32), head_rows[:, j:j + 1],
                                               None, ALU.mult).then_inc(s[f"keys_masked{b}"], 1)
            skewed("ffn1b", "pool", {"norm": lambda c: norm(LN_FFN1B, c)})

        @block.scalar
        def _(eng):
            for dst, name in SMALL:
                eng.dma_start(dst, io[name]).then_inc(s["small_loaded"], 16)

            def split_small():
                eng.wait_ge(s["small_loaded"], 16 * len(SMALL))
                eng.wait_ge(s["consts_ready"], 1)
                eng.activation(r_split[:, :, 0, :], raw_r[:].rearrange("p (r e) -> p r e", r=2), ACT.Copy)\
                   .then_inc(s["small_hi_ready"], 1)
                eng.activation(db_hi[:], raw_db[:], ACT.Copy).then_inc(s["small_hi_ready"], 1)
                eng.activation(ab[:, 0:1], vecs[:, 0:1], ACT.Exp, scale=-1.0).then_inc(s["small_hi_ready"], 1)

            def split_squares():
                eng.wait_ge(s["squares_loaded"], 16)
                eng.activation(raw_s[:, 1, :], raw_s[:, 1, :], ACT.Copy, scale=0.5).then_inc(s["half_scaled"], 1)
                eng.wait_ge(s["half_scaled"], 1)
                eng.activation(sq_hi[:], raw_s[:], ACT.Copy).then_inc(s["squares_hi_ready"], 1)

            def split_experts(g):
                raw = raw_w[:].rearrange("p (e w d) -> p e w d", e=E0, w=3)
                es = slice(E0 // 4 * g, E0 // 4 * (g + 1))
                eng.wait_ge(s[f"w_loaded{g}"], 32)
                eng.activation(w0_hi[:, es], raw[:, es], ACT.Copy).then_inc(s["w0_hi_ready"], 1)

            def norm_rows(n, c):
                k = n * NC + c
                b = k % 2
                tiles = (x_tok[:, TPC * c:TPC * (c + 1), :] if n == LN_FFN0A else
                         bank[:, T1[b], :].rearrange("p (t d) -> p t d", d=D))
                eng.wait_ge(s["offset_ready"], k + 1)
                if k >= 2:
                    eng.wait_ge(s["t2_ready"], k - 1)
                for t in range(TPC):
                    last = eng.activation(xt[:, b, t, :], tiles[:, t, :], ACT.Identity,
                                          bias=offset[:, b, t:t + 1], scale=rstd[:, b, t:t + 1])
                last.then_inc(s["normalized"], 1)

            def norm_hi(n, c):
                k = n * NC + c
                eng.wait_ge(s["t2_ready"], k + 1)
                dst = xn[:, chunk(c)] if n == LN_SSM else xn_hi[:, chunk(c)]
                eng.activation(dst, bank[:, t2_bank(n, c), :], ACT.Copy).then_inc(s["xn_hi_ready"], 1)

            def inner_scale(c):
                eng.wait_ge(s["t2_ready"], nth(LN_INNER, c))
                if c >= 2:
                    eng.wait_ge(s["x_ready"], nth(X_SSM, c - 2))
                eng.activation(tmp[:, c % 2, :], bank[:, t2_bank(LN_INNER, c), :], ACT.Identity,
                               bias=vecs[:, 6:7], scale=vecs[:, 5:6]).then_inc(s["inner_scaled"], 1)

            def router_exp(r, c):
                kr = r * NC + c
                eng.wait_ge(s["shift_ready"], kr + 1)
                ne = E0 if r < 2 else E1
                eng.activation(expd[:, kr % 2, :, 0:ne], shifted[:, kr % 2, :, 0:ne], ACT.Exp)\
                   .then_inc(s["exp_ready"], 1)

            def router_out(r, c):
                kr = r * NC + c
                nr = 2 * E0 if r < 2 else 2 * TRUE1
                eng.wait_ge(s["score_psum_ready"], kr + 1)
                eng.activation(score_t[0:nr, chunk(c)], bank[0:nr, ST, :], ACT.Copy)\
                   .then_inc(s["score_ready"], 1)

            def experts(f, done=0, upto=NC * E0 + 1):
                first, last = f * NC * E0, (f + 1) * NC * E0
                for j in range(first + done, first + upto):
                    if j < last:
                        e = j % E0
                        eng.wait_ge(s["g_ready"], j + 1)
                        if j >= 2:
                            eng.wait_ge(s["glu_s_ready"], j - 1)
                        eng.activation(glu[:, j % 2, :], bank[:, G[j % 2], :], ACT.Gelu_apprx_sigmoid,
                                       bias=b_gate[:, e:e + 1]).then_inc(s["glu_ready"], 1)
                    if j > first:
                        i = j - 1
                        eng.wait_ge(s["act_ready"], i + 1)
                        if i >= NACT:
                            eng.wait_ge(s["down_done"], i - NACT + 1)
                        eng.activation(act_hi[:, i % NACT, :], act[:, i % NACT, :], ACT.Copy)\
                           .then_inc(s["hi_ready"], 1)

            def ssm_gelu(c):
                eng.wait_ge(s["y_ready"], c + 1)
                if c >= 2:
                    eng.wait_ge(s["gelu_lo_ready"], c - 1)
                eng.activation(gelu[:, c % 2, :], ssm_z[:, c % 2, :], ACT.Gelu).then_inc(s["gelu_ready"], 1)
                eng.wait_ge(s["gelu_ready"], c + 1)
                if c >= 2:
                    eng.wait_ge(s["proj_ready"], c - 1)
                eng.activation(act_hi[:, c % 2, :], gelu[:, c % 2, :], ACT.Copy).then_inc(s["gelu_hi_ready"], 1)

            def lora_z(r, c):
                k = (r - 2) * NC + c
                eng.wait_ge(s["z_ready"], k + 1)
                if k >= 2:
                    eng.wait_ge(s["zs_ready"], k - 1)
                eng.activation(glu[:, k % 2, :], bank[:, Z, :], ACT.Copy).then_inc(s["z_copied"], 1)

            def lora_hi(r, c):
                k = (r - 2) * NC + c
                eng.wait_ge(s["zs_ready"], k + 1)
                if k >= 2:
                    eng.wait_ge(s["out1_ready"], k - 1)
                eng.activation(act_hi[:, k % 2, :], act[:, k % 2, :], ACT.Copy).then_inc(s["zs_hi_ready"], 1)

            def attn_first(c):
                o = attn_banks(c)
                eng.wait_ge(s["qkv_ready"], c + 1)
                eng.activation(kv_f, bank[:, o + 1, :], ACT.Copy).then_inc(s["kv_copied"], 1)
                if c >= 1:
                    eng.wait_ge(s["norms_ready"], c)
                eng.wait_ge(s["q_decayed"], 2 * c + 2)
                eng.activation(squares(c)[0], bank[:, o, :], ACT.Square, scale=SCALE)

            def attn_second(c):
                o = attn_banks(c)
                eng.wait_ge(s["lat_ready"], c + 1)
                eng.activation(lat_f, bank[0:LAT, o + 2, :], ACT.Copy).then_inc(s["lat_copied"], 1)
                if c >= 1:
                    eng.wait_ge(s["stack_ready"], 3 * G4 * c)
                for i in range(2):
                    eng.wait_ge(s["q_decayed"], 2 * c + i + 1)
                    eng.activation(act_hi[:, i, :], qk_f[:, i, :], ACT.Copy).then_inc(s["q_hi_ready"], 1)
                eng.wait_ge(s["kv_rec_ready"], c + 1)
                eng.activation(act_hi[:, 2, :], bank[:, o + 3, :], ACT.Copy)
                eng.activation(squares(c)[1], bank[:, o + 3, :], ACT.Square).then_inc(s["k_sq_ready"], 1)
                eng.activation(values[:, TPC * (c % QC):TPC * (c % QC + 1), :, 0:HD],
                               bank[:, o + 1, :].rearrange("p (t h d) -> p t h d", t=TPC, h=H), ACT.Copy)\
                   .then_inc(s["v_copied"], 1)

            def attn_stacks(c):
                for i in range(0, 3 * G4, 2):
                    n = c * 3 * G4 + i
                    eng.wait_ge(s["stack_ready"], n + 1)
                    eng.activation(stack_place(i, c), bank[:, attn_banks(c) + i % 4, :], ACT.Copy)\
                       .then_inc(s["stack_copied"], 1)

            def attn_fast(b):
                for u in range(UNITS):
                    g, qc, kb, hp = unit(u)
                    if kb // (CH // 128) == qc:
                        eng.wait_ge(s[f"fixed{b}"], fixes(u))
                    else:
                        eng.wait_ge(s[f"scored{b}"], u + 1)
                    if u >= NP:
                        eng.wait_ge(s[f"pv_done{b}"], (u - NP) // 2 + 1)
                    side = 1 if kb // (CH // 128) > qc else 0
                    pair = bank[:, 2 * (u % 3):2 * (u % 3) + 2, :].rearrange("p a q -> p (a q)")
                    eng.activation(probs[:, u % NP, :], pair, ACT.Exp, bias=minus_c[:, b:b + 1],
                                   scale=k_decay[:, side, kb:kb + 1]).then_inc(s[f"exped{b}"], 1)

            def attn_heads(b):
                for c in range(QC * b, QC * (b + 1)):
                    eng.wait_ge(s["ao_t_ready"], c + 1)
                    eng.activation(xn_hi[:, chunk(c)], bank[:, 4 + c % 2, :], ACT.Copy).then_inc(s["ao_hi_ready"], 1)

            def attention():
                for b in range(NB):
                    for c in range(QC * b, QC * (b + 1)):
                        if c + 1 < QC * (b + 1):
                            attn_first(c + 1)
                        attn_stacks(c)
                        if c + 1 < QC * (b + 1):
                            attn_second(c + 1)
                    eng.wait_ge(s["neg_ready"], b + 1)
                    eng.activation(minus_c[:, b:b + 1], bank[:, bound_bank(b), 0:1], ACT.Copy)\
                       .then_inc(s["minus_c_ready"], 1)
                    eng.wait_ge(s["minus_c_ready"], b + 1)
                    eng.wait_ge(s["flag_ready"], b + 1)
                    fast = eng.value_load(small_scores[0:1, b:b + 1], min_val=0, max_val=1)
                    with eng.If(fast):
                        attn_fast(b)
                    with eng.Else():
                        attn_general(b)
                    if b + 1 < NB:
                        attn_first(QC * (b + 1))
                    attn_heads(b)
                    if b + 1 < NB:
                        attn_second(QC * (b + 1))

            def attn_general(b):
                eng.dma_start(gen_decays, io["decay"]).then_inc(s[f"gen_table{b}"], 16)
                with eng.Fori(0, G4 * KB) as block_of_queries:
                    for j in range(HG):
                        n = block_of_queries * HG + j
                        eng.wait_ge(s[f"gen_neg{b}"], n + 1)
                        eng.activation(gen_s, gen_s, ACT.Exp, bias=tops[:, b, 1:2],
                                       accum_out=tops[:, b, 2:3]).then_inc(s[f"gen_probs{b}"], 1)
                        eng.wait_ge(s[f"gen_t{b}"], n + 1)
                        eng.activation(gen_pt, bank[:, 2:4, :].rearrange("p a q -> p (a q)"), ACT.Copy)\
                           .then_inc(s[f"gen_tc{b}"], 1)

            def routed_norm(n, r):
                return {"rows": lambda c: norm_rows(n, c), "hi": lambda c: norm_hi(n, c),
                        "exp": lambda c: router_exp(r, c), "out": lambda c: router_out(r, c)}

            def lora(n, r):
                return {**routed_norm(n, r), "z_copy": lambda c: lora_z(r, c), "zs_hi": lambda c: lora_hi(r, c)}

            def out_copy(c):
                eng.wait_ge(s["fin_ready"], c + 1)
                eng.activation(x_tok[:, TPC * c:TPC * (c + 1), :],
                               bank[:, T1[c % 2], :].rearrange("p (t d) -> p t d", d=D), ACT.Copy)\
                   .then_inc(s["out_copied"], 1)

            skewed("ffn0a", "act", {**routed_norm(LN_FFN0A, 0), "split": split_experts},
                   {"split_small": split_small, "split_squares": split_squares}, head=pieces(experts, 0))
            experts(0, max(HEADS["ffn0a"].values()))
            skewed("ssm", "act", {**routed_norm(LN_FFN0B, 1), "rows": lambda c: norm_rows(LN_SSM, c),
                                  "copy": lambda c: norm_hi(LN_SSM, c), "gelu": ssm_gelu,
                                  "inner_rows": lambda c: norm_rows(LN_INNER, c), "scale": inner_scale,
                                  "b_rows": lambda c: norm_rows(LN_FFN0B, c)},
                   head=pieces(experts, 1))
            experts(1, max(HEADS["ssm"].values()))
            skewed("ffn1a", "act", {**lora(LN_FFN1A, 2), "b_rows": lambda c: norm_rows(LN_ATTN, c),
                                    "b_hi": lambda c: norm_hi(LN_ATTN, c)},
                   {"first": lambda: attn_first(0), "second": lambda: attn_second(0)})
            attention()
            skewed("ffn1b", "act", {**lora(LN_FFN1B, 3), "copy": out_copy})

        @block.vector
        def _(eng):
            def take_in(c):
                eng.wait_ge(s["tok_in"], c + 1)
                eng.tensor_copy(x[:, chunk(c)], bank[:, O[c % 2], :]).then_inc(s["x_ready"], 1)

            def norm_stats(n, c):
                k = n * NC + c
                b = k % 2
                if n == LN_FFN0A:
                    eng.wait_ge(s[f"x_loaded{c}"], 16)
                    if c >= 2:
                        eng.wait_ge(s["normalized"], k - 1)
                    tiles = x_tok[:, TPC * c:TPC * (c + 1), :]
                else:
                    eng.wait_ge(s["t1_ready"], k + 1 - NC)
                    tiles = bank[:, T1[b], :].rearrange("p (t d) -> p t d", d=D)
                for t in range(TPC):
                    last = eng.bn_stats(stats[:, b, t, :], tiles[:, t, :])
                last.then_inc(s["stats_step"], 1)
                eng.wait_ge(s["stats_step"], k + 1)
                for t in range(TPC):
                    last = eng.bn_aggr(mean_var[:, b, t, :], stats[:, b, t, :])
                last.then_inc(s["stats_ready"], 1)

            def norm_lo(n, c):
                k = n * NC + c
                eng.wait_ge(s["xn_hi_ready"], nth_hi(n, c))
                eng.tensor_tensor(xn_lo[:, chunk(c)], bank[:, t2_bank(n, c), :],
                                  xn_hi[:, chunk(c)].bitcast(F32), ALU.subtract).then_inc(s["xn_ready"], 1)

            def router_pick(r, c):
                kr, b = r * NC + c, (r * NC + c) % 2
                moe = r < 2
                ne, sent = (E0, 8 - TOP0) if moe else (E1, 8 - TOP1)
                lg = logit if moe else logit1
                width = ne + sent
                eng.wait_ge(s["logits_ready"], kr + 1)
                by_hi, by_lo = [bank[:, LG, 0:TPC * 32].rearrange("p (t i e) -> p t i e", i=2, e=16)[:, :, i, 0:ne]
                                for i in range(2)]
                if moe:
                    eng.tensor_tensor(lg[:, b, :, 0:ne], by_lo, router_b[:, None, :].to_broadcast([128, TPC, E0]),
                                      ALU.add).then_inc(s["logit_half"], 1)
                else:
                    eng.tensor_copy(lg[:, b, :, 0:ne], by_lo).then_inc(s["logit_half"], 1)
                eng.wait_ge(s["logit_half"], kr + 1)
                eng.tensor_tensor(lg[:, b, :, 0:ne], lg[:, b, :, 0:ne], by_hi, ALU.add)\
                    .then_inc(s["logit_step"], 1)
                eng.wait_ge(s["logit_step"], kr + 1)
                for t in range(TPC):
                    last = eng.max(top8[:, b, t, :], lg[:, b, t, :])
                last.then_inc(s["top_step"], 1)
                eng.wait_ge(s["top_step"], kr + 1)
                for t in range(TPC):
                    last = eng.match_replace(out=taken[:, b, t, 0:width], in_to_replace=top8[:, b, t, :],
                                      in_values=lg[:, b, t, :], imm_value=TAKEN)
                last.then_inc(s["taken_step"], 1)
                eng.tensor_tensor(shifted[:, b, :, 0:ne], lg[:, b, :, 0:ne],
                                  top8[:, b, :, sent:sent + 1].to_broadcast([128, TPC, ne]), ALU.subtract)\
                    .then_inc(s["shift_ready"], 1)

            def router_share(r, c):
                kr, b = r * NC + c, (r * NC + c) % 2
                moe = r < 2
                ne = E0 if moe else TRUE1
                eng.wait_ge(s["exp_ready"], kr + 1)
                eng.wait_ge(s["taken_step"], kr + 1)
                step = 4 * min(kr, 2 * NC) + 5 * max(kr - 2 * NC, 0)

                def then(ins):
                    nonlocal step
                    step += 1
                    ins.then_inc(s["pick_step"], 1)
                    eng.wait_ge(s["pick_step"], step)

                then(eng.scalar_tensor_tensor(out=picked[:, b, :, 0:ne], in0=taken[:, b, :, 0:ne], scalar=TAKEN,
                                              in1=expd[:, b, :, 0:ne], op0=ALU.is_equal, op1=ALU.mult))
                then(eng.tensor_reduce(denom[:, b, :], picked[:, b, :, 0:ne], axis=AX.X, op=ALU.add))
                total = denom
                if not moe:
                    total = denom1
                    then(eng.scalar_tensor_tensor(out=denom1[:, b, :], in0=denom[:, b, :], scalar=0.0,
                                                  in1=denom[:, b, :], op0=ALU.is_equal, op1=ALU.add))
                then(eng.reciprocal(recip[:, b, :], total[:, b, :]))
                if kr >= 2:
                    eng.wait_ge(s["score_psum_ready"], kr - 1)
                for dst in (share[:, b, :, 0:ne], share_hl[:, b, :, 0:ne].bitcast(F32R)):
                    ins = eng.scalar_tensor_tensor(out=dst, in0=picked[:, b, :, 0:ne],
                                                   scalar=0.5 if moe else 1.0,
                                                   in1=recip[:, b, :, None].to_broadcast([128, TPC, ne]),
                                                   op0=ALU.mult, op1=ALU.mult)
                then(ins)
                eng.tensor_tensor(share_hl[:, b, :, ne:2 * ne].bitcast(F32R), share[:, b, :, 0:ne],
                                  share_hl[:, b, :, 0:ne], ALU.subtract).then_inc(s["share_ready"], 1)

            def split_small():
                eng.wait_ge(s["small_hi_ready"], 3)
                eng.tensor_tensor(r_split[:, :, 1, :], raw_r[:].rearrange("p (r e) -> p r e", r=2),
                                  r_split[:, :, 0, :].bitcast(F32), ALU.subtract)
                eng.tensor_tensor(db_lo[:], raw_db[:], db_hi[:].bitcast(F32), ALU.subtract)
                eng.tensor_scalar(b_up1[:], b_up[:], 1.0, None, ALU.add).then_inc(s["small_ready"], 1)

            def split_squares():
                eng.wait_ge(s["squares_hi_ready"], 1)
                eng.tensor_tensor(sq_lo[:], raw_s[:], sq_hi[:].bitcast(F32), ALU.subtract)\
                    .then_inc(s["squares_ready"], 1)

            def ssm_powers():
                step = 0

                def then(ins):
                    nonlocal step
                    step += 1
                    ins.then_inc(s["prep_step"], 1)
                    eng.wait_ge(s["prep_step"], step)

                then(eng.tensor_scalar(ab[:, 1:2], ab[:, 0:1], 1.0, None, ALU.add))
                then(eng.reciprocal(ab[:, 2:3], ab[:, 1:2]))
                then(eng.tensor_tensor(ab[:, 3:4], vecs[:, 2:3], vecs[:, 1:2], ALU.mult))
                then(eng.tensor_scalar(ab[:, 4:5], vecs[:, 7:8], 0.5, None, ALU.mult))
                eng.tensor_tensor_scan(pw[:, 1:L], ab[:, 2:3].to_broadcast([128, L - 1]),
                                       zero1[:, 0:1].to_broadcast([128, L - 1]), 1.0, ALU.mult, ALU.add)\
                    .then_inc(s["ab_ready"], 1)

            def split_experts(g):
                raw = raw_w[:].rearrange("p (e w d) -> p e w d", e=E0, w=3)
                es = slice(E0 // 4 * g, E0 // 4 * (g + 1))
                eng.wait_ge(s["w0_hi_ready"], g + 1)
                eng.tensor_tensor(w0_lo[:, es], raw[:, es], w0_hi[:, es].bitcast(F32), ALU.subtract)\
                    .then_inc(s["w0_lo_ready"], 1)

            def experts(f, done=0, upto=NC * E0):
                for j in range(f * NC * E0 + done, f * NC * E0 + upto):
                    e, c = j % E0, j // E0 % NC
                    eng.wait_ge(s["u_ready"], j + 1)
                    eng.tensor_scalar(up[:, j % 2, :], bank[:, U[j % 2], :], b_up1[:, e:e + 1], 1.0 - LIMIT,
                                      ALU.add, ALU.max).then_inc(s["up_ready"], 1)
                    eng.wait_ge(s["glu_ready"], j + 1)
                    eng.wait_ge(s["s_ready"], j + 1)
                    eng.scalar_tensor_tensor(out=glu_s[:, j % 2, :], in0=glu[:, j % 2, :], scalar=GLU_AT_LIMIT,
                                             in1=bank[:, S[j % 2], :], op0=ALU.min, op1=ALU.mult)\
                        .then_inc(s["glu_s_ready"], 1)
                    eng.wait_ge(s["glu_s_ready"], j + 1)
                    if j >= NACT:
                        eng.wait_ge(s["lo_ready"], j - NACT + 1)
                    eng.scalar_tensor_tensor(out=act[:, j % NACT, :], in0=up[:, j % 2, :], scalar=1.0 + LIMIT,
                                             in1=glu_s[:, j % 2, :], op0=ALU.min, op1=ALU.mult)\
                        .then_inc(s["act_ready"], 1)
                    if e == 2 and c > 0:
                        add_out(f, c - 1)
                if upto == NC * E0:
                    add_out(f, NC - 1)

            def add_out(f, c):
                eng.wait_ge(s["down_done"], E0 * nth(f, c))
                eng.tensor_tensor(x[:, chunk(c)], bank[:, O[c % 2], :], x[:, chunk(c)], ALU.add)\
                    .then_inc(s["x_ready"], 1)

            def ssm_scan(c):
                n = LN_SSM
                at = c * CH % L
                b = c % 2
                step = 2 * c
                eng.wait_ge(s["xn_hi_ready"], nth_hi(LN_SSM, c))
                eng.wait_ge(s["ab_ready"], 1)
                eng.tensor_tensor(ssm_in[:, b * CH:(b + 1) * CH], bank[:, t2_bank(n, c), :], pw[:, at:at + CH],
                                  ALU.mult).then_inc(s["xn_ready"], 1)
                eng.wait_ge(s["xn_ready"], nth_hi(n, c))
                first = 0.0 if at == 0 else ssm_sum[:, (1 - b) * CH + CH - 1:(1 - b) * CH + CH]
                eng.tensor_tensor_scan(ssm_sum[:, b * CH:(b + 1) * CH], ssm_in[:, b * CH:(b + 1) * CH],
                                       zero1[:, 0:1].to_broadcast([128, CH]), first, ALU.add, ALU.add)\
                    .then_inc(s["ssm_step"], 1)
                eng.wait_ge(s["ssm_step"], step + 1)
                hi = L - 1 - at
                back = pw[:, hi - CH + 1:hi + 1][:, ::-1]
                eng.scalar_tensor_tensor(out=ssm_y[:, b, :], in0=ssm_sum[:, b * CH:(b + 1) * CH],
                                         scalar=ab[:, 3:4], in1=back, op0=ALU.mult, op1=ALU.mult)\
                    .then_inc(s["ssm_step"], 1)
                eng.wait_ge(s["ssm_step"], step + 2)
                if c >= 2:
                    eng.wait_ge(s["gelu_ready"], c - 1)
                eng.scalar_tensor_tensor(out=ssm_z[:, b, :], in0=xn[:, chunk(c)], scalar=vecs[:, 3:4],
                                         in1=ssm_y[:, b, :], op0=ALU.mult, op1=ALU.add).then_inc(s["y_ready"], 1)

            def ssm_resid(c):
                eng.wait_ge(s["proj_ready"], c + 1)
                k = LN_INNER * NC + c
                if c >= 2:
                    eng.wait_ge(s["t1_ready"], k - 1 - NC)
                eng.scalar_tensor_tensor(out=resid[:, c % 2, :], in0=bank[:, O[c % 2], :], scalar=vecs[:, 4:5],
                                         in1=xn[:, chunk(c)], op0=ALU.add, op1=ALU.add)\
                    .then_inc(s["resid_ready"], 1)

            def ssm_out(c):
                eng.wait_ge(s["inner_scaled"], c + 1)
                eng.tensor_tensor(x[:, chunk(c)], tmp[:, c % 2, :], x[:, chunk(c)], ALU.add)\
                    .then_inc(s["x_ready"], 1)

            def lora_scaled(r, c):
                k = (r - 2) * NC + c
                eng.wait_ge(s["z_copied"], k + 1)
                eng.wait_ge(s["ew_ready"], k + 1)
                if k >= 2:
                    eng.wait_ge(s["zs_lo_ready"], k - 1)
                eng.tensor_tensor(act[:, k % 2, :], glu[:, k % 2, :], bank[:, EW, :], ALU.mult)\
                    .then_inc(s["zs_ready"], 1)

            def lora_lo(r, c):
                k = (r - 2) * NC + c
                eng.wait_ge(s["zs_hi_ready"], k + 1)
                if k >= 2:
                    eng.wait_ge(s["out1_ready"], k - 1)
                eng.tensor_tensor(act_lo[:, k % 2, :], act[:, k % 2, :], act_hi[:, k % 2, :].bitcast(F32),
                                  ALU.subtract).then_inc(s["zs_lo_ready"], 1)

            def lora_out(r, c):
                k = (r - 2) * NC + c
                eng.wait_ge(s["out1_ready"], k + 1)
                eng.scalar_tensor_tensor(out=x[:, chunk(c)], in0=bank[:, OUT1, :], scalar=ab[:, 4:5],
                                         in1=x[:, chunk(c)], op0=ALU.add, op1=ALU.add)\
                    .then_inc(s["x_ready"], 1)

            def routed_norm(n, r):
                return {"stats": lambda c: norm_stats(n, c), "lo": lambda c: norm_lo(n, c),
                        "pick": lambda c: router_pick(r, c), "share": lambda c: router_share(r, c)}

            def lora(n, r):
                return {**routed_norm(n, r), "zs": lambda c: lora_scaled(r, c), "zs_lo": lambda c: lora_lo(r, c),
                        "add": lambda c: lora_out(r, c)}

            def attn_first(c):
                o = attn_banks(c)
                eng.wait_ge(s["qkv_ready"], c + 1)
                if c == 0:
                    eng.wait_ge(s["prep_loaded"], 16 * len(LATER))
                else:
                    eng.wait_ge(s["q_lo_ready"], 2 * c)
                at = slice(c % QC * CH, (c % QC + 1) * CH)
                for i in range(2):
                    eng.tensor_tensor(qk_f[:, i, :], bank[:, o, :], q_decay[:, i, at], ALU.mult)\
                        .then_inc(s["q_decayed"], 1)

            def attn_second(c):
                o = attn_banks(c)
                for i in range(2):
                    eng.wait_ge(s["q_hi_ready"], 2 * c + i + 1)
                    eng.tensor_tensor(act_lo[:, i, :], qk_f[:, i, :], act_hi[:, i, :].bitcast(F32), ALU.subtract)\
                        .then_inc(s["q_lo_ready"], 1)
                eng.wait_ge(s["k_sq_ready"], c + 1)
                eng.tensor_tensor(act_lo[:, 2, :], bank[:, o + 3, :], act_hi[:, 2, :].bitcast(F32), ALU.subtract)\
                    .then_inc(s["k_lo_ready"], 1)
                b = c // QC
                eng.wait_ge(s["norms_ready"], c + 1)
                eng.reduce_max(head_max[:, b, 0, c % QC:c % QC + 1], bank[:, o, :], axis=AX.X)
                eng.reduce_max(head_max[:, b, 1, c % QC:c % QC + 1], bank[:, o + 2, :], axis=AX.X)\
                    .then_inc(s["maxes_ready"], 1)

            def attn_stacks(c):
                for i in range(1, 3 * G4, 2):
                    n = c * 3 * G4 + i
                    eng.wait_ge(s["stack_ready"], n + 1)
                    eng.tensor_copy(stack_place(i, c), bank[:, attn_banks(c) + i % 4, :])\
                        .then_inc(s["stack_copied_v"], 1)
                    if i == 5:
                        b, at = c // QC, slice(CH * (c % QC), CH * (c % QC + 1))
                        eng.wait_ge(s["stack_copied"], 3 * G4 // 2 * c + 1)
                        for j in range(HG // 2, HG):
                            eng.tensor_scalar(head_keys(b, 0, j)[:, at], k_stack[0][:, at].bitcast(F32),
                                              head_rows[:, j:j + 1], None, ALU.mult)\
                                .then_inc(s[f"first_masked{b}"], 1)

            def attn_bound(b):
                eng.wait_ge(s["maxes_ready"], QC * (b + 1))
                eng.tensor_reduce(tops[:, b, 0:2], head_max[:, b], axis=AX.X, op=ALU.max)\
                    .then_inc(s["bound_step"], 1)
                eng.wait_ge(s["bound_step"], b + 1)
                eng.tensor_tensor(tops[:, b, 2:3], tops[:, b, 0:1], tops[:, b, 1:2], ALU.mult)\
                    .then_inc(s["tops_ready"], 1)
                eng.wait_ge(s["tops_row"], b + 1)
                eng.reduce_max(bound[:, b, 0:1], bank[0:1, bound_bank(b), 0:128], axis=AX.X)\
                    .then_inc(s["bound_ready"], 1)
                eng.wait_ge(s["bound_ready"], b + 1)
                eng.tensor_scalar(small_scores[:, b:b + 1], bound[:, b, 0:1], SAFE_BOUND ** 2, None, ALU.is_le)\
                    .then_inc(s["flag_ready"], 1)
                eng.wait_ge(s["flag_ready"], b + 1)

            def attn_fast(b):
                def take_out(n):
                    g, qc = n // QC, n % QC
                    o = 6 + n % 2
                    eng.wait_ge(s[f"pv_done{b}"], KB * (n + 1))
                    if n >= 2:
                        eng.wait_ge(s[f"ot_ready{b}"], n - 1)
                    eng.tensor_copy(out_t[:, n % 2, :], bank[:, o, :]).then_inc(s[f"ot_copied{b}"], 1)

                def normalize(n):
                    g, qc = n // QC, n % QC
                    rows = bank[:, 6 + n % 2, :].rearrange("p (t j m) -> p t j m", t=TPC, j=HG)
                    eng.wait_ge(s[f"ot_ready{b}"], n + 1)
                    eng.reciprocal(out_recip[:], rows[:, :, :, HD]).then_inc(s[f"recip_ready{b}"], 1)
                    eng.wait_ge(s[f"recip_ready{b}"], n + 1)
                    at = KB * b + TPC * qc
                    place = x_tok[:, at:at + TPC, HG * HD * g:HG * HD * (g + 1)]
                    ins = eng.tensor_tensor(place.rearrange("p t (j d) -> p t j d", j=HG), rows[:, :, :, 0:HD],
                                            out_recip[:, :, :, None].to_broadcast([128, TPC, HG, HD]), ALU.mult)
                    ins.then_inc(s[f"normed{b}"], 1)

                for u in range(UNITS):
                    g, qc, kb, hp = unit(u)
                    if kb // (CH // 128) == qc:
                        i = kb % (CH // 128)
                        w = 128 * (i + 1)
                        turned = fix[:, None, CH - w:CH].to_broadcast([128, 2, w])
                        pair = bank[:, 2 * (u % 3):2 * (u % 3) + 2, 0:w]
                        eng.wait_ge(s[f"scored{b}"], u + 1)
                        eng.tensor_tensor(pair, pair, turned, ALU.mult)\
                            .then_inc(s[f"fixed{b}"], 1)
                    n = u // (2 * KB)
                    if u % (2 * KB) == 4 and n > 0:
                        take_out(n - 1)
                    if u % (2 * KB) == 8 and n > 0:
                        normalize(n - 1)
                take_out(G4 * QC - 1)
                normalize(G4 * QC - 1)

            def attn_general(b):
                eng.wait_ge(s[f"gen_table{b}"], 16)
                for half in range(2):
                    with eng.Fori(0, 2) as gl:
                        with eng.Fori(0, KB) as qb:
                            eng.tensor_copy(gen_k, k_parts[half][:, bass.ds(gl, 1), :].bitcast(F32)
                                            .rearrange("p a t -> p (a t)"))
                            eng.tensor_copy(gen_q, q_stack[0][:, bass.ds(2 * half + gl, 1), bass.ds(128 * qb, 128)]
                                            .bitcast(F32).rearrange("p a t -> p (a t)"))
                            eng.tensor_copy(gen_unscale, k_decay[:, 0, bass.ds(qb, 1)])
                            eng.tensor_copy(gen_decay, gen_decays[:, bass.ds(L - 128 - 128 * qb, L)])
                            eng.tensor_copy(gen_v, values[:, :, bass.ds(HG * (2 * half + gl), HG), :])\
                                .then_inc(s[f"gen_staged{b}"], 1)
                            for j in range(HG):
                                n = (2 * half * KB + gl * KB + qb) * HG + j
                                eng.wait_ge(s[f"gen_scored{b}"], n + 1)
                                eng.tensor_scalar(gen_s, bank[:, 0:2, :].rearrange("p a q -> p (a q)"), gen_unscale,
                                                  -CLAMP, ALU.mult, ALU.max).then_inc(s[f"gen_clipped{b}"], 1)
                                eng.wait_ge(s[f"gen_clipped{b}"], n + 1)
                                eng.scalar_tensor_tensor(out=gen_s, in0=gen_s, scalar=CLAMP,
                                                         in1=gen_decay,
                                                         op0=ALU.min, op1=ALU.mult).then_inc(s[f"gen_decayed{b}"], 1)
                                eng.wait_ge(s[f"gen_decayed{b}"], n + 1)
                                eng.reduce_max(tops[:, b, 0:1], gen_s, axis=AX.X).then_inc(s[f"gen_max{b}"], 1)
                                eng.wait_ge(s[f"gen_max{b}"], n + 1)
                                eng.tensor_scalar(tops[:, b, 1:2], tops[:, b, 0:1], -1.0, None, ALU.mult)\
                                    .then_inc(s[f"gen_neg{b}"], 1)
                                eng.wait_ge(s[f"gen_pv{b}"], n + 1)
                                eng.reciprocal(gen_recip, tops[:, b, 2:3]).then_inc(s[f"gen_recip{b}"], 1)
                                eng.wait_ge(s[f"gen_recip{b}"], n + 1)
                                eng.tensor_scalar(gen_heads[:, HD * j:HD * (j + 1)], bank[:, 4, 0:HD], gen_recip,
                                                  None, ALU.mult).then_inc(s[f"gen_out{b}"], 1)
                            eng.wait_ge(s[f"gen_out{b}"], (2 * half * KB + gl * KB + qb + 1) * HG)
                            eng.tensor_copy(gen_spare, gen_recip)
                            eng.tensor_copy(x_tok[:, bass.ds(KB * b + qb, 1), bass.ds(HG * HD * (2 * half + gl), HG * HD)]
                                            .rearrange("p a d -> p (a d)"), gen_heads)

            def attn_heads(b):
                for c in range(QC * b, QC * (b + 1)):
                    eng.wait_ge(s["ao_hi_ready"], c + 1)
                    eng.tensor_tensor(xn_lo[:, chunk(c)], bank[:, 4 + c % 2, :], xn_hi[:, chunk(c)].bitcast(F32),
                                      ALU.subtract).then_inc(s["ao_lo_ready"], 1)

            def attn_out(b):
                for c in range(QC * b, QC * (b + 1)):
                    eng.wait_ge(s["attn_out"], c + 1)
                    eng.tensor_tensor(x[:, chunk(c)], bank[:, 6 + c % 2, :], x[:, chunk(c)], ALU.add)\
                        .then_inc(s["x_ready"], 1)

            def attention():
                eng.memset(values[:, :, :, HD:VW], 1.0)
                for b in range(NB):
                    for c in range(QC * b, QC * (b + 1)):
                        if c + 1 < QC * (b + 1):
                            attn_first(c + 1)
                        else:
                            attn_bound(b)
                        attn_stacks(c)
                        if c + 1 < QC * (b + 1):
                            attn_second(c + 1)
                    fast = eng.value_load(small_scores[0:1, b:b + 1], min_val=0, max_val=1)
                    with eng.If(fast):
                        attn_fast(b)
                    with eng.Else():
                        attn_general(b)
                    eng.memset(tops[:, b, 0:1], 0.0).then_inc(s["ao_ready"], 1)
                    if b + 1 < NB:
                        attn_first(QC * (b + 1))
                    attn_heads(b)
                    if b + 1 < NB:
                        attn_second(QC * (b + 1))
                for b in range(NB):
                    attn_out(b)

            def take_in_and_stats(c):
                norm_stats(LN_FFN0A, c)
                take_in(c)

            eng.wait_ge(s["consts_ready"], 1)
            skewed("ffn0a", "dve", {**routed_norm(LN_FFN0A, 0), "stats": take_in_and_stats, "split": split_experts},
                   {"split_small": split_small, "powers": ssm_powers, "split_squares": split_squares},
                   head=pieces(experts, 0))
            experts(0, max(HEADS["ffn0a"].values()))
            skewed("ssm", "dve", {**routed_norm(LN_FFN0B, 1), "stats": lambda c: norm_stats(LN_SSM, c),
                                  "scan": ssm_scan, "resid": ssm_resid, "add": ssm_out,
                                  "inner_stats": lambda c: norm_stats(LN_INNER, c),
                                  "b_stats": lambda c: norm_stats(LN_FFN0B, c)},
                   head=pieces(experts, 1))
            experts(1, max(HEADS["ssm"].values()))
            skewed("ffn1a", "dve", {**lora(LN_FFN1A, 2), "b_stats": lambda c: norm_stats(LN_ATTN, c),
                                    "b_lo": lambda c: norm_lo(LN_ATTN, c)},
                   {"first": lambda: attn_first(0), "second": lambda: attn_second(0)})
            attention()
            skewed("ffn1b", "dve", lora(LN_FFN1B, 3))

        @block.tensor
        def _(pe):
            def split_matmul(out, w_hi, w_lo, v_hi, v_lo, start, stop):
                pe.matmul(out, w_hi, v_hi, start=start, stop=False)
                pe.matmul(out, w_lo, v_hi, start=False, stop=False)
                return pe.matmul(out, w_hi, v_lo, start=False, stop=stop)

            def take_in(c):
                pe.wait_ge(s[f"x_loaded{c}"], 16)
                if c >= 2:
                    pe.wait_ge(s["x_ready"], nth(X_IN, c - 2))
                for t in range(TPC):
                    last = pe.transpose(bank[:, O[c % 2], 128 * t:128 * (t + 1)], x_tok[:, TPC * c + t, :], ident[:])
                last.then_inc(s["tok_in"], 1)

            def norm_in(n, c, version):
                k = n * NC + c
                b = k % 2
                if n == LN_INNER:
                    pe.wait_ge(s["resid_ready"], c + 1)
                else:
                    pe.wait_ge(s["x_ready"], nth(version, c))
                pe.wait_ge(s["normalized"], k - 1)
                for t in range(TPC):
                    src = (resid[:, c % 2, 128 * t:128 * (t + 1)] if n == LN_INNER else
                           x[:, c * CH + 128 * t:c * CH + 128 * (t + 1)])
                    last = pe.transpose(bank[:, T1[b], 128 * t:128 * (t + 1)], src, ident[:])
                last.then_inc(s["t1_ready"], 1)

            def norm_out(n, c):
                k = n * NC + c
                b = k % 2
                pe.wait_ge(s["normalized"], k + 1)
                last_n, last_c = divmod(k - (2 if n < LN_FFN1A else 1), NC)
                if last_n == LN_INNER:
                    pe.wait_ge(s["inner_scaled"], last_c + 1)
                elif k >= 2:
                    pe.wait_ge(s["xn_ready"], nth_hi(last_n, last_c))
                for t in range(TPC):
                    last = pe.transpose(bank[:, t2_bank(n, c), 128 * t:128 * (t + 1)], xt[:, b, t, :], ident[:])
                last.then_inc(s["t2_ready"], 1)

            def router_logits(r, n, c):
                kr = r * NC + c
                weights = r_split[:, 0 if r < 2 else 1].rearrange("p i e -> p (i e)")
                pe.wait_ge(s["xn_ready"], nth_hi(n, c))
                pe.wait_ge(s["small_ready"], 1)
                if kr >= 1:
                    pe.wait_ge(s["logit_step"], kr)
                for t in range(TPC):
                    at = slice(c * CH + 128 * t, c * CH + 128 * (t + 1))
                    out = bank[:, LG, 32 * t:32 * (t + 1)]
                    pe.matmul(out, xn_hi[:, at], weights, start=True, stop=False)
                    last = pe.matmul(out, xn_lo[:, at], weights, start=False, stop=True)
                last.then_inc(s["logits_ready"], 1)

            def router_scores(r, c):
                kr = r * NC + c
                nr = 2 * E0 if r < 2 else 2 * TRUE1
                pe.wait_ge(s["share_ready"], kr + 1)
                if kr >= 1:
                    pe.wait_ge(s["score_ready"], kr)
                for t in range(TPC):
                    last = pe.transpose(bank[0:nr, ST, 128 * t:128 * (t + 1)], share_hl[:, kr % 2, t, 0:nr], ident[:])
                last.then_inc(s["score_psum_ready"], 1)

            def experts(f, done=0, upto=NC * E0 + 2):
                def down(j):
                    e, c, slot = j % E0, j // E0 % NC, j % NACT
                    out = bank[:, O[c % 2], :]
                    if e == 0:
                        if c == 1:
                            pe.wait_ge(s["score_ready"], nth(f, NC - 1))
                        if c >= 2:
                            pe.wait_ge(s["x_ready"], nth(X_FFN0A if f == 0 else X_FFN0B, c - 2))
                        pe.matmul(out, db_hi[:], score_t[:, chunk(c)], start=True, stop=False)
                        pe.matmul(out, db_lo[:], score_t[:, chunk(c)], start=False, stop=False)
                    pe.wait_ge(s["hi_ready"], j + 1)
                    pe.matmul(out, w0_hi[:, e, 2, :], act_hi[:, slot, :], start=False, stop=False)
                    pe.matmul(out, w0_lo[:, e, 2, :], act_hi[:, slot, :], start=False, stop=False)
                    pe.wait_ge(s["lo_ready"], j + 1)
                    last = pe.matmul(out, w0_hi[:, e, 2, :], act_lo[:, slot, :], start=False, stop=e == E0 - 1)
                    last.then_inc(s["down_done"], 1)

                first, end = f * NC * E0, (f + 1) * NC * E0
                pe.wait_ge(s["cast_loaded"], 64)
                for j in range(first + done, first + upto):
                    if j < end:
                        e, c, b = j % E0, j // E0 % NC, j % 2
                        at = chunk(c)
                        if j == first:
                            pe.wait_ge(s["xn_ready"], nth_hi(LN_FFN0A if f == 0 else LN_FFN0B, NC - 1))
                        if f == 0 and c == 0 and e % 4 == 0:
                            pe.wait_ge(s["w0_lo_ready"], e // 4 + 1)
                        if j >= 2:
                            pe.wait_ge(s["glu_ready"], j - 1)
                        split_matmul(bank[:, G[b], :], w0_hi[:, e, 0, :], w0_lo[:, e, 0, :],
                                     xn_hi[:, at], xn_lo[:, at], True, True).then_inc(s["g_ready"], 1)
                        if j >= 2:
                            pe.wait_ge(s["up_ready"], j - 1)
                        split_matmul(bank[:, U[b], :], w0_hi[:, e, 1, :], w0_lo[:, e, 1, :],
                                     xn_hi[:, at], xn_lo[:, at], True, True).then_inc(s["u_ready"], 1)
                        if j >= 2:
                            pe.wait_ge(s["glu_s_ready"], j - 1)
                        if e == 0:
                            pe.wait_ge(s["score_ready"], nth(f, c))
                        if j == first + 1:
                            pe.wait_ge(s["logit_step"], nth(f, NC - 1))
                        pe.matmul(bank[:, S[b], :], sel0[:, e, :], score_t[:, at], start=True, stop=True)\
                          .then_inc(s["s_ready"], 1)
                    if j - 2 >= first:
                        down(j - 2)

            def ssm_proj(c):
                pe.wait_ge(s["squares_ready"], 1)
                pe.wait_ge(s["gelu_lo_ready"], c + 1)
                if c >= 2:
                    pe.wait_ge(s["resid_ready"], c - 1)
                split_matmul(bank[:, O[c % 2], :], sq_hi[:, 0, :], sq_lo[:, 0, :], act_hi[:, c % 2, :],
                             act_lo[:, c % 2, :], True, True).then_inc(s["proj_ready"], 1)

            def lora_front(r, c):
                k = (r - 2) * NC + c
                at = chunk(c)
                if k >= 1:
                    pe.wait_ge(s["z_copied"], k)
                split_matmul(bank[:, Z, :], sq_hi[:, 2, :], sq_lo[:, 2, :], xn_hi[:, at], xn_lo[:, at],
                             True, True).then_inc(s["z_ready"], 1)
                if k >= 1:
                    pe.wait_ge(s["zs_ready"], k)
                pe.wait_ge(s["score_ready"], nth(r, c))
                pe.matmul(bank[:, EW, :], sel1[:], score_t[0:2 * TRUE1, at], start=True, stop=True)\
                  .then_inc(s["ew_ready"], 1)

            def lora_back(r, c):
                k = (r - 2) * NC + c
                at = chunk(c)
                if c >= 1:
                    pe.wait_ge(s["x_ready"], nth(X_FFN1A if r == 2 else X_FFN1B, c - 1))
                split_matmul(bank[:, OUT1, :], sq_hi[:, 1, :], sq_lo[:, 1, :], xn_hi[:, at], xn_lo[:, at],
                             True, False)
                pe.wait_ge(s["zs_lo_ready"], k + 1)
                split_matmul(bank[:, OUT1, :], sq_hi[:, 3, :], sq_lo[:, 3, :], act_hi[:, k % 2, :],
                             act_lo[:, k % 2, :], False, True).then_inc(s["out1_ready"], 1)

            def routed_norm(n, r, version):
                return {"t1": lambda c: norm_in(n, c, version), "t2": lambda c: norm_out(n, c),
                        "logits": lambda c: router_logits(r, n, c), "scores": lambda c: router_scores(r, c)}

            def lora(n, r, version):
                return {**routed_norm(n, r, version), "z": lambda c: lora_front(r, c),
                        "back": lambda c: lora_back(r, c)}

            def attn_first(c):
                o = attn_banks(c)
                at = chunk(c)
                pe.wait_ge(s["xn_ready"], nth_hi(LN_ATTN, c))
                if c == 0:
                    pe.wait_ge(s["x_ready"], nth(X_FFN1A, NC - 1))
                elif c == 1:
                    pe.wait_ge(s["xn_ready"], nth_hi(LN_ATTN, NC - 1))
                elif c == QC + 1:
                    pe.wait_ge(s["ao_lo_ready"], QC)
                split_matmul(bank[:, o, :], sq_hi[:, WQ, :], sq_lo[:, WQ, :], xn_hi[:, at], xn_lo[:, at], True, True)
                split_matmul(bank[:, o + 1, :], sq_hi[:, WK, :], sq_lo[:, WK, :], xn_hi[:, at], xn_lo[:, at],
                             True, False)
                split_matmul(bank[:, o + 1, :], sq_hi[:, WV, :], sq_lo[:, WV, :], xn_hi[:, at], xn_lo[:, at],
                             False, True).then_inc(s["qkv_ready"], 1)

            def attn_second(c):
                o = attn_banks(c)
                pe.wait_ge(s["prep_loaded"], 16 * len(LATER))
                pe.wait_ge(s["kv_copied"], c + 1)
                pe.matmul(bank[0:LAT, o + 2, :], w_down[:], kv_f, start=True, stop=True).then_inc(s["lat_ready"], 1)
                pe.wait_ge(s["lat_copied"], c + 1)
                pe.matmul(bank[:, o + 3, :], w_up[:, 0, :], lat_f, start=True, stop=True)
                for t in range(TPC):
                    last = pe.matmul(bank[:, o + 1, 128 * t:128 * (t + 1)], lat_f[:, 128 * t:128 * (t + 1)],
                                     w_up[:, 1, :], start=True, stop=True)
                last.then_inc(s["kv_rec_ready"], 1)
                pe.wait_ge(s["q_decayed"], 2 * c + 2)
                pe.wait_ge(s["k_sq_ready"], c + 1)
                pe.wait_ge(s["cast_loaded"], 64)
                pe.matmul(bank[:, o, :], same_head[:], squares(c)[0], start=True, stop=True)
                pe.matmul(bank[:, o + 2, :], same_head[:], squares(c)[1], start=True, stop=True)\
                  .then_inc(s["norms_ready"], 1)

            def attn_stacks(c):
                pe.wait_ge(s["cast_loaded"], 64)
                pe.wait_ge(s["maxes_ready"], c + 1)
                pe.wait_ge(s["k_lo_ready"], c + 1)
                pe.wait_ge(s["v_copied"], c + 1)
                for i in range(3 * G4):
                    n = c * 3 * G4 + i
                    g, kind = i // 3, (i + 2) % 3
                    if n >= 4:
                        pe.wait_ge(s["stack_copied"] if i % 2 == 0 else s["stack_copied_v"], (n - 4) // 2 + 1)
                    part = 2 if kind == 2 else 0
                    out = bank[:, attn_banks(c) + i % 4, :]
                    pe.matmul(out, sel_h[:, g, part, :], act_hi[:, kind, :], start=True, stop=False)
                    pe.matmul(out, sel_h[:, g, part + 1, :], act_lo[:, kind, :], start=False, stop=True)\
                      .then_inc(s["stack_ready"], 1)

            def attn_bound(b):
                pe.wait_ge(s["stack_copied"], 3 * G4 // 2 * (QC * (b + 1) - 1))
                pe.wait_ge(s["stack_copied_v"], 3 * G4 // 2 * (QC * (b + 1) - 1))
                pe.wait_ge(s["tops_ready"], b + 1)
                pe.transpose(bank[0:1, bound_bank(b), 0:128], tops[:, b, 2:3], ident[:]).then_inc(s["tops_row"], 1)

            def attn_spread(b):
                pe.wait_ge(s["sqrt_ready"], b + 1)
                pe.wait_ge(s["flag_ready"], b + 1)
                pe.matmul(bank[:, bound_bank(b), 0:1], minus_one[:], bound[:, b, 1:2], start=True, stop=True)\
                  .then_inc(s["neg_ready"], 1)
                pe.wait_ge(s[f"keys_masked{b}"], HG // 2 * QC)
                pe.wait_ge(s[f"first_masked{b}"], HG // 2 * QC)
                pe.wait_ge(s["stack_copied"], 3 * G4 // 2 * QC * (b + 1))
                pe.wait_ge(s["stack_copied_v"], 3 * G4 // 2 * QC * (b + 1))
                pe.wait_ge(s["minus_c_ready"], b + 1)

            def attn_fast(b):
                def scores(u):
                    g, qc, kb, hp = unit(u)
                    side = 1 if kb // (CH // 128) > qc else 0
                    if u >= 3:
                        pe.wait_ge(s[f"exped{b}"], u - 2)
                    if g >= 1 and qc == 0 and kb == 0:
                        pe.wait_ge(s[f"keys_masked{b}"], HG // 2 * QC + HG * (g - 1) + 2 * hp + 2)
                    for a in range(2):
                        j = 2 * hp + a
                        last = pe.matmul(bank[:, 2 * (u % 3) + a, :], head_keys(b, g, j)[:, 128 * kb:128 * (kb + 1)],
                                         q_stack[side][:, g, CH * qc:CH * (qc + 1)], start=True, stop=True)
                    last.then_inc(s[f"scored{b}"], 1)

                def weigh(t):
                    n, i = t // KB, t % KB
                    g, _, kb, _ = unit(2 * t)
                    if i == 0 and n >= 2:
                        pe.wait_ge(s[f"normed{b}"], n - 1)
                    for j in range(HG):
                        u = 2 * t + j // 2
                        pe.wait_ge(s[f"exped{b}"], u + 1)
                        last = pe.matmul(bank[32 * j:32 * j + VW, 6 + n % 2, :], values[:, kb, HG * g + j, :],
                                         probs[:, u % NP, CH * (j % 2):CH * (j % 2 + 1)],
                                         start=i == 0, stop=i == KB - 1, tile_position=(0, 32 * j))
                    last.then_inc(s[f"pv_done{b}"], 1)

                def turn(n):
                    pe.wait_ge(s[f"ot_copied{b}"], n + 1)
                    for t in range(TPC):
                        last = pe.transpose(bank[:, 6 + n % 2, 128 * t:128 * (t + 1)],
                                            out_t[:, n % 2, 128 * t:128 * (t + 1)], ident[:])
                    last.then_inc(s[f"ot_ready{b}"], 1)

                steps = UNITS // 2
                for t in range(steps + 1):
                    if t < steps:
                        scores(2 * t)
                        scores(2 * t + 1)
                    if t >= 1:
                        weigh(t - 1)
                    if t % KB == 4 and t >= KB:
                        turn(t // KB - 1)
                turn(G4 * QC - 1)

            def attn_general(b):
                with pe.Fori(0, G4 * KB) as block_of_queries:
                    pe.wait_ge(s[f"gen_staged{b}"], block_of_queries + 1)
                    for j in range(HG):
                        n = block_of_queries * HG + j
                        rows = slice(32 * j, 32 * (j + 1))
                        for a in range(2):
                            last = pe.matmul(bank[:, a, :], act_hi[rows, 2, 0:128], act_hi[rows, a, :],
                                             start=True, stop=True)
                        last.then_inc(s[f"gen_scored{b}"], 1)
                        pe.wait_ge(s[f"gen_probs{b}"], n + 1)
                        for kb in range(KB):
                            last = pe.transpose(bank[:, 2 + kb // 4, 128 * (kb % 4):128 * (kb % 4 + 1)],
                                                gen_s[:, 128 * kb:128 * (kb + 1)], ident[:])
                        last.then_inc(s[f"gen_t{b}"], 1)
                        pe.wait_ge(s[f"gen_tc{b}"], n + 1)
                        for kb in range(KB):
                            last = pe.matmul(bank[:, 4, 0:HD], gen_pt[:, 128 * kb:128 * (kb + 1)],
                                             gen_v[:, kb, j, 0:HD], start=kb == 0, stop=kb == KB - 1)
                        last.then_inc(s[f"gen_pv{b}"], 1)

            def attn_heads(b):
                pe.wait_ge(s["ao_ready"], b + 1)
                for c in range(QC * b, QC * (b + 1)):
                    for t in range(TPC):
                        last = pe.transpose(bank[:, 4 + c % 2, 128 * t:128 * (t + 1)], x_tok[:, TPC * c + t, :],
                                            ident[:])
                    last.then_inc(s["ao_t_ready"], 1)

            def attn_out(b):
                for c in range(QC * b, QC * (b + 1)):
                    pe.wait_ge(s["ao_lo_ready"], c + 1)
                    if c >= 2:
                        pe.wait_ge(s["x_ready"], nth(X_ATTN, c - 2))
                    split_matmul(bank[:, 6 + c % 2, :], sq_hi[:, WO, :], sq_lo[:, WO, :], xn_hi[:, chunk(c)],
                                 xn_lo[:, chunk(c)], True, True).then_inc(s["attn_out"], 1)

            def attention():
                for b in range(NB):
                    for c in range(QC * b, QC * (b + 1)):
                        if c + 1 < QC * (b + 1):
                            attn_first(c + 1)
                        else:
                            attn_bound(b)
                        attn_stacks(c)
                        if c + 1 < QC * (b + 1):
                            attn_second(c + 1)
                    attn_spread(b)
                    fast = pe.value_load(small_scores[0:1, b:b + 1], min_val=0, max_val=1)
                    with pe.If(fast):
                        attn_fast(b)
                    with pe.Else():
                        attn_general(b)
                    if b + 1 < NB:
                        attn_first(QC * (b + 1))
                    attn_heads(b)
                    if b + 1 < NB:
                        attn_second(QC * (b + 1))
                for b in range(NB):
                    attn_out(b)

            pe.wait_ge(s["ident_loaded"], 16)
            skewed("ffn0a", "pe", {**routed_norm(LN_FFN0A, 0, None), "take_in": take_in},
                   head=pieces(experts, 0))
            experts(0, max(HEADS["ffn0a"].values()))
            skewed("ssm", "pe", {**routed_norm(LN_FFN0B, 1, X_SSM), "t1": lambda c: norm_in(LN_SSM, c, X_FFN0A),
                                 "t2": lambda c: norm_out(LN_SSM, c), "proj": ssm_proj,
                                 "inner_t1": lambda c: norm_in(LN_INNER, c, None),
                                 "inner_t2": lambda c: norm_out(LN_INNER, c),
                                 "b_t1": lambda c: norm_in(LN_FFN0B, c, X_SSM),
                                 "b_t2": lambda c: norm_out(LN_FFN0B, c)},
                   head=pieces(experts, 1))
            experts(1, max(HEADS["ssm"].values()))
            skewed("ffn1a", "pe", {**lora(LN_FFN1A, 2, X_FFN0B), "b_t1": lambda c: norm_in(LN_ATTN, c, X_FFN1A),
                                   "b_t2": lambda c: norm_out(LN_ATTN, c)},
                   {"first": lambda: attn_first(0), "second": lambda: attn_second(0)})
            attention()

            def turn_back(c):
                pe.wait_ge(s["x_ready"], nth(X_FFN1B, c))
                if c >= 2:
                    pe.wait_ge(s["out_copied"], c - 1)
                for t in range(TPC):
                    at = slice(c * CH + 128 * t, c * CH + 128 * (t + 1))
                    last = pe.transpose(bank[:, T1[c % 2], 128 * t:128 * (t + 1)], x[:, at], ident[:])
                last.then_inc(s["fin_ready"], 1)

            skewed("ffn1b", "pe", {**lora(LN_FFN1B, 3, X_ATTN), "turn": turn_back})


def position_tables():
    t = np.arange(L, dtype=np.float64)
    side = np.array([-1.0, 1.0])
    grow = np.exp(-DECAY * side[:, None] * (t - L // 2))
    p, q = np.arange(128)[:, None], np.arange(CH)[None, :]
    row = np.arange(128)
    col_head, col_slot, col_d = row // 32, row % 32 // HD, row % HD
    sel = np.zeros((128, G4, 4, 128))
    for g in range(G4):
        same = row[:, None] == (HG * g + col_head[None, :]) * HD + col_d[None, :]
        for part, slots in enumerate(((0, 1), (2, 3), (0, 2), (1, 3))):
            sel[:, g, part, :] = same & np.isin(col_slot, slots)[None, :]
    tables = {
        "q_decay": np.broadcast_to(SCALE * grow[::-1][None], (128, 2, L)),
        "k_decay": grow.reshape(2, KB, 128).transpose(2, 0, 1),
        "fix": np.exp(-2 * DECAY * np.maximum(CH - 128 + p - q, 0)),
        "decay": np.exp(-DECAY * np.abs(np.arange(128)[:, None] - (np.arange(2 * L - 128) - (L - 128))[None, :])),
        "same_head": row[:, None] // HD == row[None, :] // HD,
        "sel_h": sel,
        "head_rows": row[:, None] // 32 == np.arange(HG)[None, :],
    }
    return {k: v.astype(np.float32) for k, v in tables.items()}


def kernel(**inputs):
    import concourse.bacc as bacc
    from concourse.bass_utils import run_bass_kernel_spmd

    a = {k: np.asarray(v) for k, v in inputs.items()}
    p = "L0_ffn_"
    gate_up = a[p + "gate_up_proj"].reshape(E0, D, D, 2)
    bias = a[p + "gate_up_bias"].reshape(E0, D, 2)
    k32, m128 = np.arange(2 * E0), np.arange(128)
    host = {
        "x": a["L0_attn_x"].reshape(T, D),
        "gate_up": gate_up.transpose(1, 0, 3, 2),
        "down": a[p + "down_proj"].transpose(1, 0, 2),
        "down_bias": a[p + "down_bias"],
        "router_w": a[p + "router_w"],
        "router_b": np.broadcast_to(a[p + "router_b"], (128, E0)),
        "gate_w": a["L1_ffn_gate_w"].T,
        "b_gate": bias[:, :, 0].T,
        "b_up": bias[:, :, 1].T,
        "vecs": np.stack([a["L0_attn_" + n] for n in ("A_param", "B_vec", "C_vec", "D_vec", "b_proj", "gamma",
                                                      "beta")] + [a["L1_ffn_base_b"]], axis=1),
        "squares": np.stack([a["L0_attn_W_proj"].T, a["L1_ffn_base_w"].T,
                             a["L1_ffn_lora_A"].reshape(TRUE1 * RANK, D).T,
                             a["L1_ffn_lora_B"].transpose(0, 2, 1).reshape(TRUE1 * RANK, D),
                             a["L1_attn_Wq"], a["L1_attn_Wk"], a["L1_attn_Wv"], a["L1_attn_Wo"]], axis=1),
        "w_down": a["L1_attn_W_down_kv"],
        "w_up": np.stack([a["L1_attn_W_up_k"], a["L1_attn_W_up_v"]], axis=1),
        **position_tables(),
        "ident": np.eye(128, dtype=np.float32),
        "sel0": np.broadcast_to((k32[:, None] % E0 == np.arange(E0))[:, :, None], (2 * E0, E0, 128))
                  .astype(np.float32),
        "sel1": (np.arange(2 * TRUE1)[:, None] % TRUE1 == m128 // RANK).astype(np.float32),
    }
    nc = bacc.Bacc("TRN2", target_bir_lowering=False, num_devices=1)
    arrays, io = {}, {}
    for name, v in host.items():
        v = np.ascontiguousarray(v)
        arrays[f"in_{name}"] = v
        io[name] = nc.dram_tensor(f"in_{name}", v.shape, mybir.dt.from_np(v.dtype), kind="ExternalInput").ap()
    io["out"] = nc.dram_tensor("out_0", (T, D), F32, kind="ExternalOutput").ap()
    build(nc, io)
    result = run_bass_kernel_spmd(nc, [arrays], core_ids=[0])
    return result.results[0]["out_0"].reshape(NB, L, D)
```
